# Optimizing a Trainium2 kernel written in Bass

```python
import numpy as np
import jax
import jax.numpy as jnp

def _softmax(x, axis=-1):
    return jax.nn.softmax(x, axis=axis)

def _gelu(x):
    return jax.nn.gelu(x, approximate=True)

def _silu(x):
    return jax.nn.silu(x)

def _sigmoid(x):
    return jax.nn.sigmoid(x)

def _layernorm(x, axis=-1, eps=1e-05):
    m = jnp.mean(x, axis=axis, keepdims=True)
    v = jnp.var(x, axis=axis, keepdims=True)
    return (x - m) / jnp.sqrt(v + eps)

def _scatter_add(tgt, idx, src, axis=0):
    return tgt.at[idx].add(src)

def _segment_sum(src, seg, n):
    return jax.ops.segment_sum(src, seg, n)
kernel_name = 'mk_gnn_ffn_d2_gnn_r8_8fb75c'

def setup_inputs(seed: int=0):
    np.random.seed(seed)
    _w = jnp.asarray

    def _rec_inputs():
        import jax
        import jax.numpy as jnp
        _gk = jax.random.key(seed)
        x = -0.0002117 + 1 * jax.random.normal(jax.random.fold_in(_gk, 1), (1250, 512), jnp.float32)
        src = jax.random.randint(jax.random.fold_in(_gk, 2), (20000,), 0, 1250, jnp.int32)
        dst = jax.random.randint(jax.random.fold_in(_gk, 3), (20000,), 0, 1250, jnp.int32)
        _o = jnp.argsort(dst, stable=True)
        src = src[_o]
        dst = dst[_o]
        edge_weight = jax.random.uniform(jax.random.fold_in(_gk, 13), (20000,), jnp.float32, 0.0, 0.999994)
        return (x, src, dst, edge_weight)
    x, src, dst, edge_weight = _rec_inputs()

    def _L0_gnn_setup():
        import jax, jax.numpy as jnp
        import numpy as np
        BN_EPS = 1e-05

        def batch_norm(h, gamma, beta):
            mu = jnp.mean(h, axis=0)
            var = jnp.var(h, axis=0)
            return (h - mu) * jax.lax.rsqrt(var + BN_EPS) * gamma + beta
        key = jax.random.key(seed)
        ks = jax.random.split(key, 6)
        N, E, dim = (6250, 200000, 512)
        hidden = dim * 2
        x = jax.random.normal(ks[0], (N, dim), dtype=jnp.float32)
        edge_index = jax.random.randint(ks[1], (2, E), 0, N, dtype=jnp.int64)
        s1 = 1.0 / np.sqrt(dim)
        s2 = 1.0 / np.sqrt(hidden)
        return {'x': x, 'edge_index': edge_index, 'eps': jnp.float32(0.0), 'W1': jax.random.uniform(ks[2], (dim, hidden), jnp.float32, -s1, s1), 'b1': jnp.zeros((hidden,), jnp.float32), 'g1': jnp.ones((hidden,), jnp.float32), 'be1': jnp.zeros((hidden,), jnp.float32), 'W2': jax.random.uniform(ks[3], (hidden, dim), jnp.float32, -s2, s2), 'b2': jnp.zeros((dim,), jnp.float32), 'g2': jnp.ones((dim,), jnp.float32), 'be2': jnp.zeros((dim,), jnp.float32)}
    _L0_gnn_all = _L0_gnn_setup()
    _L0_gnn_in = {k: v for k, v in _L0_gnn_all.items() if k in ('eps', 'W1', 'b1', 'g1', 'be1', 'W2', 'b2', 'g2', 'be2')}
    del _L0_gnn_all

    def _L0_ffn_setup():
        import jax, jax.numpy as jnp
        import numpy as np
        SINKHORN_ITERS = 8
        TEMPERATURE = 1.0
        EPS = 1e-10

        def sinkhorn(gates):
            t = jnp.log(jnp.clip(gates, EPS)) / TEMPERATURE

            def body(t, _):
                t = t - jax.nn.logsumexp(t, axis=-2, keepdims=True)
                t = t - jax.nn.logsumexp(t, axis=-1, keepdims=True)
                return (t, None)
            t, _ = jax.lax.scan(body, t, None, length=SINKHORN_ITERS)
            return jnp.exp(t)
        key = jax.random.key(seed)
        k1, k2, k3 = jax.random.split(key, 3)
        b, n, d, e, h = (4, 1024, 512, 8, 1)
        x = jax.random.normal(k1, (b, n, d), dtype=jnp.float32)
        gate_w = jax.random.normal(k2, (h, d, e), dtype=jnp.float32)
        experts = jax.random.normal(k3, (e, d, d), dtype=jnp.float32) / np.sqrt(d)
        return {'x': x, 'gate_w': gate_w, 'experts': experts}
    _L0_ffn_all = _L0_ffn_setup()
    _L0_ffn_in = {k: v for k, v in _L0_ffn_all.items() if k in ('gate_w', 'experts')}
    del _L0_ffn_all

    def _L1_gnn_setup():
        import jax, jax.numpy as jnp
        import numpy as np
        N_NODES = 2500
        N_EDGES = 20000
        N_IN = 512
        N_OUT = 512
        key = jax.random.key(seed)
        k1, k2, k3, k4, k5 = jax.random.split(key, 5)
        x = jax.random.normal(k1, (N_NODES, N_IN), dtype=jnp.float32)
        vals = jax.random.uniform(k2, (N_EDGES,), dtype=jnp.float32)
        bound = 1.0 / np.sqrt(N_IN)
        weight = jax.random.uniform(k3, (N_OUT, N_IN), minval=-bound, maxval=bound, dtype=jnp.float32)
        row = jax.random.randint(k4, (N_EDGES,), 0, N_NODES, dtype=jnp.int32)
        col = jax.random.randint(k5, (N_EDGES,), 0, N_NODES, dtype=jnp.int32)
        return {'x': x, 'vals': vals, 'weight': weight, 'row': row, 'col': col}
    _L1_gnn_all = _L1_gnn_setup()
    _L1_gnn_in = {k: v for k, v in _L1_gnn_all.items() if k in ('weight',)}
    del _L1_gnn_all

    def _L1_ffn_setup():
        import jax, jax.numpy as jnp
        import numpy as np
        DIM, DEPTH, MULT = (512, 3, 4)
        E = 2 ** DEPTH
        HID = MULT * DIM
        B, S = (4, 1024)

        def _leaf_probs(flat_x, rw, rb):
            n_tok = flat_x.shape[0]
            leaf = jnp.ones((n_tok, 1), dtype=flat_x.dtype)
            for d in range(DEPTH):
                off, n = (2 ** d - 1, 2 ** d)
                logits = flat_x @ rw[off:off + n].T + rb[off:off + n]
                p = jax.nn.sigmoid(logits)
                leaf = (leaf[:, :, None] * jnp.stack([1.0 - p, p], axis=2)).reshape(n_tok, 2 * n)
            return leaf
        key = jax.random.key(seed)
        ks = jax.random.split(key, 7)
        sd = 1.0 / np.sqrt(DIM)
        sh = 1.0 / np.sqrt(HID)
        return {'x': jax.random.normal(ks[0], (B, S, DIM), dtype=jnp.float32), 'rw': jax.random.normal(ks[1], (E - 1, DIM), dtype=jnp.float32) * sd, 'rb': jax.random.normal(ks[2], (E - 1,), dtype=jnp.float32) * sd, 'w1': jax.random.normal(ks[3], (E, DIM, HID), dtype=jnp.float32) * sd, 'b1': jax.random.normal(ks[4], (E, HID), dtype=jnp.float32) * sd, 'w2': jax.random.normal(ks[5], (E, HID, DIM), dtype=jnp.float32) * sh, 'b2': jax.random.normal(ks[6], (E, DIM), dtype=jnp.float32) * sh}
    _L1_ffn_all = _L1_ffn_setup()
    _L1_ffn_in = {k: v for k, v in _L1_ffn_all.items() if k in ('rw', 'rb', 'w1', 'b1', 'w2', 'b2')}
    del _L1_ffn_all
    return {'x': x, 'src': src, 'dst': dst, 'edge_weight': edge_weight, 'L0_gnn_eps': _L0_gnn_in['eps'], 'L0_gnn_W1': _L0_gnn_in['W1'], 'L0_gnn_b1': _L0_gnn_in['b1'], 'L0_gnn_g1': _L0_gnn_in['g1'], 'L0_gnn_be1': _L0_gnn_in['be1'], 'L0_gnn_W2': _L0_gnn_in['W2'], 'L0_gnn_b2': _L0_gnn_in['b2'], 'L0_gnn_g2': _L0_gnn_in['g2'], 'L0_gnn_be2': _L0_gnn_in['be2'], 'L0_ffn_gate_w': _L0_ffn_in['gate_w'], 'L0_ffn_experts': _L0_ffn_in['experts'], 'L1_gnn_weight': _L1_gnn_in['weight'], 'L1_ffn_rw': _L1_ffn_in['rw'], 'L1_ffn_rb': _L1_ffn_in['rb'], 'L1_ffn_w1': _L1_ffn_in['w1'], 'L1_ffn_b1': _L1_ffn_in['b1'], 'L1_ffn_w2': _L1_ffn_in['w2'], 'L1_ffn_b2': _L1_ffn_in['b2']}

def reference(x, src, dst, edge_weight, L0_gnn_eps, L0_gnn_W1, L0_gnn_b1, L0_gnn_g1, L0_gnn_be1, L0_gnn_W2, L0_gnn_b2, L0_gnn_g2, L0_gnn_be2, L0_ffn_gate_w, L0_ffn_experts, L1_gnn_weight, L1_ffn_rw, L1_ffn_rb, L1_ffn_w1, L1_ffn_b1, L1_ffn_w2, L1_ffn_b2):
    import jax
    import jax.numpy as jnp

    def _L0_gnn_ref(x, edge_index, eps, W1, b1, g1, be1, W2, b2, g2, be2):
        import jax, jax.numpy as jnp
        import numpy as np
        BN_EPS = 1e-05

        def batch_norm(h, gamma, beta):
            mu = jnp.mean(h, axis=0)
            var = jnp.var(h, axis=0)
            return (h - mu) * jax.lax.rsqrt(var + BN_EPS) * gamma + beta
        N = x.shape[0]
        src, dst = (edge_index[0], edge_index[1])
        agg = jax.ops.segment_sum(x[src], dst, num_segments=N)
        h = (1.0 + eps) * x + agg
        h = jax.nn.relu(batch_norm(h @ W1 + b1, g1, be1))
        h = h @ W2 + b2
        h = jax.nn.relu(batch_norm(h, g2, be2))
        return x + h

    def _L0_ffn_ref(x, gate_w, experts):
        import jax, jax.numpy as jnp
        import numpy as np
        SINKHORN_ITERS = 8
        TEMPERATURE = 1.0
        EPS = 1e-10

        def sinkhorn(gates):
            t = jnp.log(jnp.clip(gates, EPS)) / TEMPERATURE

            def body(t, _):
                t = t - jax.nn.logsumexp(t, axis=-2, keepdims=True)
                t = t - jax.nn.logsumexp(t, axis=-1, keepdims=True)
                return (t, None)
            t, _ = jax.lax.scan(body, t, None, length=SINKHORN_ITERS)
            return jnp.exp(t)
        b, n, d = x.shape
        h = gate_w.shape[0]
        e = experts.shape[0]
        N = b * n
        m = n // e
        x4 = x[:, None]
        gates = jnp.einsum('bhnd,hde->bhne', x4, gate_w)
        xf = jnp.transpose(x4, (1, 0, 2, 3)).reshape(h, N, d)
        gf = jnp.transpose(gates, (1, 0, 2, 3)).reshape(h, N, e)
        cg = sinkhorn(gf)
        vals, idx = jax.lax.top_k(jnp.transpose(cg, (0, 2, 1)), m)
        gate_values = (vals > 0.5).astype(x.dtype)
        gate_values = jnp.transpose(gate_values, (0, 2, 1))
        idx = jnp.transpose(idx, (0, 2, 1))
        routed = xf[jnp.arange(h)[:, None, None], idx]
        outputs = jnp.einsum('hmei,eio->hmeo', routed, experts)
        outputs = outputs * gate_values[..., None]
        o_dim = outputs.shape[-1]
        src = outputs.reshape(h, m * e, o_dim)
        idx_flat = idx.reshape(h, m * e)

        def combine(idxf, srcf):
            s = jnp.zeros((N, o_dim), srcf.dtype).at[idxf].add(srcf)
            c = jnp.zeros((N,), srcf.dtype).at[idxf].add(1.0)
            return s / (c + 1.0)[:, None]
        out = jax.vmap(combine)(idx_flat, src)
        out = out.reshape(h, b, n, o_dim)
        out = jnp.transpose(out, (1, 0, 2, 3))[:, 0]
        return out

    def _L1_gnn_ref(x, vals, weight, row, col):
        import jax, jax.numpy as jnp
        import numpy as np
        N_NODES = 2500
        N_EDGES = 20000
        N_IN = 512
        N_OUT = 512
        n = x.shape[0]
        msgs = x[col] * vals[:, None]
        agg = jax.ops.segment_sum(msgs, row, num_segments=n)
        return jnp.einsum('nd,od->no', agg, weight)

    def _L1_ffn_ref(x, rw, rb, w1, b1, w2, b2):
        import jax, jax.numpy as jnp
        import numpy as np
        DIM, DEPTH, MULT = (512, 3, 4)
        E = 2 ** DEPTH
        HID = MULT * DIM
        B, S = (4, 1024)

        def _leaf_probs(flat_x, rw, rb):
            n_tok = flat_x.shape[0]
            leaf = jnp.ones((n_tok, 1), dtype=flat_x.dtype)
            for d in range(DEPTH):
                off, n = (2 ** d - 1, 2 ** d)
                logits = flat_x @ rw[off:off + n].T + rb[off:off + n]
                p = jax.nn.sigmoid(logits)
                leaf = (leaf[:, :, None] * jnp.stack([1.0 - p, p], axis=2)).reshape(n_tok, 2 * n)
            return leaf
        b, s, dim = x.shape
        flat_x = x.reshape(b * s, dim)
        leaf_probs = _leaf_probs(flat_x, rw, rb)
        h = jnp.einsum('nd,edh->neh', flat_x, w1) + b1[None]
        h = jax.nn.gelu(h, approximate=False)
        y = jnp.einsum('neh,ehd->ned', h, w2) + b2[None]
        out = jnp.einsum('ned,ne->nd', y, leaf_probs)
        return out.reshape(b, s, dim)
    edge_index = jnp.stack([src, dst])
    x = x + _L0_gnn_ref(_layernorm(x, axis=-1), edge_index, L0_gnn_eps, L0_gnn_W1, L0_gnn_b1, L0_gnn_g1, L0_gnn_be1, L0_gnn_W2, L0_gnn_b2, L0_gnn_g2, L0_gnn_be2)
    x = x + _L0_ffn_ref(_layernorm(x, axis=-1)[None], L0_ffn_gate_w, L0_ffn_experts)[0]
    x = x + _L1_gnn_ref(_layernorm(x, axis=-1), edge_weight, L1_gnn_weight, src, dst)
    x = x + _L1_ffn_ref(_layernorm(x, axis=-1)[None], L1_ffn_rw, L1_ffn_rb, L1_ffn_w1, L1_ffn_b1, L1_ffn_w2, L1_ffn_b2)[0]
    return x

_drawn_inputs = setup_inputs


def setup_inputs(seed=0):
    import zlib

    import numpy as np

    out = dict(_drawn_inputs(seed))
    spreads = {'L0_gnn_b1': (0.0, 0.8),
     'L0_gnn_g1': (1.0, 0.2),
     'L0_gnn_be1': (0.0, 0.1),
     'L0_gnn_b2': (0.0, 0.8),
     'L0_gnn_g2': (1.0, 0.2),
     'L0_gnn_be2': (0.0, 0.1)}
    factors = {'L1_ffn_rb': 8.0, 'L1_ffn_b1': 8.0, 'L1_ffn_b2': 8.0}
    for name, (base, spread) in spreads.items():
        noise = np.random.default_rng([zlib.crc32(name.encode()), seed]).standard_normal(out[name].shape)
        drawn = base * np.exp(spread * noise) if base else spread * noise
        out[name] = jnp.asarray(drawn.astype(out[name].dtype))
    for name, factor in factors.items():
        out[name] = (out[name] * factor).astype(out[name].dtype)
    return out
```

```python
from contextlib import ExitStack

import numpy as np

import concourse.bass as bass
from concourse import mybir

F32 = mybir.dt.float32
F32R = mybir.dt.float32r
F16 = mybir.dt.float16
BF16 = mybir.dt.bfloat16
I32 = mybir.dt.int32
ACT = mybir.ActivationFunctionType
ALU = mybir.AluOpType
X = mybir.AxisListType.X

N = 1250
D = 512
TR = 125
NT = N // TR
KD = D // 128
EDGES = 20000
EB = 125
NB = EDGES // EB
EQ = NB // 2
WIN = 32
NW = -(-N // WIN)
NC = NT * 128
ND = NW * WIN
KEY = 2048
HID0 = 1024
KH0 = HID0 // 128
NE = 8
TOP = N // NE
HID1 = 2048
EPS = 1e-5
FLOOR = 1e-10
SINKHORN = 8
BLOCKS = [(0, 418), (418, 834), (834, 1250)]
BW = 418
SHIFTS = [26, 22, 18, 14, 10, 6, 2, 0]

C_ID, C_ONE, C_BLK, C_SEL, C_LSEL, C_LONE, C_ROW = 0, 128, 256, 384, 512, 536, 539
C_I32, C_W2K, C_BLKNO, C_I10 = 540, 572, 612, 772
C_END = C_I10 + NC


def shape_constants():
    c = np.zeros((128, C_END), np.float32)
    p = np.arange(128)
    c[:, C_ID:C_ID + 128] = np.eye(128)
    c[:, C_ONE:C_ONE + 128] = 1
    c[:, C_BLK:C_BLK + 128] = p[:, None] // 16 == p[None] // 16
    c[0:NE, C_SEL:C_SEL + 128] = p[0:NE, None] == p[None] // 16
    for depth in range(3):
        for e in range(NE):
            node, bit = 2**depth - 1 + (e >> (3 - depth)), (e >> (2 - depth)) & 1
            c[node, C_LSEL + 8 * depth + e] = 1 if bit else -1
            c[e, C_LONE + depth] = 0 if bit else 1
    c[:, C_ROW] = p
    c[:, C_I32:C_I32 + WIN] = np.arange(WIN)
    c[:, C_W2K:C_W2K + NW] = KEY * np.arange(NW)
    c[:, C_BLKNO:C_BLKNO + NB] = (2 * np.arange(EQ)[None] + np.arange(2)[:, None]).reshape(-1)
    i10 = np.full((NT, 128), -1.0)
    i10[:, :TR] = np.arange(N).reshape(NT, TR)
    c[:, C_I10:] = i10.reshape(-1)
    bits = np.zeros((128, len(SHIFTS)), np.int32)
    for r, s in enumerate(SHIFTS):
        limit = 4 if r == len(SHIFTS) - 1 else 16
        bits[:, r] = np.where(p % 16 < limit, (p % 16) << s, 0x40000000)
    return c, bits




X_AT = 10240
REG = X_AT + NT * D * 4
A1_END = REG + NT * ND * 4
ROWS = NT * D * 4
COLS = KD * N * 4


class Record:
    pass


class Room:

    def __init__(self, nc, start):
        self.nc, self.next = nc, start

    def __call__(self, name, shape, dtype):
        width = {F32: 4, F32R: 4, I32: 4, F16: 2, BF16: 2}[dtype]
        start = -(-self.nc.sbuf_base // 32) * 32
        buffer = self.nc.alloc_sbuf_tensor_at(name, shape, dtype, offset=start + self.next)
        self.next += -(-int(np.prod(shape[1:])) * width // 32) * 32
        return buffer


class Steps:

    def __init__(self, engine, semaphore):
        self.engine, self.semaphore, self.n = engine, semaphore, 0

    def mark(self, ins):
        ins.then_inc(self.semaphore, 1)
        self.n += 1

    def wait(self):
        self.engine.wait_ge(self.semaphore, self.n)

    def then(self, ins):
        self.mark(ins)
        self.wait()


def pieces(lo, hi):
    return [(t, max(lo, t * TR) - t * TR, min(hi, (t + 1) * TR) - t * TR)
            for t in range(NT) if t * TR < hi and (t + 1) * TR > lo]


def halves(ap):
    return ap.rearrange("p (q h) -> p q h", h=2)


def phase_edges(nc, sem, g):
    room = Room(nc, g.scratch_at)
    raw_i = room("edge_ints", [EQ, 2, 2 * EB], I32)
    wraw = room("edge_w", [EQ, 2 * EB], F32)
    win_i = room("edge_win", [EQ, 2 * EB], I32)
    rem_i = room("edge_rem", [EQ, 2 * EB], I32)
    keyrem = room("edge_keyrem", [EQ, 2, 2 * EB], F32)
    extent = room("edge_extent", [EQ, 4], F32)
    spread = room("edge_spread", [EQ, 4, NW], F32)
    rem = room("rem", [EB, NB], F32)
    wcol = room("wcol", [EB, NB], F32)
    wres = room("wres", [EB, NB], F32)
    wres2 = room("wres2", [EB, NB], F32)
    parts = room("parts", [EB, NB, 3], BF16)
    meets1 = room("meets1", [NW, NB], F32)
    meets = room("meets", [NW, NB], F32)
    pick = room("pick", [NW, 2, NB], F32)
    ends = room("ends", [NW, 2], F32)
    lohi = room("lohi", [NW, 2], F32)
    i10f = room("i10f", [128, NC], F32)

    loaded = sem("e_loaded")
    own = sem("e_own")
    keyed = sem("e_keyed")
    spread_out = sem("e_spread")
    bounded = sem("e_bounded")
    turned = sem("e_turned")

    loads = [
        (g.small[:, :], g.consts_d[:, 0:C_I10]), (raw_i[:, 0, :], g.src.rearrange("(q e) -> q e", q=EQ)),
        (raw_i[:, 1, :], g.dst.rearrange("(q e) -> q e", q=EQ)),
        (wraw[:, :], g.edge_weight.rearrange("(q e) -> q e", q=EQ)), (i10f[:, :], g.consts_d[:, C_I10:C_END]),
        (g.kshift[:, :], g.bits_d), (g.eps0[:, :], g.gnn0_eps.partition_broadcast(128)),
        (g.vecrows[0:8, :], g.gnn0_b1.rearrange("(t p) -> t p", p=128)),
        (g.vecrows[8:16, :], g.gnn0_g1.rearrange("(t p) -> t p", p=128)),
        (g.vecrows[16:24, :], g.gnn0_be1.rearrange("(t p) -> t p", p=128)),
        (g.vecrows[24:28, :], g.gnn0_b2.rearrange("(t p) -> t p", p=128)),
        (g.vecrows[28:32, :], g.gnn0_g2.rearrange("(t p) -> t p", p=128)),
        (g.vecrows[32:36, :], g.gnn0_be2.rearrange("(t p) -> t p", p=128)),
        (g.vecrows[36:68, :], g.b2.rearrange("e (t p) -> (e t) p", p=128)),
        (g.vecrows[68:96, :], g.rw.rearrange("n (t p) -> (n t) p", p=128)),
        (g.b1rows[:, :], g.b1.rearrange("e (t p) -> (e t) p", p=128)),
        (g.gate[:, :, :], g.gate_w[0].rearrange("(k p) e -> p k e", p=128)),
        (g.rb_col[0:7, :], g.rb.rearrange("(n a) -> n a", a=1)),
    ]

    with nc.Block() as block:
        @block.sync
        def _(sp):
            for to, of in loads:
                sp.dma_start(to, of).then_inc(loaded, 16)
            sp.dma_start(g.x_rows[:, :, :], g.x.rearrange("(t p) d -> p t d", p=TR)).then_inc(g.x_loaded, 16)

        @block.vector
        def _(v):
            s = Steps(v, own)
            v.wait_ge(loaded, 16 * len(loads))
            s.mark(v.tensor_copy(g.i10[:, :], i10f[0:EB, :]))
            s.mark(v.memset(g.zeros[:, :], 0.0))
            s.mark(v.memset(g.key[:, :], -1.0))
            s.mark(v.memset(g.D_all[:, NB:NB + 1, :, :], 0.0))
            s.mark(v.tensor_single_scalar(win_i[:, :], raw_i[:, 1, :], 5, ALU.logical_shift_right))
            s.then(v.tensor_single_scalar(rem_i[:, :], raw_i[:, 1, :], WIN - 1, ALU.bitwise_and))
            v.scalar_tensor_tensor(out=keyrem[:, 0, :], in0=win_i[:, :], scalar=float(KEY), in1=raw_i[:, 0, :],
                                   op0=ALU.mult, op1=ALU.add).then_inc(keyed, 1)
            v.tensor_copy(keyrem[:, 1, :], rem_i[:, :]).then_inc(keyed, 1)
            by_block = win_i[:, :].rearrange("q (h e) -> q h e", h=2)
            s.mark(v.tensor_reduce(extent[:, 0:2], by_block, X, ALU.min))
            s.then(v.tensor_reduce(extent[:, 2:4], by_block, X, ALU.max))
            for a in range(4):
                v.tensor_scalar(spread[:, a, :], g.ones[0:EQ, 0:NW], extent[:, a:a + 1], None,
                                ALU.mult).then_inc(spread_out, 1)
            v.wait_ge(turned, 1)
            table = g.psum[0:EB, 0, 0:6 * EQ].rearrange("p (a h q) -> p a q h", a=3, h=2)
            s.mark(v.tensor_copy(halves(g.key[:, 0:NB]), table[:, 0]))
            s.mark(v.tensor_copy(halves(rem[:, :]), table[:, 1]))
            s.then(v.tensor_copy(halves(wcol[:, :]), table[:, 2]))
            s.then(v.tensor_copy(parts[:, :, 0], wcol[:, :]))
            s.then(v.tensor_tensor(wres[:, :], wcol[:, :], parts[:, :, 0], ALU.subtract))
            s.then(v.tensor_copy(parts[:, :, 1], wres[:, :]))
            s.then(v.tensor_tensor(wres2[:, :], wres[:, :], parts[:, :, 1], ALU.subtract))
            s.then(v.tensor_copy(parts[:, :, 2], wres2[:, :]))
            v.wait_ge(turned, 2)
            ext = g.psum[0:NW, 1, 0:2 * NB].rearrange("w (a b) -> w a b", a=2)
            s.then(v.tensor_scalar(meets1[:, :], ext[:, 0], g.rowno[0:NW, :], None, ALU.is_le))
            s.then(v.scalar_tensor_tensor(out=meets[:, :], in0=ext[:, 1], scalar=g.rowno[0:NW, :],
                                          in1=meets1[:, :], op0=ALU.is_ge, op1=ALU.mult))
            s.mark(v.scalar_tensor_tensor(out=pick[:, 0, :], in0=meets[:, :], scalar=-256.0,
                                          in1=g.blkno[0:NW, :], op0=ALU.mult, op1=ALU.add))
            s.then(v.tensor_tensor(pick[:, 1, :], meets[:, :], g.blkno[0:NW, :], ALU.mult))
            s.mark(v.tensor_reduce(ends[:, 0:1], pick[:, 0, :], X, ALU.min))
            s.then(v.tensor_reduce(ends[:, 1:2], pick[:, 1, :], X, ALU.max))
            v.tensor_scalar(lohi[:, 0:1], ends[:, 0:1], 256.0, float(NB - 1), ALU.add,
                            ALU.min).then_inc(bounded, 1)
            v.tensor_scalar(lohi[:, 1:2], ends[:, 1:2], 1.0, None, ALU.add).then_inc(bounded, 1)
            d = g.D_all[:, 0:NB, :, :]
            s.then(v.tensor_tensor(d[:, :, 0, :], rem[:, :].unsqueeze(2).to_broadcast([EB, NB, WIN]),
                                   g.iota32[0:EB, :].unsqueeze(1).to_broadcast([EB, NB, WIN]), ALU.is_equal))
            for c in range(3):
                s.mark(v.tensor_tensor(d[:, :, 1 + c, :], d[:, :, 0, :],
                                       parts[:, :, c:c + 1].to_broadcast([EB, NB, WIN]), ALU.mult))
            v.wait_ge(turned, 3)
            s.mark(v.tensor_copy(g.bounds[:, :], g.psum[0:1, 2, 0:2 * NW]))
            v.wait_ge(turned, 4)
            s.mark(v.tensor_copy(g.vecs[:, :], g.psum[:, 3, 0:96]))
            s.mark(v.tensor_copy(g.b1cols[:, :], g.psum[:, 3, 128:256]))

        @block.tensor
        def _(t):
            t.wait_ge(loaded, 16 * len(loads))
            t.wait_ge(keyed, 2)
            for a, of in enumerate([keyrem[:, 0, :], keyrem[:, 1, :], wraw[:, :]]):
                for h in range(2):
                    o = (2 * a + h) * EQ
                    ins = t.transpose(g.psum[0:EB, 0, o:o + EQ], of[:, h * EB:(h + 1) * EB],
                                      g.ident[0:EQ, 0:EQ])
            ins.then_inc(turned, 1)
            t.wait_ge(spread_out, 4)
            for a in range(4):
                ins = t.matmul(g.psum[0:NW, 1, a * EQ:(a + 1) * EQ], spread[:, a, :], g.ident[0:EQ, 0:EQ],
                               start=True, stop=True)
            ins.then_inc(turned, 1)
            t.wait_ge(bounded, 2)
            for a in range(2):
                ins = t.transpose(g.psum[0:1, 2, a * NW:(a + 1) * NW], lohi[:, a:a + 1],
                                  g.ident[0:NW, 0:NW])
            ins.then_inc(turned, 1)
            t.transpose(g.psum[:, 3, 0:96], g.vecrows[0:96, :], g.ident[0:96, 0:96])
            t.transpose(g.psum[:, 3, 128:256], g.b1rows[:, :], g.ident[:, :]).then_inc(turned, 1)


def phase_adjacency(nc, sem, g):
    room = Room(nc, g.scratch_at)
    S = room("src_onehot", [EB, 2, NC], BF16)
    rkey = room("rkey", [EB, NB + 2], F32)
    WP = room("weight_parts", [128, 2, NT, 3, WIN], F32)
    T = room("weight_sum", [128, NT, WIN], F32)

    rkeys = sem("a_rkeys")
    keyed = sem("a_keyed")
    made = sem("a_made")
    used = sem("a_used")
    summed = sem("a_summed")
    drained = sem("a_drained")
    copied = sem("a_copied")
    parts_free = sem("a_parts_free")
    added = sem("a_added")

    def banks(par):
        return g.psum[:, 3 * par:3 * par + 3, :].rearrange("p a b -> p (a b)")[:, 0:NC]

    def window(eng, w):
        lo = eng.value_load(g.bounds[0:1, bass.ds(w, 1)], min_val=0, max_val=NB - 1)
        hi = eng.value_load(g.bounds[0:1, bass.ds(w + NW, 1)], min_val=1, max_val=NB)
        return lo, hi

    with nc.Block() as block:
        @block.vector
        def _(v):
            v.sem_inc(made, 1)
            n = v.alloc_register("made_blocks")
            v.reg_mov(n, 1)
            with v.Fori(0, NW) as w:
                lo, hi = window(v, w)
                v.wait_ge(made, v.snap(n))
                v.tensor_scalar(rkey[:, :], g.key[:, :], g.w2k[0:EB, bass.ds(w, 1)], None,
                                ALU.subtract).then_inc(rkeys, 1)
                v.wait_ge(rkeys, w + 1)
                v.sem_inc(keyed, 1)
                with v.Fori(lo, hi, 2) as b:
                    for u in range(2):
                        v.wait_ge(used, v.snap(n))
                        v.tensor_scalar(S[:, u, :], g.i10[:, :], rkey[:, bass.ds(b + u, 1)], None,
                                        ALU.is_equal).then_inc(made, 1)
                        v.reg_add(n, n, 1)

        @block.tensor
        def _(t):
            t.sem_inc(used, 2)
            t.sem_inc(drained, 2)
            n = t.alloc_register("used_blocks")
            t.reg_mov(n, 1)
            with t.Fori(0, NW // 2) as w2:
                for par in range(2):
                    lo, hi = window(t, w2 * 2 + par)
                    ps = banks(par)
                    t.wait_ge(drained, w2 * 2 + par + 1)
                    for c in range(0, NT, 4):
                        t.matmul(ps[:, c * 128:(c + 1) * 128], g.zeros[0:EB, :], g.zeros[0:EB, :],
                                 start=True, stop=False, skip_group_check=True)
                    with t.Fori(lo, hi, 2) as b:
                        for u in range(2):
                            t.wait_ge(made, t.snap(n) + 1)
                            for c in range(NT):
                                ins = t.matmul(ps[:, c * 128:(c + 1) * 128], S[:, u, c * 128:(c + 1) * 128],
                                               g.D_flat[:, bass.ds((b + u) * 128, 128)],
                                               start=False, stop=False, skip_group_check=True)
                            ins.then_inc(used, 1)
                            t.reg_add(n, n, 1)
                    t.matmul(ps[:, 0:128], g.zeros[0:EB, :], g.zeros[0:EB, :], start=False, stop=True,
                             skip_group_check=True).then_inc(summed, 1)

        @block.scalar
        def _(a):
            with a.Fori(0, NW // 2) as w2:
                for par in range(2):
                    w = w2 * 2 + par
                    ps = banks(par).rearrange("p (c a w) -> p c a w", c=NT, a=4)
                    a.wait_ge(summed, w + 1)
                    a.wait_ge(parts_free, w + 1)
                    a.activation(WP[:, par], ps[:, :, 1:4, :], ACT.Copy).then_inc(copied, 1)
                    a.activation(g.A0T[:, :, bass.ds(w * WIN, WIN)], ps[:, :, 0, :],
                                 ACT.Copy).then_inc(drained, 1)

        @block.gpsimd
        def _(q):
            q.sem_inc(parts_free, 2)
            with q.Fori(0, NW // 2) as w2:
                for par in range(2):
                    w = w2 * 2 + par
                    q.wait_ge(copied, w + 1)
                    q.wait_ge(parts_free, w + 2)
                    q.tensor_tensor(T[:, :, :], WP[:, par, :, 0, :], WP[:, par, :, 1, :],
                                    ALU.add).then_inc(added, 1)
                    q.wait_ge(added, w + 1)
                    q.tensor_tensor(g.A1T[:, :, bass.ds(w * WIN, WIN)], T[:, :, :], WP[:, par, :, 2, :],
                                    ALU.add).then_inc(parts_free, 1)


def norm_sems(sem, name):
    n = Record()
    n.own = sem(name + "_own")
    n.var = sem(name + "_var")
    n.dev = sem(name + "_dev")
    n.normed = sem(name + "_normed")
    return n


def norm_vector(v, g, to, n):
    s = Steps(v, n.own)
    for t in range(NT):
        s.mark(v.bn_stats(g.stats[:, t, :], g.x_rows[:, t, :]))
    s.wait()
    for t in range(NT):
        s.mark(v.bn_aggr(g.meanvar[:, t, :], g.stats[:, t, :]))
    s.wait()
    v.tensor_scalar(g.dev[:, :], g.meanvar[:, :, 1], EPS, None, ALU.add).then_inc(n.var, 1)
    v.wait_ge(n.dev, 1)
    s.then(v.reciprocal(g.rstd[:, :], g.dev2[:, :]))
    for t in range(NT):
        v.tensor_scalar(to[:, t, :], g.x_rows[:, t, :], g.meanvar[:, t, 0:1], g.rstd[:, t:t + 1],
                        ALU.subtract, ALU.mult).then_inc(n.normed, 1)
    return s


def norm_scalar(a, g, n):
    a.wait_ge(n.var, 1)
    a.activation(g.dev2[:, :], g.dev[:, :], ACT.Sqrt).then_inc(n.dev, 1)


def phase_norm0(nc, sem, g):
    n = norm_sems(sem, "n0")
    hi_cut = sem("n0_hi")
    lo_cut = sem("n0_lo")
    xed = sem("n0_x")

    with nc.Block() as block:
        @block.vector
        def _(v):
            v.wait_ge(g.x_loaded, 16)
            s = norm_vector(v, g, g.xn, n)
            s.then(v.tensor_scalar(g.eps0[:, :], g.eps0[:, :], 1.0, None, ALU.add))
            for t in range(NT):
                v.wait_ge(hi_cut, t + 1)
                v.tensor_tensor(g.rlo[:, t, :], g.xn[:, t, :], g.rhi[:, t, :].bitcast(F32),
                                ALU.subtract).then_inc(lo_cut, 1)
            for t in range(NT):
                v.wait_ge(lo_cut, t + 1)
                v.wait_ge(xed, t + 1)
                s.mark(v.tensor_scalar(g.xn[:, t, :], g.xn[:, t, :], g.eps0[0:TR, :], None, ALU.mult))

        @block.scalar
        def _(a):
            norm_scalar(a, g, n)
            for t in range(NT):
                a.wait_ge(n.normed, t + 1)
                a.activation(g.rhi[:, t, :], g.xn[:, t, :], ACT.Copy).then_inc(hi_cut, 1)

        @block.gpsimd
        def _(q):
            for t in range(NT):
                q.wait_ge(n.normed, t + 1)
                q.tensor_tensor(g.x_rows[:, t, :], g.x_rows[:, t, :], g.xn[:, t, :],
                                ALU.add).then_inc(xed, 1)


def cut_products(t, out, stat, mov, start, stop):
    t.matmul(out, stat[0], mov[0], start=start, stop=False)
    t.matmul(out, stat[0], mov[1], start=False, stop=False)
    return t.matmul(out, stat[1], mov[0], start=False, stop=stop)


def phase_gather0(nc, sem, g):
    RING = 2
    chunk = g.a0chunk
    cut = sem("g0_cut")
    used = sem("g0_used")
    summed = sem("g0_summed")
    hi_cut = sem("g0_hi")
    lo_cut = sem("g0_lo")
    order = [(b, k) for b in range(3) for k in range(NT)]

    with nc.Block() as block:
        @block.scalar
        def _(a):
            def drain(b):
                lo, hi = BLOCKS[b]
                a.wait_ge(summed, b + 1)
                for d in range(KD):
                    a.activation(g.thi[:, d, lo:hi], g.psum[:, b % 2 * 4 + d, 0:hi - lo],
                                 ACT.Copy).then_inc(hi_cut, 1)

            for i, (b, k) in enumerate(order):
                if k == 2 and b:
                    drain(b - 1)
                lo, hi = BLOCKS[b]
                if i >= RING:
                    a.wait_ge(used, i - RING + 1)
                a.activation(chunk[:, i % RING, 0:hi - lo], g.A0T[0:TR, k, lo:hi], ACT.Copy).then_inc(cut, 1)
            drain(2)

        @block.tensor
        def _(t):
            for i, (b, k) in enumerate(order):
                lo, hi = BLOCKS[b]
                if k == 0 and b == 2:
                    t.wait_ge(lo_cut, KD)
                t.wait_ge(cut, i + 1)
                for d in range(KD):
                    ps = g.psum[:, b % 2 * 4 + d, 0:hi - lo]
                    t.matmul(ps, g.rhi[:, k, d * 128:(d + 1) * 128], chunk[:, i % RING, 0:hi - lo],
                             start=k == 0, stop=False)
                    ins = t.matmul(ps, g.rlo[:, k, d * 128:(d + 1) * 128], chunk[:, i % RING, 0:hi - lo],
                                   start=False, stop=False)
                ins.then_inc(used, 1)
                if k == NT - 1:
                    for tile, p0, p1 in pieces(lo, hi):
                        o = tile * TR + p0 - lo
                        for d in range(KD):
                            ins = t.matmul(g.psum[:, b % 2 * 4 + d, o:o + p1 - p0],
                                           g.xn[:, tile, d * 128:(d + 1) * 128], g.ident[0:TR, p0:p1],
                                           start=False, stop=tile * TR + p1 >= hi)
                    ins.then_inc(summed, 1)

        @block.vector
        def _(v):
            for b, (lo, hi) in enumerate(BLOCKS):
                for d in range(KD):
                    v.wait_ge(hi_cut, b * KD + d + 1)
                    v.tensor_tensor(g.tlo[:, d, lo:hi], g.psum[:, b % 2 * 4 + d, 0:hi - lo],
                                    g.thi[:, d, lo:hi].bitcast(F32), ALU.subtract).then_inc(lo_cut, 1)


def bn_scale_shift(v, s, g, var, dev, n, mean, var_ap, bias, gamma, beta, scale, shift, scratch):
    v.tensor_scalar(scratch[0], var_ap, EPS, None, ALU.add).then_inc(var, 1)
    s.then(v.tensor_tensor(scratch[1], mean, bias, ALU.add))
    s.then(v.tensor_tensor(scratch[1], bias, scratch[1], ALU.subtract))
    v.wait_ge(dev, n)
    s.then(v.reciprocal(scratch[3], scratch[2]))
    s.then(v.tensor_tensor(scale, scratch[3], gamma, ALU.mult))
    s.then(v.tensor_tensor(scratch[1], scratch[1], scale, ALU.mult))


def phase_mlp1(nc, sem, g):
    room = Room(nc, g.w1_at)
    raw = room("W1_raw", [128, 2, KD, 256], F32)
    whi = room("W1_hi", [128, 2, KD, 128], F32R)
    wlo = room("W1_lo", [128, 2, KD, 128], F32R)

    loaded = [sem("m1_loaded0"), sem("m1_loaded1")]
    hi_cut = sem("m1_hi")
    lo_cut = sem("m1_lo")
    summed = sem("m1_summed")
    own = sem("m1_own")
    var = sem("m1_var")
    dev = sem("m1_dev")
    scaled = sem("m1_scaled")
    drained = sem("m1_drained")
    bn = g.bn

    with nc.Block() as block:
        @block.sync
        def _(sp):
            for p in range(KH0 // 2):
                if p >= 2:
                    sp.wait_ge(lo_cut, 2 * (p - 1))
                sp.dma_start(raw[:, p % 2], g.gnn0_W1.rearrange("(k p) h -> p k h", p=128)[
                    :, :, p * 256:(p + 1) * 256]).then_inc(loaded[p % 2], 16)
            sp.dma_start(g.W2_raw[:, :, :], g.gnn0_W2.rearrange("(k p) d -> p k d", p=128)).then_inc(
                g.W2_loaded, 16)

        @block.vector
        def _(v):
            s = Steps(v, own)

            def cut(m):
                p = m // 2
                v.wait_ge(loaded[p % 2], 16 * (p // 2 + 1))
                if m >= 2:
                    v.wait_ge(summed, m - 1)
                of = raw[:, p % 2, :, m % 2 * 128:(m % 2 + 1) * 128]
                v.tensor_copy(whi[:, m % 2], of).then_inc(hi_cut, 1)
                v.wait_ge(hi_cut, m + 1)
                v.tensor_tensor(wlo[:, m % 2], of, whi[:, m % 2].bitcast(F32), ALU.subtract).then_inc(lo_cut, 1)

            cut(0)
            cut(1)
            for m in range(KH0):
                v.wait_ge(summed, m + 1)
                for b, (lo, hi) in enumerate(BLOCKS):
                    s.mark(v.bn_stats(bn.stats[:, b, :], g.psum[:, m % 2 * 3 + b, 0:hi - lo]))
                s.wait()
                s.then(v.bn_aggr(bn.mv[:, :], bn.stats[:, 0:3, :]))
                c = slice(m, m + 1)
                bn_scale_shift(v, s, g, var, dev, m + 1, bn.mv[:, 0:1], bn.mv[:, 1:2], g.b1v[:, c], g.g1v[:, c],
                               g.be1v[:, c], bn.scale[:, c], None,
                               [bn.a[:, c], bn.b[:, c], bn.c[:, c], bn.d[:, c]])
                v.tensor_tensor(bn.shift[:, c], bn.b[:, c], g.be1v[:, c], ALU.add).then_inc(scaled, 1)
                if m + 2 < KH0:
                    cut(m + 2)

        @block.scalar
        def _(a):
            for m in range(KH0):
                a.wait_ge(var, m + 1)
                a.activation(bn.c[:, m:m + 1], bn.a[:, m:m + 1], ACT.Sqrt).then_inc(dev, 1)
                a.wait_ge(scaled, m + 1)
                for b, (lo, hi) in enumerate(BLOCKS):
                    a.activation(g.h1[:, m, lo:hi], g.psum[:, m % 2 * 3 + b, 0:hi - lo], ACT.Relu,
                                 bias=bn.shift[:, m:m + 1], scale=bn.scale[:, m:m + 1]).then_inc(drained, 1)

        @block.tensor
        def _(t):
            for m in range(KH0):
                t.wait_ge(lo_cut, m + 1)
                if m >= 2:
                    t.wait_ge(drained, 3 * (m - 1))
                for b, (lo, hi) in enumerate(BLOCKS):
                    for k in range(KD):
                        ins = cut_products(t, g.psum[:, m % 2 * 3 + b, 0:hi - lo],
                                           (whi[:, m % 2, k, :], wlo[:, m % 2, k, :]),
                                           (g.thi[:, k, lo:hi], g.tlo[:, k, lo:hi]), k == 0, k == KD - 1)
                ins.then_inc(summed, 1)


def phase_mlp2(nc, sem, g):
    RING = 3
    room = Room(nc, g.w2_cut_at)
    whi = room("W2_hi", [128, KH0, D], F32R)
    wlo = room("W2_lo", [128, KH0, D], F32R)
    hhi = room("h1_hi", [128, RING, BW], F32R)
    hlo = room("h1_lo", [128, RING, BW], F32R)

    w_hi = sem("m2_whi")
    w_lo = sem("m2_wlo")
    hi_cut = sem("m2_hi")
    lo_cut = sem("m2_lo")
    used = sem("m2_used")
    summed = sem("m2_summed")
    drained = sem("m2_drained")
    own = sem("m2_own")
    var = sem("m2_var")
    dev = sem("m2_dev")
    scaled = sem("m2_scaled")
    done = sem("m2_done")
    order = [(b, k) for b in range(3) for k in range(KH0)]
    bn = g.bn

    with nc.Block() as block:
        @block.scalar
        def _(a):
            def drain(b):
                lo, hi = BLOCKS[b]
                a.wait_ge(summed, b + 1)
                for d in range(KD):
                    a.activation(g.yT[:, d, lo:hi], g.psum[:, b % 2 * 4 + d, 0:hi - lo],
                                 ACT.Copy).then_inc(drained, 1)

            for i, (b, k) in enumerate(order):
                if k == 2 and b:
                    drain(b - 1)
                lo, hi = BLOCKS[b]
                if i >= RING:
                    a.wait_ge(used, i - RING + 1)
                a.activation(hhi[:, i % RING, 0:hi - lo], g.h1[:, k, lo:hi], ACT.Copy).then_inc(hi_cut, 1)
            drain(2)
            a.wait_ge(var, 1)
            a.activation(bn.c[:, 0:KD], bn.a[:, 0:KD], ACT.Sqrt).then_inc(dev, 1)
            a.wait_ge(scaled, 1)
            for d in range(KD):
                a.activation(g.yT[:, d, :], g.yT[:, d, :], ACT.Relu, bias=bn.shift[:, d:d + 1],
                             scale=bn.scale[:, d:d + 1]).then_inc(done, 1)

        @block.vector
        def _(v):
            s = Steps(v, own)
            v.wait_ge(g.W2_loaded, 16)
            for i, (b, k) in enumerate(order):
                lo, hi = BLOCKS[b]
                if b == 0:
                    v.tensor_copy(whi[:, k, :], g.W2_raw[:, k, :]).then_inc(w_hi, 1)
                    v.wait_ge(w_hi, k + 1)
                    v.tensor_tensor(wlo[:, k, :], g.W2_raw[:, k, :], whi[:, k, :].bitcast(F32),
                                    ALU.subtract).then_inc(w_lo, 1)
                v.wait_ge(hi_cut, i + 1)
                if i >= RING:
                    v.wait_ge(used, i - RING + 1)
                v.tensor_tensor(hlo[:, i % RING, 0:hi - lo], g.h1[:, k, lo:hi],
                                hhi[:, i % RING, 0:hi - lo].bitcast(F32), ALU.subtract).then_inc(lo_cut, 1)
            for b, (lo, hi) in enumerate(BLOCKS):
                v.wait_ge(drained, KD * (b + 1))
                for d in range(KD):
                    s.mark(v.bn_stats(bn.stats[:, d * 3 + b, :], g.yT[:, d, lo:hi]))
            s.wait()
            for d in range(KD):
                s.mark(v.bn_aggr(bn.mv4[:, d, :], bn.stats[:, 3 * d:3 * d + 3, :]))
            s.wait()
            bn_scale_shift(v, s, g, var, dev, 1, bn.mv4[:, :, 0], bn.mv4[:, :, 1], g.b2v[:, :], g.g2v[:, :],
                           g.be2v[:, :], bn.scale[:, 0:KD], None,
                           [bn.a[:, 0:KD], bn.b[:, 0:KD], bn.c[:, 0:KD], bn.d[:, 0:KD]])
            v.tensor_tensor(bn.shift[:, 0:KD], bn.b[:, 0:KD], g.be2v[:, :], ALU.add).then_inc(scaled, 1)

        @block.tensor
        def _(t):
            for i, (b, k) in enumerate(order):
                lo, hi = BLOCKS[b]
                if b == 0:
                    t.wait_ge(w_lo, k + 1)
                if b == 2 and k == 0:
                    t.wait_ge(drained, KD)
                t.wait_ge(lo_cut, i + 1)
                for d in range(KD):
                    f = slice(d * 128, (d + 1) * 128)
                    ins = cut_products(t, g.psum[:, b % 2 * 4 + d, 0:hi - lo], (whi[:, k, f], wlo[:, k, f]),
                                       (hhi[:, i % RING, 0:hi - lo], hlo[:, i % RING, 0:hi - lo]),
                                       k == 0, k == KH0 - 1)
                ins.then_inc(used, 1)
                if k == KH0 - 1:
                    t.matmul(g.psum[:, b % 2 * 4 + 3, 0:2], g.zeros[:, :], g.zeros[:, 0:2], start=False,
                             stop=True, skip_group_check=True).then_inc(summed, 1)


def add_turned(nc, sem, g, name, cols):
    turned = sem(name + "_turned")
    added = sem(name + "_added")
    with nc.Block() as block:
        @block.tensor
        def _(t):
            for i in range(NT):
                if i >= 8:
                    t.wait_ge(added, i - 7)
                for d in range(KD):
                    ins = t.transpose(g.psum[0:TR, i % 8, d * 128:(d + 1) * 128],
                                      cols[:, d, i * TR:(i + 1) * TR], g.ident[:, :])
                ins.then_inc(turned, 1)

        @block.vector
        def _(v):
            for i in range(NT):
                v.wait_ge(turned, i + 1)
                v.tensor_tensor(g.x_rows[:, i, :], g.x_rows[:, i, :], g.psum[0:TR, i % 8, :],
                                ALU.add).then_inc(added, 1)


def norm_and_turn(nc, sem, g, name, rows, thi, tlo):
    n = norm_sems(sem, name)
    turned = sem(name + "_turned")
    hi_cut = sem(name + "_hi")
    lo_cut = sem(name + "_lo")

    def cols(i):
        return g.psum[:, i % 8, 0:KD * TR].rearrange("p (k c) -> p k c", k=KD)

    with nc.Block() as block:
        @block.vector
        def _(v):
            norm_vector(v, g, rows, n)
            for i in range(NT):
                v.wait_ge(hi_cut, i + 1)
                v.tensor_tensor(tlo[:, :, i * TR:(i + 1) * TR], cols(i),
                                thi[:, :, i * TR:(i + 1) * TR].bitcast(F32), ALU.subtract).then_inc(lo_cut, 1)

        @block.scalar
        def _(a):
            norm_scalar(a, g, n)
            for i in range(NT):
                a.wait_ge(turned, i + 1)
                a.activation(thi[:, :, i * TR:(i + 1) * TR], cols(i), ACT.Copy).then_inc(hi_cut, 1)

        @block.tensor
        def _(t):
            for i in range(NT):
                t.wait_ge(n.normed, i + 1)
                if i >= 8:
                    t.wait_ge(lo_cut, i - 7)
                for k in range(KD):
                    ins = t.transpose(g.psum[:, i % 8, k * TR:(k + 1) * TR], rows[:, i, k * 128:(k + 1) * 128],
                                      g.ident[0:TR, 0:TR])
                ins.then_inc(turned, 1)


def phase_route(nc, sem, g):
    room = Room(nc, g.route_at)
    ghi = room("gate_hi", [128, KD, 128], F32R)
    glo = room("gate_lo", [128, KD, 128], F32R)
    gT = room("gates_T", [NE, N], F32)
    P = room("plan", [TR, NT, 128], F32)
    V = room("plan_T", [128, N], F32)
    above = room("above", [128, N], F32)
    equal = room("equal", [128, N], F32)
    cum = room("equal_so_far", [128, N], F32)
    small = Room(nc, g.route_small)
    colsum = small("colsum", [TR, NE], F32)
    rcol = small("rcol", [TR, NE], F32)
    rowsum = small("rowsum", [TR, NT], F32)
    rrow = small("rrow", [TR, NT], F32)
    bits = small("threshold_bits", [128, 1], I32)
    cand = small("candidate_bits", [128, 1], I32)
    count = small("count", [128, 1], F32)
    enough = small("enough", [128, 1], F32)
    nth = small("nth", [128, 1], I32)
    nths = small("nth_shifted", [128, 1], I32)
    need = small("need", [128, 1], F32)
    chosen_by = small("chosen_by", [TR, NT], F32)
    share = small("share", [TR, NT], F32)

    own = sem("r_own")
    cut = sem("r_cut")
    gated = sem("r_gated")
    copied = sem("r_copied")
    turned = sem("r_turned")
    to_sum = sem("r_to_sum")
    cols_summed = sem("r_cols_summed")
    planned = sem("r_planned")
    plan_turned = sem("r_plan_turned")
    spread = sem("r_spread")
    to_count = sem("r_to_count")
    counted = sem("r_counted")
    selected = sem("r_selected")
    back = sem("r_back")
    plan = P[:, :, 0:NE]

    with nc.Block() as block:
        @block.vector
        def _(v):
            s = Steps(v, own)
            s.mark(v.memset(ghi[:, :, :].bitcast(F32), 0.0))
            s.mark(v.memset(glo[:, :, :].bitcast(F32), 0.0))
            s.mark(v.memset(bits[:, :], 0))
            s.then(v.memset(P[:, :, :], 0.0))
            s.then(v.tensor_copy(ghi[:, :, 0:NE], g.gate[:, :, :]))
            v.tensor_tensor(glo[:, :, 0:NE], g.gate[:, :, :], ghi[:, :, 0:NE].bitcast(F32),
                            ALU.subtract).then_inc(cut, 1)
            v.wait_ge(turned, 1)
            s.then(v.tensor_scalar(plan, g.psum[0:TR, 3, 0:NT * NE].rearrange("p (t e) -> p t e", t=NT),
                                   FLOOR, None, ALU.max))
            for i in range(SINKHORN):
                v.tensor_reduce(colsum[:, :], plan.rearrange("p t e -> p e t"), X, ALU.add).then_inc(to_sum, 1)
                v.wait_ge(cols_summed, i + 1)
                s.then(v.reciprocal(rcol[:, :], g.psum[0:TR, 4, 0:NE]))
                s.then(v.tensor_tensor(plan, plan, rcol[:, :].unsqueeze(1).to_broadcast([TR, NT, NE]), ALU.mult))
                s.then(v.tensor_reduce(rowsum[:, :], plan, X, ALU.add))
                s.then(v.reciprocal(rrow[:, :], rowsum[:, :]))
                s.then(v.tensor_tensor(plan, plan, rrow[:, :].unsqueeze(2).to_broadcast([TR, NT, NE]), ALU.mult))
            v.sem_inc(planned, 1)
            v.wait_ge(spread, 3)
            for r, shift in enumerate(SHIFTS):
                s.then(v.tensor_tensor(cand[:, :], bits[:, :], g.kshift[:, r:r + 1], ALU.bitwise_or))
                s.then(v.tensor_scalar(above[:, :], V[:, :], cand[:, :].bitcast(F32), 0.0, ALU.is_ge, ALU.add,
                                       accum_out=count[:, :]))
                v.tensor_scalar(enough[:, :], count[:, :], float(TOP), None, ALU.is_ge).then_inc(to_count, 1)
                v.wait_ge(counted, r + 1)
                s.then(v.tensor_scalar(nth[:, :], g.psum[:, 4, 16:17], -1.0, None, ALU.add))
                s.then(v.tensor_single_scalar(nths[:, :], nth[:, :], shift, ALU.logical_shift_left))
                s.then(v.tensor_tensor(bits[:, :], bits[:, :], nths[:, :], ALU.bitwise_or))
            least = bits[:, :].bitcast(F32)
            s.mark(v.tensor_scalar(above[:, :], V[:, :], least, 0.0, ALU.is_gt, ALU.add, accum_out=count[:, :]))
            s.then(v.tensor_scalar(equal[:, :], V[:, :], least, None, ALU.is_equal))
            s.mark(v.tensor_scalar(need[:, :], count[:, :], -1.0, float(TOP), ALU.mult, ALU.add))
            s.then(v.tensor_tensor_scan(cum[:, :], equal[:, :], equal[:, :], 0.0, ALU.add, ALU.max))
            s.then(v.scalar_tensor_tensor(out=equal[:, :], in0=cum[:, :], scalar=need[:, :], in1=equal[:, :],
                                          op0=ALU.is_le, op1=ALU.mult))
            s.then(v.tensor_tensor(above[:, :], above[:, :], equal[:, :], ALU.add))
            s.then(v.scalar_tensor_tensor(out=equal[:, :], in0=V[:, :], scalar=0.5, in1=above[:, :],
                                          op0=ALU.is_gt, op1=ALU.mult))
            v.sem_inc(selected, 1)
            v.wait_ge(back, 1)

            def by_token(bank):
                flat = g.psum[0:TR, bank:bank + 3, :].rearrange("p a b -> p (a b)")
                return flat[:, 0:NT * 128].rearrange("p (t e c) -> p t e c", t=NT, e=NE)[:, :, :, 0]

            s.then(v.tensor_reduce(chosen_by[:, :], by_token(0), X, ALU.add))
            s.then(v.tensor_scalar(chosen_by[:, :], chosen_by[:, :], 1.0, None, ALU.add))
            s.then(v.reciprocal(share[:, :], chosen_by[:, :]))
            s.then(v.tensor_tensor(g.mix[:, :, :], by_token(3), share[:, :].unsqueeze(2).to_broadcast([TR, NT, NE]),
                                   ALU.mult))

        @block.tensor
        def _(t):
            t.wait_ge(cut, 1)
            for b, (lo, hi) in enumerate(BLOCKS):
                for k in range(KD):
                    ins = cut_products(t, g.psum[:, b, 0:hi - lo], (ghi[:, k, :], glo[:, k, :]),
                                       (g.cthi[:, k, lo:hi], g.ctlo[:, k, lo:hi]), k == 0, k == KD - 1)
            ins.then_inc(gated, 1)
            t.wait_ge(copied, 3)
            for i in range(NT):
                ins = t.transpose(g.psum[0:TR, 3, i * NE:(i + 1) * NE], gT[:, i * TR:(i + 1) * TR],
                                  g.ident[0:NE, 0:NE])
            ins.then_inc(turned, 1)
            for i in range(SINKHORN):
                t.wait_ge(to_sum, i + 1)
                t.matmul(g.psum[0:TR, 4, 0:NE], g.ones[0:TR, 0:TR], colsum[:, :], start=True,
                         stop=True).then_inc(cols_summed, 1)
            t.wait_ge(planned, 1)
            for i in range(NT):
                ins = t.transpose(g.psum[:, 5 + i // 4, i % 4 * TR:(i % 4 + 1) * TR], P[:, i, :],
                                  g.ident[0:TR, 0:TR])
            ins.then_inc(plan_turned, 1)
            t.wait_ge(copied, 6)
            for b, (lo, hi) in enumerate(BLOCKS):
                t.matmul(g.psum[:, b, 0:hi - lo], g.sel16[0:NE, :], gT[:, lo:hi], start=True,
                         stop=True).then_inc(gated, 1)
            for r in range(len(SHIFTS)):
                t.wait_ge(to_count, r + 1)
                t.matmul(g.psum[:, 4, 16:17], g.blk16[:, :], enough[:, :], start=True, stop=True).then_inc(counted, 1)
            t.wait_ge(selected, 1)
            for bank, of in ((0, above), (3, equal)):
                for i in range(NT):
                    ins = t.transpose(g.psum[0:TR, bank + i // 4, i % 4 * 128:(i % 4 + 1) * 128],
                                      of[:, i * TR:(i + 1) * TR], g.ident[:, :])
            ins.then_inc(back, 1)

        @block.scalar
        def _(a):
            a.wait_ge(gated, 1)
            for b, (lo, hi) in enumerate(BLOCKS):
                a.activation(gT[:, lo:hi], g.psum[0:NE, b, 0:hi - lo], ACT.Copy).then_inc(copied, 1)
            a.wait_ge(plan_turned, 1)
            for i in range(3):
                n = min(4, NT - 4 * i) * TR
                a.activation(gT[:, 4 * i * TR:4 * i * TR + n], g.psum[0:NE, 5 + i, 0:n],
                             ACT.Copy).then_inc(copied, 1)
            for b, (lo, hi) in enumerate(BLOCKS):
                a.wait_ge(gated, b + 2)
                a.activation(V[:, lo:hi], g.psum[:, b, 0:hi - lo], ACT.Copy).then_inc(spread, 1)


def phase_experts(nc, sem, g):
    room = Room(nc, g.experts_at)
    raw = room("expert_raw", [128, 2, KD, D], F32)
    whi = room("expert_hi", [128, 2, KD, D], F32R)
    wlo = room("expert_lo", [128, 2, KD, D], F32R)

    loaded = [sem("x_loaded0"), sem("x_loaded1")]
    hi_cut = sem("x_hi")
    lo_cut = sem("x_lo")
    summed = sem("x_summed")
    added = sem("x_added")

    with nc.Block() as block:
        @block.sync
        def _(sp):
            with sp.Fori(0, NE // 2) as i:
                for u in range(2):
                    sp.wait_ge(lo_cut, i * 2 + u + 1)
                    sp.dma_start(raw[:, u], g.experts[bass.ds(i * 2 + u, 1)].rearrange(
                        "e (k p) d -> p (e k) d", p=128)).then_inc(loaded[u], 16)

        @block.scalar
        def _(a):
            with a.Fori(0, NE // 2) as i:
                for u in range(2):
                    a.wait_ge(loaded[u], i * 16 + 16)
                    a.wait_ge(summed, i * (2 * NT) + (u + 1) * NT)
                    a.activation(whi[:, u], raw[:, u], ACT.Copy).then_inc(hi_cut, 1)

        @block.tensor
        def _(t):
            t.sem_inc(summed, 2 * NT)
            with t.Fori(0, NE // 2) as i:
                for u in range(2):
                    t.wait_ge(lo_cut, i * 2 + u + 3)
                    for r in range(NT):
                        j = u * NT + r
                        t.wait_ge(added, i * (2 * NT) + j + 1)
                        for k in range(KD):
                            ins = cut_products(t, g.psum[0:TR, j % 4, :],
                                               (g.cthi[:, k, r * TR:(r + 1) * TR],
                                                g.ctlo[:, k, r * TR:(r + 1) * TR]),
                                               (whi[:, u, k, :], wlo[:, u, k, :]), k == 0, k == KD - 1)
                        ins.then_inc(summed, 1)

        @block.vector
        def _(v):
            v.sem_inc(lo_cut, 2)
            v.sem_inc(added, 4)

            def cut(i, u):
                v.wait_ge(hi_cut, i * 2 + u + 1)
                v.tensor_tensor(wlo[:, u], raw[:, u], whi[:, u].bitcast(F32), ALU.subtract).then_inc(lo_cut, 1)

            cut(0, 0)

            def expert(i, u, more):
                for r in range(NT):
                    j = u * NT + r
                    v.wait_ge(summed, i * (2 * NT) + 2 * NT + j + 1)
                    v.scalar_tensor_tensor(out=g.x_rows[:, r, :], in0=g.psum[0:TR, j % 4, :],
                                           scalar=g.mix[:, r, bass.ds(i * 2 + u, 1)], in1=g.x_rows[:, r, :],
                                           op0=ALU.mult, op1=ALU.add).then_inc(added, 1)
                    if r == 1 and more:
                        cut(i + u, 1 - u)

            with v.Fori(0, NE // 2 - 1) as i:
                expert(i, 0, True)
                expert(i, 1, True)
            expert(NE // 2 - 1, 0, True)
            expert(NE // 2 - 1, 1, False)


def phase_norm1(nc, sem, g):
    n = norm_sems(sem, "n1")
    hi_cut = sem("n1_hi")
    lo_cut = sem("n1_lo")
    w_loaded = sem("n1_w")
    turned = sem("n1_turned")
    w_hi = sem("n1_whi")
    w_lo = sem("n1_wlo")

    with nc.Block() as block:
        @block.sync
        def _(sp):
            sp.dma_start(g.W_rows[:, :, :], g.gnn1_weight.rearrange("(o p) d -> p o d", p=128)).then_inc(w_loaded, 16)

        @block.vector
        def _(v):
            norm_vector(v, g, g.xn1, n)
            for t in range(NT):
                v.wait_ge(hi_cut, t + 1)
                v.tensor_tensor(g.r1lo[:, t, :], g.xn1[:, t, :], g.r1hi[:, t, :].bitcast(F32),
                                ALU.subtract).then_inc(lo_cut, 1)
            for k in range(KD):
                v.wait_ge(w_hi, k + 1)
                v.tensor_tensor(g.WTlo[:, k, :], g.psum[:, k, :], g.WThi[:, k, :].bitcast(F32),
                                ALU.subtract).then_inc(w_lo, 1)

        @block.scalar
        def _(a):
            for k in range(KD):
                a.wait_ge(turned, k + 1)
                a.activation(g.WThi[:, k, :], g.psum[:, k, :], ACT.Copy).then_inc(w_hi, 1)
            norm_scalar(a, g, n)
            for t in range(NT):
                a.wait_ge(n.normed, t + 1)
                a.activation(g.r1hi[:, t, :], g.xn1[:, t, :], ACT.Copy).then_inc(hi_cut, 1)

        @block.tensor
        def _(t):
            t.wait_ge(w_loaded, 16)
            for k in range(KD):
                for o in range(KD):
                    ins = t.transpose(g.psum[:, k, o * 128:(o + 1) * 128],
                                      g.W_rows[:, o, k * 128:(k + 1) * 128], g.ident[:, :])
                ins.then_inc(turned, 1)


def phase_turn(nc, sem, g):
    turned = sem("tn_turned")
    moved = sem("tn_moved")
    A = g.A1T
    groups = [(t, c, min(4, NT - c)) for t in range(NT) for c in range(t, NT, 4)]

    with nc.Block() as block:
        @block.tensor
        def _(t):
            for i, (r, c0, n) in enumerate(groups):
                if i >= 4:
                    t.wait_ge(moved, 2 * (i - 3))
                for j in range(n):
                    t.transpose(g.psum[0:TR, i % 4 * 2, j * TR:(j + 1) * TR],
                                A[0:TR, c0 + j, r * TR:(r + 1) * TR], g.ident[0:TR, 0:TR])
                    ins = t.transpose(g.psum[0:TR, i % 4 * 2 + 1, j * TR:(j + 1) * TR],
                                      A[0:TR, r, (c0 + j) * TR:(c0 + j + 1) * TR], g.ident[0:TR, 0:TR])
                ins.then_inc(turned, 1)

        @block.scalar
        def _(a):
            for i, (r, c0, n) in enumerate(groups):
                a.wait_ge(turned, i + 1)
                a.activation(A[0:TR, r, c0 * TR:(c0 + n) * TR], g.psum[0:TR, i % 4 * 2, 0:n * TR],
                             ACT.Copy).then_inc(moved, 1)
                a.wait_ge(moved, 2 * i + 1)
                a.activation(A[0:TR, c0:c0 + n, r * TR:(r + 1) * TR],
                             g.psum[0:TR, i % 4 * 2 + 1, 0:n * TR].rearrange("p (c w) -> p c w", c=n),
                             ACT.Copy).then_inc(moved, 1)


def phase_gather1(nc, sem, g):
    RING = 3
    hi_cut = sem("g1_hi")
    lo_cut = sem("g1_lo")
    used = sem("g1_used")
    summed = sem("g1_summed")
    t_hi = sem("g1_thi")
    t_lo = sem("g1_tlo")
    order = [(b, k) for b in range(3) for k in range(NT)]
    chi, clo = g.a1hi, g.a1lo

    with nc.Block() as block:
        @block.scalar
        def _(a):
            def drain(b):
                lo, hi = BLOCKS[b]
                a.wait_ge(summed, b + 1)
                for d in range(KD):
                    a.activation(g.gthi[:, d, lo:hi], g.psum[:, b % 2 * 4 + d, 0:hi - lo],
                                 ACT.Copy).then_inc(t_hi, 1)

            for i, (b, k) in enumerate(order):
                if k == 2 and b:
                    drain(b - 1)
                lo, hi = BLOCKS[b]
                if i >= RING:
                    a.wait_ge(used, i - RING + 1)
                a.activation(chi[:, i % RING, 0:hi - lo], g.A1T[0:TR, k, lo:hi], ACT.Copy).then_inc(hi_cut, 1)
            drain(2)

        @block.vector
        def _(v):
            def drain(b):
                lo, hi = BLOCKS[b]
                for d in range(KD):
                    v.wait_ge(t_hi, b * KD + d + 1)
                    v.tensor_tensor(g.gtlo[:, d, lo:hi], g.psum[:, b % 2 * 4 + d, 0:hi - lo],
                                    g.gthi[:, d, lo:hi].bitcast(F32), ALU.subtract).then_inc(t_lo, 1)

            for i, (b, k) in enumerate(order):
                if k == 3 and b:
                    drain(b - 1)
                lo, hi = BLOCKS[b]
                v.wait_ge(hi_cut, i + 1)
                v.tensor_tensor(clo[:, i % RING, 0:hi - lo], g.A1T[0:TR, k, lo:hi],
                                chi[:, i % RING, 0:hi - lo].bitcast(F32), ALU.subtract).then_inc(lo_cut, 1)
            drain(2)

        @block.tensor
        def _(t):
            for i, (b, k) in enumerate(order):
                lo, hi = BLOCKS[b]
                if k == 0 and b == 2:
                    t.wait_ge(t_lo, KD)
                t.wait_ge(lo_cut, i + 1)
                for d in range(KD):
                    f = slice(d * 128, (d + 1) * 128)
                    ins = cut_products(t, g.psum[:, b % 2 * 4 + d, 0:hi - lo],
                                       (g.r1hi[:, k, f], g.r1lo[:, k, f]),
                                       (chi[:, i % RING, 0:hi - lo], clo[:, i % RING, 0:hi - lo]),
                                       k == 0, k == NT - 1)
                ins.then_inc(used, 1)
                if k == NT - 1:
                    t.matmul(g.psum[:, b % 2 * 4 + 3, 0:2], g.zeros[:, :], g.zeros[:, 0:2], start=False,
                             stop=True, skip_group_check=True).then_inc(summed, 1)


def phase_project(nc, sem, g):
    summed = sem("p_summed")
    added = sem("p_added")
    with nc.Block() as block:
        @block.tensor
        def _(t):
            for i in range(NT):
                if i >= 8:
                    t.wait_ge(added, i - 7)
                c = slice(i * TR, (i + 1) * TR)
                for k in range(KD):
                    ins = cut_products(t, g.psum[0:TR, i % 8, :], (g.gthi[:, k, c], g.gtlo[:, k, c]),
                                       (g.WThi[:, k, :], g.WTlo[:, k, :]), k == 0, k == KD - 1)
                ins.then_inc(summed, 1)

        @block.vector
        def _(v):
            for i in range(NT):
                v.wait_ge(summed, i + 1)
                v.tensor_tensor(g.x_rows[:, i, :], g.x_rows[:, i, :], g.psum[0:TR, i % 8, :],
                                ALU.add).then_inc(added, 1)


def phase_leaves(nc, sem, g):
    room = Room(nc, g.leaves_at)
    rhi = room("rw_hi", [128, KD, 128], F32R)
    rlo = room("rw_lo", [128, KD, 128], F32R)
    p7 = room("node_p", [7, N], F32)
    f = [room(f"factor{d}", [NE, N], F32) for d in range(3)]
    leaf = room("leaf", [NE, N], F32)

    own = sem("l_own")
    cut = sem("l_cut")
    summed = sem("l_summed")
    nodes = sem("l_nodes")
    spread = sem("l_spread")
    factors = sem("l_factors")
    ready = sem("l_ready")

    with nc.Block() as block:
        @block.vector
        def _(v):
            s = Steps(v, own)
            s.mark(v.memset(rhi[:, :, :].bitcast(F32), 0.0))
            s.mark(v.memset(rlo[:, :, :].bitcast(F32), 0.0))
            s.mark(v.tensor_scalar(g.b2half[:, :], g.vecs[:, 36:68], 0.5, None, ALU.mult))
            s.mark(v.memset(g.acc[:, :, :], 0.0))
            s.wait()
            rw = g.vecs[:, 68:96].rearrange("p (n k) -> p k n", n=7)
            s.then(v.tensor_copy(rhi[:, :, 0:7], rw))
            v.tensor_tensor(rlo[:, :, 0:7], rw, rhi[:, :, 0:7].bitcast(F32), ALU.subtract).then_inc(cut, 1)
            v.wait_ge(factors, 9)
            s.then(v.tensor_tensor(f[0][:, :], f[0][:, :], f[1][:, :], ALU.mult))
            v.tensor_tensor(leaf[:, :], f[0][:, :], f[2][:, :], ALU.mult).then_inc(ready, 1)

        @block.tensor
        def _(t):
            t.wait_ge(cut, 1)
            for b, (lo, hi) in enumerate(BLOCKS):
                for k in range(KD):
                    ins = cut_products(t, g.psum[:, b, 0:hi - lo], (rhi[:, k, :], rlo[:, k, :]),
                                       (g.fthi[:, k, lo:hi], g.ftlo[:, k, lo:hi]), k == 0, k == KD - 1)
                ins.then_inc(summed, 1)
            t.wait_ge(nodes, 3)
            for b, (lo, hi) in enumerate(BLOCKS):
                if b == 2:
                    t.wait_ge(factors, 3)
                for d in range(3):
                    t.matmul(g.psum[0:NE, b % 2 * 3 + d, 0:hi - lo], g.leafsel[0:7, 8 * d:8 * d + 8],
                             p7[:, lo:hi], start=True, stop=True).then_inc(spread, 1)

        @block.scalar
        def _(a):
            for b, (lo, hi) in enumerate(BLOCKS):
                a.wait_ge(summed, b + 1)
                a.activation(p7[:, lo:hi], g.psum[0:7, b, 0:hi - lo], ACT.Sigmoid,
                             bias=g.rb_col[0:7, :]).then_inc(nodes, 1)
            for b, (lo, hi) in enumerate(BLOCKS):
                for d in range(3):
                    a.wait_ge(spread, b * 3 + d + 1)
                    a.activation(f[d][:, lo:hi], g.psum[0:NE, b % 2 * 3 + d, 0:hi - lo], ACT.Identity,
                                 bias=g.leafone[0:NE, d:d + 1]).then_inc(factors, 1)

        @block.sync
        def _(sp):
            sp.wait_ge(ready, 1)
            sp.dma_start(g.leaf_dram, leaf[:, :]).then_inc(g.leaf_stored, 16)
            sp.wait_ge(g.leaf_stored, 16)


def phase_tree(nc, sem, g):
    PAIRS = HID1 // 256
    STEPS = 48
    room = Room(nc, g.tree_at)
    w1hi = room("w1_hi", [128, 4, KD, 256], F32R)
    w1lo = room("w1_lo", [128, 4, KD, 256], F32R)
    w2hi = room("w2_hi", [128, 4, 2, D], F32R)
    w2lo = room("w2_lo", [128, 4, 2, D], F32R)
    raw1 = room("w1_raw", [128, 2, KD, 256], F32)
    raw2 = room("w2_raw", [128, 2, 2, D], F32)
    room.next += COLS
    leafb = room("leaf_all", [128, N], F32)
    G = room("gelu", [128, 3, BW], F32)
    hhi = room("hidden_hi", [128, 4, BW], F32R)
    hlo = room("hidden_lo", [128, 4, BW], F32R)
    ytmp = room("y_scaled", [128, KD, BW], F32)

    loaded = [sem("t_loaded0"), sem("t_loaded1")]
    w_hi = sem("t_whi")
    cut = sem("t_cut")
    hidden = sem("t_hidden")
    begun = sem("t_begun")
    active = sem("t_active")
    hi_cut = sem("t_hi")
    lo_cut = sem("t_lo")
    used = sem("t_used")
    y_sum = sem("t_ysum")
    y_free = sem("t_yfree")
    acc_done = sem("t_acc")
    leaf_in = sem("t_leaf")

    w1_d = g.w1.rearrange("e (k p) h -> e p k h", p=128)
    w2_d = g.w2.rearrange("e (j p) d -> e p j d", p=128)

    def where(s):
        return s // 24, s % 24 // 8, s % 8 // 2, s % 2

    with nc.Block() as block:
        @block.sync
        def _(sp):
            with sp.Fori(0, NE) as e:
                for p in range(PAIRS):
                    if p == 4:
                        sp.wait_ge(y_free, e * 24 + 4)
                        sp.dma_start(leafb[:, :], g.leaf_dram[bass.ds(e, 1), :].partition_broadcast(128)
                                     ).then_inc(leaf_in, 16)
                    sp.wait_ge(cut, e * PAIRS + p + 1)
                    sp.dma_start(raw1[:, p % 2], w1_d[bass.ds(e, 1), :, :, p * 256:(p + 1) * 256].rearrange(
                        "e p k h -> p (e k) h")).then_inc(loaded[p % 2], 16)
                    sp.dma_start(raw2[:, p % 2], w2_d[bass.ds(e, 1), :, 2 * p:2 * p + 2, :].rearrange(
                        "e p j d -> p (e j) d")).then_inc(loaded[p % 2], 16)

        @block.vector
        def _(v):
            v.sem_inc(cut, 2)
            v.sem_inc(lo_cut, 3)
            v.sem_inc(y_free, 4)

            def cut1(e, p):
                q = p % 4
                v.wait_ge(loaded[p % 2], e * (16 * PAIRS) + 32 * (p // 2 + 1))
                v.wait_ge(used, (e * 2 + p // 4) * 24 + 18 + 2 * q)
                v.tensor_copy(w1hi[:, q], raw1[:, p % 2]).then_inc(w_hi, 1)
                v.wait_ge(w_hi, e * (2 * PAIRS) + 2 * p + 1)
                v.tensor_tensor(w1lo[:, q], raw1[:, p % 2], w1hi[:, q].bitcast(F32), ALU.subtract)

            def cut2(e, p):
                q = p % 4
                v.tensor_copy(w2hi[:, q], raw2[:, p % 2]).then_inc(w_hi, 1)
                v.wait_ge(w_hi, e * (2 * PAIRS) + 2 * p + 2)
                v.tensor_tensor(w2lo[:, q], raw2[:, p % 2], w2hi[:, q].bitcast(F32),
                                ALU.subtract).then_inc(cut, 1)

            def cuts(e, s, last):
                r = (s - 20) % 24
                if r < 8:
                    p = (s - 20) // 24 * 4 + 4 + r // 2
                    at = e
                    if p >= PAIRS:
                        if last:
                            return
                        at, p = e + 1, p - PAIRS
                    (cut2 if r % 2 else cut1)(at, p)

            def drain(e, m):
                lo, hi = BLOCKS[m % 3]
                if m == 0:
                    v.wait_ge(leaf_in, e * 16 + 16)
                for d in range(KD):
                    if d < 3:
                        v.wait_ge(y_sum, e * 18 + 3 * m + d + 1)
                    else:
                        v.wait_ge(used, e * STEPS + 24 + 8 * m + 8)
                    v.wait_ge(acc_done, e * 24 + 4 * m + d + 1)
                    v.scalar_tensor_tensor(out=ytmp[:, d, 0:hi - lo], in0=g.psum[:, d, 0:hi - lo],
                                           scalar=g.b2half[:, bass.ds(e * 4 + d, 1)], in1=leafb[:, lo:hi],
                                           op0=ALU.add, op1=ALU.mult).then_inc(y_free, 1)

            def expert(e, last):
                for s in range(STEPS):
                    half, b, _, _ = where(s)
                    w = BLOCKS[b][1] - BLOCKS[b][0]
                    v.wait_ge(hi_cut, e * STEPS + s + 1)
                    v.tensor_tensor(hlo[:, s % 4, 0:w], G[:, s % 3, 0:w], hhi[:, s % 4, 0:w].bitcast(F32),
                                    ALU.subtract).then_inc(lo_cut, 1)
                    if s % 8 == 0 and s:
                        drain(e, s // 8 - 1)
                    cuts(e, s, last)
                drain(e, 5)

            for p in range(2):
                cut1(0, p)
                cut2(0, p)
            with v.Fori(0, NE - 1) as e:
                expert(e, False)
            expert(NE - 1, True)

        @block.gpsimd
        def _(q):
            q.sem_inc(acc_done, 4)
            with q.Fori(0, NE) as e:
                for m in range(6):
                    lo, hi = BLOCKS[m % 3]
                    for d in range(KD):
                        q.wait_ge(y_free, e * 24 + 4 * m + d + 5)
                        q.tensor_tensor(g.acc[:, d, lo:hi], g.acc[:, d, lo:hi], ytmp[:, d, 0:hi - lo],
                                        ALU.add).then_inc(acc_done, 1)

        @block.scalar
        def _(a):
            a.sem_inc(active, 4)
            with a.Fori(0, NE) as e:
                for s in range(STEPS):
                    half, b, q, j = where(s)
                    w = BLOCKS[b][1] - BLOCKS[b][0]
                    a.wait_ge(hidden, e * STEPS + s + 1)
                    a.wait_ge(lo_cut, e * STEPS + s + 1)
                    a.sem_inc(begun, 1)
                    a.activation(G[:, s % 3, 0:w], g.psum[:, 4 + s % 4, 0:w], ACT.Gelu,
                                 bias=g.b1cols[:, bass.ds(e * 16 + half * 8 + 2 * q + j, 1)]).then_inc(active, 1)
                    a.wait_ge(active, e * STEPS + s + 5)
                    a.wait_ge(used, e * STEPS + s + 21)
                    a.activation(hhi[:, s % 4, 0:w], G[:, s % 3, 0:w], ACT.Copy).then_inc(hi_cut, 1)

        @block.tensor
        def _(t):
            t.sem_inc(used, 24)

            def first(e, s):
                half, b, q, j = where(s)
                lo, hi = BLOCKS[b]
                if b == 0 and j == 0:
                    t.wait_ge(cut, e * PAIRS + half * 4 + q + 3)
                t.wait_ge(active, e * STEPS + s + 1)
                c = slice(j * 128, (j + 1) * 128)
                for k in range(KD):
                    ins = cut_products(t, g.psum[:, 4 + s % 4, 0:hi - lo], (w1hi[:, q, k, c], w1lo[:, q, k, c]),
                                       (g.fthi[:, k, lo:hi], g.ftlo[:, k, lo:hi]), k == 0, k == KD - 1)
                ins.then_inc(hidden, 1)

            def second(e, s):
                half, b, q, j = where(s)
                w = BLOCKS[b][1] - BLOCKS[b][0]
                t.wait_ge(lo_cut, e * STEPS + s + 4)
                for d in range(KD):
                    if s % 8 == 0:
                        t.wait_ge(y_free, e * 24 + 4 * (s // 8) + d + 1)
                    c = slice(d * 128, (d + 1) * 128)
                    ins = cut_products(t, g.psum[:, d, 0:w], (w2hi[:, q, j, c], w2lo[:, q, j, c]),
                                       (hhi[:, s % 4, 0:w], hlo[:, s % 4, 0:w]), s % 8 == 0, s % 8 == 7)
                    if d == 3:
                        ins.then_inc(used, 1)
                    elif s % 8 == 7:
                        ins.then_inc(y_sum, 1)

            first(0, 0)
            first(0, 1)
            with t.Fori(0, NE - 1) as e:
                for s in range(STEPS):
                    second(e, s)
                    if s + 2 < STEPS:
                        first(e, s + 2)
                    else:
                        first(e + 1, s + 2 - STEPS)
            for s in range(STEPS):
                second(NE - 1, s)
                if s + 2 < STEPS:
                    first(NE - 1, s + 2)


def phase_out(nc, sem, g):
    turned = sem("o_turned")
    added = sem("o_added")
    stored = sem("o_stored")
    with nc.Block() as block:
        @block.tensor
        def _(t):
            for i in range(NT):
                if i >= 8:
                    t.wait_ge(added, i - 7)
                for d in range(KD):
                    ins = t.transpose(g.psum[0:TR, i % 8, d * 128:(d + 1) * 128],
                                      g.acc[:, d, i * TR:(i + 1) * TR], g.ident[:, :])
                ins.then_inc(turned, 1)

        @block.vector
        def _(v):
            for i in range(NT):
                v.wait_ge(turned, i + 1)
                v.tensor_tensor(g.x_rows[:, i, :], g.x_rows[:, i, :], g.psum[0:TR, i % 8, :],
                                ALU.add).then_inc(added, 1)

        @block.sync
        def _(sp):
            for i in range(NT):
                sp.wait_ge(added, i + 1)
                sp.dma_start(g.out[i * TR:(i + 1) * TR, :], g.x_rows[:, i, :]).then_inc(stored, 16)
            sp.wait_ge(stored, 16 * NT)


INPUTS = ["x", "src", "dst", "edge_weight", "gnn0_eps", "gnn0_W1", "gnn0_b1", "gnn0_g1", "gnn0_be1",
          "gnn0_W2", "gnn0_b2", "gnn0_g2", "gnn0_be2", "gate_w", "experts", "gnn1_weight", "rw", "rb",
          "w1", "b1", "w2", "b2", "consts_d", "bits_d"]


def gnn_ffn_kernel(nc, x, src, dst, edge_weight, gnn0_eps, gnn0_W1, gnn0_b1, gnn0_g1, gnn0_be1, gnn0_W2,
                   gnn0_b2, gnn0_g2, gnn0_be2, gate_w, experts, gnn1_weight, rw, rb, w1, b1, w2, b2,
                   consts_d, bits_d, out):
    with ExitStack() as ctx:
        def sem(name):
            return ctx.enter_context(nc.semaphore(name))

        g = Record()
        g.x, g.src, g.dst, g.edge_weight, g.out = x, src, dst, edge_weight, out
        g.gnn0_eps, g.gnn0_W1, g.gnn0_b1, g.gnn0_g1, g.gnn0_be1 = gnn0_eps, gnn0_W1, gnn0_b1, gnn0_g1, gnn0_be1
        g.gnn0_W2, g.gnn0_b2, g.gnn0_g2, g.gnn0_be2 = gnn0_W2, gnn0_b2, gnn0_g2, gnn0_be2
        g.gate_w, g.experts, g.gnn1_weight = gate_w, experts, gnn1_weight
        g.rw, g.rb, g.w1, g.b1, g.w2, g.b2 = rw, rb, w1, b1, w2, b2
        g.consts_d, g.bits_d = consts_d, bits_d
        g.psum = ctx.enter_context(nc.psum_tensor("psum", [128, 8, 512], F32))
        g.leaf_dram = nc.dram_tensor("leaf_rows", (NE, N), F32).ap()
        g.x_loaded, g.W2_loaded, g.leaf_stored = sem("x_loaded"), sem("W2_loaded"), sem("leaf_stored")

        keep = Room(nc, 0)
        g.small = keep("small_consts", [128, C_I10], F32)
        g.ident = g.small[:, C_ID:C_ID + 128]
        g.ones = g.small[:, C_ONE:C_ONE + 128]
        g.blk16 = g.small[:, C_BLK:C_BLK + 128]
        g.sel16 = g.small[:, C_SEL:C_SEL + 128]
        g.leafsel = g.small[:, C_LSEL:C_LSEL + 24]
        g.leafone = g.small[:, C_LONE:C_LONE + 3]
        g.rowno = g.small[:, C_ROW:C_ROW + 1]
        g.iota32 = g.small[:, C_I32:C_I32 + WIN]
        g.w2k = g.small[:, C_W2K:C_W2K + NW]
        g.blkno = g.small[:, C_BLKNO:C_BLKNO + NB]
        g.kshift = keep("kshift", [128, len(SHIFTS)], I32)
        g.eps0 = keep("eps0", [128, 1], F32)
        g.vecrows = keep("vecrows", [96, 128], F32)
        g.b1rows = keep("b1rows", [128, 128], F32)
        g.gate = keep("gate", [128, KD, NE], F32)
        g.rb_col = keep("rb_col", [7, 1], F32)
        g.vecs = keep("vecs", [128, 96], F32)
        g.b1v, g.g1v, g.be1v = g.vecs[:, 0:8], g.vecs[:, 8:16], g.vecs[:, 16:24]
        g.b2v, g.g2v, g.be2v = g.vecs[:, 24:28], g.vecs[:, 28:32], g.vecs[:, 32:36]
        g.b1cols = keep("b1cols", [128, 128], F32)
        g.b2half = keep("b2half", [128, 32], F32)
        g.zeros = keep("zeros", [128, 128], BF16)
        g.bounds = keep("bounds", [1, 2 * NW], I32)
        g.key = keep("key", [EB, NB + 2], F32)
        g.mix = keep("mix", [TR, NT, NE], F32)
        g.stats = keep("stats", [TR, NT, 6], F32)
        g.meanvar = keep("meanvar", [TR, NT, 2], F32)
        g.dev = keep("dev", [TR, NT], F32)
        g.dev2 = keep("dev2", [TR, NT], F32)
        g.rstd = keep("rstd", [TR, NT], F32)
        bn = g.bn = Record()
        bn.stats = keep("bn_stats", [128, 12, 6], F32)
        bn.mv = keep("bn_mv", [128, 2], F32)
        bn.mv4 = keep("bn_mv4", [128, KD, 2], F32)
        bn.a = keep("bn_var", [128, KH0], F32)
        bn.b = keep("bn_mean", [128, KH0], F32)
        bn.c = keep("bn_dev", [128, KH0], F32)
        bn.d = keep("bn_rdev", [128, KH0], F32)
        bn.scale = keep("bn_scale", [128, KH0], F32)
        bn.shift = keep("bn_shift", [128, KH0], F32)
        g.route_small = keep.next
        assert keep.next + 32 * 16 <= X_AT, keep.next
        g.x_rows = Room(nc, X_AT)("x_rows", [TR, NT, D], F32)

        room = Room(nc, REG)
        g.A1T = room("A1T", [128, NT, ND], F32)
        g.A0T = room("A0T", [128, NT, ND], BF16)
        g.D_all = room("dst_onehot", [EB, NB + 1, 4, WIN], BF16)
        g.D_flat = g.D_all[:, :, :, :].rearrange("p b a w -> p (b a w)")
        g.i10 = room("i10", [EB, NC], F16)
        g.scratch_at = room.next
        phase_edges(nc, sem, g)
        phase_adjacency(nc, sem, g)

        room = Room(nc, A1_END + NT * ND * 2)
        g.rhi = room("xn_hi", [TR, NT, D], F32R)
        g.rlo = room("xn_lo", [TR, NT, D], F32R)
        g.xn = room("xn", [TR, NT, D], F32)
        g.a0chunk = room("A0_chunk", [TR, 2, BW], F32R)
        g.thi = room("hT_hi", [128, KD, N], F32R)
        g.tlo = room("hT_lo", [128, KD, N], F32R)
        phase_norm0(nc, sem, g)
        phase_gather0(nc, sem, g)
        room = Room(nc, A1_END)
        g.h1 = room("h1", [128, KH0, N], F32)
        g.w1_at = room.next
        g.yT = room("yT", [128, KD, N], F32)
        g.W2_raw = room("W2_raw", [128, KH0, D], F32)
        g.w2_cut_at = room.next
        phase_mlp1(nc, sem, g)
        phase_mlp2(nc, sem, g)
        add_turned(nc, sem, g, "y0", g.yT)

        room = Room(nc, A1_END)
        g.experts_at = room.next
        room.next += 6 * KD * D * 4
        g.cthi = room("c_xT_hi", [128, KD, N], F32R)
        g.ctlo = room("c_xT_lo", [128, KD, N], F32R)
        g.route_at = room.next
        rows = Room(nc, g.route_at)("c_rows", [TR, NT, D], F32)
        norm_and_turn(nc, sem, g, "c", rows, g.cthi, g.ctlo)
        phase_route(nc, sem, g)
        phase_experts(nc, sem, g)

        room = Room(nc, A1_END)
        g.r1hi = room("d_rows_hi", [TR, NT, D], F32R)
        g.r1lo = room("d_rows_lo", [TR, NT, D], F32R)
        g.W_rows = room("W_rows", [128, KD, D], F32)
        g.WThi = room("WT_hi", [128, KD, D], F32R)
        g.WTlo = room("WT_lo", [128, KD, D], F32R)
        g.xn1 = Room(nc, room.next)("d_rows", [TR, NT, D], F32)
        g.gthi = room("aggT_hi", [128, KD, N], F32R)
        g.gtlo = room("aggT_lo", [128, KD, N], F32R)
        g.a1hi = room("A1_hi", [TR, 3, BW], F32R)
        g.a1lo = room("A1_lo", [TR, 3, BW], F32R)
        phase_turn(nc, sem, g)
        phase_norm1(nc, sem, g)
        phase_gather1(nc, sem, g)
        phase_project(nc, sem, g)

        room = Room(nc, REG)
        g.fthi = room("f_xT_hi", [128, KD, N], F32R)
        g.ftlo = room("f_xT_lo", [128, KD, N], F32R)
        g.tree_at = room.next
        acc_at = g.tree_at + 5 * 16384
        rows = Room(nc, acc_at)("f_rows", [TR, NT, D], F32)
        g.acc = Room(nc, acc_at)("acc", [128, KD, N], F32)
        norm_and_turn(nc, sem, g, "f", rows, g.fthi, g.ftlo)
        g.leaves_at = g.tree_at
        phase_leaves(nc, sem, g)
        phase_tree(nc, sem, g)
        phase_out(nc, sem, g)


def kernel(**inputs):
    import concourse.bacc as bacc
    from concourse.bass_utils import run_bass_kernel_spmd

    nc = bacc.Bacc("TRN2", target_bir_lowering=False, num_devices=1)
    names = {
        "gnn0_eps": "L0_gnn_eps", "gnn0_W1": "L0_gnn_W1", "gnn0_b1": "L0_gnn_b1", "gnn0_g1": "L0_gnn_g1",
        "gnn0_be1": "L0_gnn_be1", "gnn0_W2": "L0_gnn_W2", "gnn0_b2": "L0_gnn_b2", "gnn0_g2": "L0_gnn_g2",
        "gnn0_be2": "L0_gnn_be2", "gate_w": "L0_ffn_gate_w", "experts": "L0_ffn_experts",
        "gnn1_weight": "L1_gnn_weight", "rw": "L1_ffn_rw", "rb": "L1_ffn_rb", "w1": "L1_ffn_w1",
        "b1": "L1_ffn_b1", "w2": "L1_ffn_w2", "b2": "L1_ffn_b2",
    }
    consts, bits = shape_constants()
    arrays, drams = {}, {}
    for name in INPUTS:
        a = {"consts_d": consts, "bits_d": bits}.get(name)
        if a is None:
            a = np.ascontiguousarray(inputs[names.get(name, name)])
            a = a.reshape(1) if a.ndim == 0 else a
        arrays["in_" + name] = a
        drams[name] = nc.dram_tensor("in_" + name, a.shape, mybir.dt.from_np(a.dtype), kind="ExternalInput").ap()
    drams["out"] = nc.dram_tensor("out_rows", (N, D), F32, kind="ExternalOutput").ap()
    gnn_ffn_kernel(nc, **drams)
    got = run_bass_kernel_spmd(nc, [arrays], core_ids=[0])
    return got.results[0]["out_rows"]
```

```python
from contextlib import ExitStack

import numpy as np

import concourse.bass as bass
from concourse import mybir

F32 = mybir.dt.float32
F32R = mybir.dt.float32r
F16 = mybir.dt.float16
BF16 = mybir.dt.bfloat16
I32 = mybir.dt.int32
ACT = mybir.ActivationFunctionType
ALU = mybir.AluOpType
X = mybir.AxisListType.X

N = 1250
D = 512
TR = 125
NT = N // TR
KD = D // 128
EDGES = 20000
EB = 125
NB = EDGES // EB
EQ = NB // 2
WIN = 32
NW = -(-N // WIN)
NC = NT * 128
ND = NW * WIN
SLOTS = 6
KEY = 2048
HID0 = 1024
KH0 = HID0 // 128
NE = 8
TOP = N // NE
PLACES = 160
NP = NE * PLACES
CH = PLACES // 2
NG = NP // 128
FAR = 3000
HID1 = 2048
EPS = 1e-5
FLOOR = 1e-10
SINKHORN = 8
BLOCKS = [(0, 418), (418, 834), (834, 1250)]
BW = 418
SHIFTS = [26, 22, 18, 14, 10, 6, 2, 0]

C_ID, C_ONE, C_BLK, C_SEL, C_LSEL, C_LONE, C_ROW = 0, 128, 256, 384, 512, 536, 539
C_I32, C_W2K, C_BLKNO, C_PLACE, C_FAR, C_I10 = 540, 572, 612, 772, 773, 774
C_END = C_I10 + NC


def shape_constants():
    c = np.zeros((128, C_END), np.float32)
    p = np.arange(128)
    c[:, C_ID:C_ID + 128] = np.eye(128)
    c[:, C_ONE:C_ONE + 128] = 1
    c[:, C_BLK:C_BLK + 128] = p[:, None] // 16 == p[None] // 16
    c[0:NE, C_SEL:C_SEL + 128] = p[0:NE, None] == p[None] // 16
    for depth in range(3):
        for e in range(NE):
            node, bit = 2**depth - 1 + (e >> (3 - depth)), (e >> (2 - depth)) & 1
            c[node, C_LSEL + 8 * depth + e] = 1 if bit else -1
            c[e, C_LONE + depth] = 0 if bit else 1
    c[:, C_ROW] = p
    c[:, C_I32:C_I32 + WIN] = np.arange(WIN)
    c[:, C_W2K:C_W2K + NW] = KEY * np.arange(NW)
    c[:, C_BLKNO:C_BLKNO + NB] = (2 * np.arange(EQ)[None] + np.arange(2)[:, None]).reshape(-1)
    c[:, C_PLACE] = p // 16 * PLACES
    c[:, C_FAR] = FAR + p
    i10 = np.full((NT, 128), -1.0)
    i10[:, :TR] = np.arange(N).reshape(NT, TR)
    c[:, C_I10:] = i10.reshape(-1)
    bits = np.zeros((128, len(SHIFTS)), np.int32)
    for r, s in enumerate(SHIFTS):
        limit = 4 if r == len(SHIFTS) - 1 else 16
        bits[:, r] = np.where(p % 16 < limit, (p % 16) << s, 0x40000000)
    return c, bits




X_AT = 10240
REG = X_AT + NT * D * 4
A1_END = REG + NT * ND * 4
ROWS = NT * D * 4
COLS = KD * N * 4


class Record:
    pass


class Room:

    def __init__(self, nc, start):
        self.nc, self.next = nc, start

    def __call__(self, name, shape, dtype):
        width = {F32: 4, F32R: 4, I32: 4, F16: 2, BF16: 2}[dtype]
        start = -(-self.nc.sbuf_base // 32) * 32
        buffer = self.nc.alloc_sbuf_tensor_at(name, shape, dtype, offset=start + self.next)
        self.next += -(-int(np.prod(shape[1:])) * width // 32) * 32
        return buffer


class Steps:

    def __init__(self, engine, semaphore):
        self.engine, self.semaphore, self.n = engine, semaphore, 0

    def mark(self, ins):
        ins.then_inc(self.semaphore, 1)
        self.n += 1

    def wait(self):
        self.engine.wait_ge(self.semaphore, self.n)

    def then(self, ins):
        self.mark(ins)
        self.wait()


def pieces(lo, hi):
    return [(t, max(lo, t * TR) - t * TR, min(hi, (t + 1) * TR) - t * TR)
            for t in range(NT) if t * TR < hi and (t + 1) * TR > lo]


def halves(ap):
    return ap.rearrange("p (q h) -> p q h", h=2)


def phase_edges(nc, sem, g):
    room = Room(nc, g.scratch_at)
    raw_i = room("edge_ints", [EQ, 2, 2 * EB], I32)
    wraw = room("edge_w", [EQ, 2 * EB], F32)
    win_i = room("edge_win", [EQ, 2 * EB], I32)
    rem_i = room("edge_rem", [EQ, 2 * EB], I32)
    keyrem = room("edge_keyrem", [EQ, 2, 2 * EB], F32)
    extent = room("edge_extent", [EQ, 4], F32)
    spread = room("edge_spread", [EQ, 4, NW], F32)
    rem = room("rem", [EB, NB], F32)
    wcol = room("wcol", [EB, NB], F32)
    wres = room("wres", [EB, NB], F32)
    wres2 = room("wres2", [EB, NB], F32)
    parts = room("parts", [EB, NB, 3], BF16)
    meets1 = room("meets1", [NW, NB], F32)
    meets = room("meets", [NW, NB], F32)
    pick = room("pick", [NW, 2, NB], F32)
    ends = room("ends", [NW, 2], F32)
    lohi = room("lohi", [NW, 2], F32)
    i10f = room("i10f", [128, NC], F32)

    loaded = sem("e_loaded")
    own = sem("e_own")
    keyed = sem("e_keyed")
    spread_out = sem("e_spread")
    bounded = sem("e_bounded")
    turned = sem("e_turned")

    loads = [
        (g.small[:, :], g.consts_d[:, 0:C_I10]), (raw_i[:, 0, :], g.src.rearrange("(q e) -> q e", q=EQ)),
        (raw_i[:, 1, :], g.dst.rearrange("(q e) -> q e", q=EQ)),
        (wraw[:, :], g.edge_weight.rearrange("(q e) -> q e", q=EQ)), (i10f[:, :], g.consts_d[:, C_I10:C_END]),
        (g.kshift[:, :], g.bits_d), (g.eps0[:, :], g.gnn0_eps.partition_broadcast(128)),
        (g.vecrows[0:8, :], g.gnn0_b1.rearrange("(t p) -> t p", p=128)),
        (g.vecrows[8:16, :], g.gnn0_g1.rearrange("(t p) -> t p", p=128)),
        (g.vecrows[16:24, :], g.gnn0_be1.rearrange("(t p) -> t p", p=128)),
        (g.vecrows[24:28, :], g.gnn0_b2.rearrange("(t p) -> t p", p=128)),
        (g.vecrows[28:32, :], g.gnn0_g2.rearrange("(t p) -> t p", p=128)),
        (g.vecrows[32:36, :], g.gnn0_be2.rearrange("(t p) -> t p", p=128)),
        (g.vecrows[36:68, :], g.b2.rearrange("e (t p) -> (e t) p", p=128)),
        (g.vecrows[68:96, :], g.rw.rearrange("n (t p) -> (n t) p", p=128)),
        (g.b1rows[:, :], g.b1.rearrange("e (t p) -> (e t) p", p=128)),
        (g.gate[:, :, :], g.gate_w[0].rearrange("(k p) e -> p k e", p=128)),
        (g.rb_col[0:7, :], g.rb.rearrange("(n a) -> n a", a=1)),
    ]

    with nc.Block() as block:
        @block.sync
        def _(sp):
            for to, of in loads:
                sp.dma_start(to, of).then_inc(loaded, 16)
            sp.dma_start(g.x_rows[:, :, :], g.x.rearrange("(t p) d -> p t d", p=TR)).then_inc(g.x_loaded, 16)

        @block.vector
        def _(v):
            s = Steps(v, own)
            v.wait_ge(loaded, 16 * len(loads))
            s.mark(v.tensor_copy(g.i10[:, :], i10f[0:EB, :]))
            s.mark(v.memset(g.zeros[:, :], 0.0))
            s.mark(v.memset(g.key[:, :], -1.0))
            s.mark(v.memset(g.D_all[:, NB:NB + SLOTS, :, :], 0.0))
            s.mark(v.tensor_single_scalar(win_i[:, :], raw_i[:, 1, :], 5, ALU.logical_shift_right))
            s.then(v.tensor_single_scalar(rem_i[:, :], raw_i[:, 1, :], WIN - 1, ALU.bitwise_and))
            v.scalar_tensor_tensor(out=keyrem[:, 0, :], in0=win_i[:, :], scalar=float(KEY), in1=raw_i[:, 0, :],
                                   op0=ALU.mult, op1=ALU.add).then_inc(keyed, 1)
            v.tensor_copy(keyrem[:, 1, :], rem_i[:, :]).then_inc(keyed, 1)
            by_block = win_i[:, :].rearrange("q (h e) -> q h e", h=2)
            s.mark(v.tensor_reduce(extent[:, 0:2], by_block, X, ALU.min))
            s.then(v.tensor_reduce(extent[:, 2:4], by_block, X, ALU.max))
            for a in range(4):
                v.tensor_scalar(spread[:, a, :], g.ones[0:EQ, 0:NW], extent[:, a:a + 1], None,
                                ALU.mult).then_inc(spread_out, 1)
            v.wait_ge(turned, 1)
            table = g.psum[0:EB, 0, 0:6 * EQ].rearrange("p (a h q) -> p a q h", a=3, h=2)
            s.mark(v.tensor_copy(halves(g.key[:, 0:NB]), table[:, 0]))
            s.mark(v.tensor_copy(halves(rem[:, :]), table[:, 1]))
            s.then(v.tensor_copy(halves(wcol[:, :]), table[:, 2]))
            s.then(v.tensor_copy(parts[:, :, 0], wcol[:, :]))
            s.then(v.tensor_tensor(wres[:, :], wcol[:, :], parts[:, :, 0], ALU.subtract))
            s.then(v.tensor_copy(parts[:, :, 1], wres[:, :]))
            s.then(v.tensor_tensor(wres2[:, :], wres[:, :], parts[:, :, 1], ALU.subtract))
            s.then(v.tensor_copy(parts[:, :, 2], wres2[:, :]))
            v.wait_ge(turned, 2)
            ext = g.psum[0:NW, 1, 0:2 * NB].rearrange("w (a b) -> w a b", a=2)
            s.then(v.tensor_scalar(meets1[:, :], ext[:, 0], g.rowno[0:NW, :], None, ALU.is_le))
            s.then(v.scalar_tensor_tensor(out=meets[:, :], in0=ext[:, 1], scalar=g.rowno[0:NW, :],
                                          in1=meets1[:, :], op0=ALU.is_ge, op1=ALU.mult))
            s.mark(v.scalar_tensor_tensor(out=pick[:, 0, :], in0=meets[:, :], scalar=-256.0,
                                          in1=g.blkno[0:NW, :], op0=ALU.mult, op1=ALU.add))
            s.then(v.tensor_tensor(pick[:, 1, :], meets[:, :], g.blkno[0:NW, :], ALU.mult))
            s.mark(v.tensor_reduce(ends[:, 0:1], pick[:, 0, :], X, ALU.min))
            s.then(v.tensor_reduce(ends[:, 1:2], pick[:, 1, :], X, ALU.max))
            v.tensor_scalar(lohi[:, 0:1], ends[:, 0:1], 256.0, float(NB - 1), ALU.add,
                            ALU.min).then_inc(bounded, 1)
            v.tensor_scalar(lohi[:, 1:2], ends[:, 1:2], 1.0, None, ALU.add).then_inc(bounded, 1)
            d = g.D_all[:, 0:NB, :, :]
            s.then(v.tensor_tensor(d[:, :, 0, :], rem[:, :].unsqueeze(2).to_broadcast([EB, NB, WIN]),
                                   g.iota32[0:EB, :].unsqueeze(1).to_broadcast([EB, NB, WIN]), ALU.is_equal))
            for c in range(3):
                s.mark(v.tensor_tensor(d[:, :, 1 + c, :], d[:, :, 0, :],
                                       parts[:, :, c:c + 1].to_broadcast([EB, NB, WIN]), ALU.mult))
            v.wait_ge(turned, 3)
            s.mark(v.tensor_copy(g.bounds[:, :].rearrange("o (w a) -> o a w", a=2),
                                 g.psum[0:1, 2, 0:2 * NW].rearrange("o (a w) -> o a w", a=2)))
            v.wait_ge(turned, 4)
            s.mark(v.tensor_copy(g.vecs[:, :], g.psum[:, 3, 0:96]))
            s.mark(v.tensor_copy(g.b1cols[:, :], g.psum[:, 3, 128:256]))

        @block.tensor
        def _(t):
            t.wait_ge(loaded, 16 * len(loads))
            t.wait_ge(keyed, 2)
            for a, of in enumerate([keyrem[:, 0, :], keyrem[:, 1, :], wraw[:, :]]):
                for h in range(2):
                    o = (2 * a + h) * EQ
                    ins = t.transpose(g.psum[0:EB, 0, o:o + EQ], of[:, h * EB:(h + 1) * EB],
                                      g.ident[0:EQ, 0:EQ])
            ins.then_inc(turned, 1)
            t.wait_ge(spread_out, 4)
            for a in range(4):
                ins = t.matmul(g.psum[0:NW, 1, a * EQ:(a + 1) * EQ], spread[:, a, :], g.ident[0:EQ, 0:EQ],
                               start=True, stop=True)
            ins.then_inc(turned, 1)
            t.wait_ge(bounded, 2)
            for a in range(2):
                ins = t.transpose(g.psum[0:1, 2, a * NW:(a + 1) * NW], lohi[:, a:a + 1],
                                  g.ident[0:NW, 0:NW])
            ins.then_inc(turned, 1)
            t.transpose(g.psum[:, 3, 0:96], g.vecrows[0:96, :], g.ident[0:96, 0:96])
            t.transpose(g.psum[:, 3, 128:256], g.b1rows[:, :], g.ident[:, :]).then_inc(turned, 1)


def phase_adjacency(nc, sem, g):
    room = Room(nc, g.scratch_at)
    S = room("src_onehot", [EB, SLOTS, NC], BF16)
    rkey = room("rkey", [EB, 2, SLOTS], F32)
    S_more = room("src_onehot_more", [EB, NC], BF16)
    rkey_more = room("rkey_more", [EB, 1], F32)
    WP = room("weight_parts", [128, 2, NT, 3, WIN], F32)
    T = room("weight_sum", [128, NT, WIN], F32)
    PAIRS = SLOTS // 2

    keyed = sem("a_keyed")
    made = sem("a_made")
    used = sem("a_used")
    more_keyed = sem("a_more_keyed")
    more_made = sem("a_more_made")
    more_used = sem("a_more_used")
    summed = sem("a_summed")
    drained = sem("a_drained")
    copied = sem("a_copied")
    parts_free = sem("a_parts_free")
    added = sem("a_added")

    def banks(par):
        return g.psum[:, 3 * par:3 * par + 3, :].rearrange("p a b -> p (a b)")[:, 0:NC]

    def two_windows(eng, regs, w2):
        eng.load(regs, g.bounds[0:1, bass.ds(w2 * 4, 4)])
        return [(eng.snap(regs[2 * i], min_val=0, max_val=NB - 1), eng.snap(regs[2 * i + 1], min_val=1, max_val=NB))
                for i in range(2)]

    with nc.Block() as block:
        @block.vector
        def _(v):
            regs = [v.alloc_register(f"v_bound{i}") for i in range(4)]
            n = v.alloc_register("more_made_blocks")
            v.reg_mov(n, 1)
            with v.Fori(0, NW // 2) as w2:
                bounds = two_windows(v, regs, w2)
                v.wait_ge(made, w2 * (2 * PAIRS))
                for par, (lo, hi) in enumerate(bounds):
                    v.tensor_scalar(rkey[:, par, :], g.key[:, bass.ds(lo, SLOTS)],
                                    g.w2k[0:EB, bass.ds(w2 * 2 + par, 1)], None, ALU.subtract).then_inc(keyed, 1)
                for par, (lo, hi) in enumerate(bounds):
                    v.wait_ge(keyed, w2 * 2 + par + 1)
                    for p in range(PAIRS):
                        v.wait_ge(used, w2 * (2 * PAIRS) + par * PAIRS + p + 1)
                        for u in (2 * p, 2 * p + 1):
                            ins = v.tensor_scalar(S[:, u, :], g.i10[:, :], rkey[:, par, u:u + 1], None, ALU.is_equal)
                        ins.then_inc(made, 1)
                    with v.Fori(lo + SLOTS, hi) as b:
                        v.wait_ge(more_used, v.snap(n))
                        v.tensor_scalar(rkey_more[:, :], g.key[:, bass.ds(b, 1)],
                                        g.w2k[0:EB, bass.ds(w2 * 2 + par, 1)], None,
                                        ALU.subtract).then_inc(more_keyed, 1)
                        v.wait_ge(more_keyed, v.snap(n))
                        v.tensor_scalar(S_more[:, :], g.i10[:, :], rkey_more[:, :], None,
                                        ALU.is_equal).then_inc(more_made, 1)
                        v.reg_add(n, n, 1)

        @block.tensor
        def _(t):
            t.sem_inc(used, PAIRS)
            t.sem_inc(more_used, 1)
            t.sem_inc(drained, 2)
            regs = [t.alloc_register(f"t_bound{i}") for i in range(4)]
            n = t.alloc_register("more_used_blocks")
            t.reg_mov(n, 1)
            with t.Fori(0, NW // 2) as w2:
                bounds = two_windows(t, regs, w2)
                for par, (lo, hi) in enumerate(bounds):
                    ps = banks(par)
                    t.wait_ge(drained, w2 * 2 + par + 1)
                    for p in range(PAIRS):
                        t.wait_ge(made, w2 * (2 * PAIRS) + par * PAIRS + p + 1)
                        for u in (2 * p, 2 * p + 1):
                            for c in range(NT):
                                ins = t.matmul(ps[:, c * 128:(c + 1) * 128], S[:, u, c * 128:(c + 1) * 128],
                                               g.D_flat[:, bass.ds((lo + u) * 128, 128)],
                                               start=u == 0 and c % 4 == 0, stop=False, skip_group_check=True)
                        ins.then_inc(used, 1)
                    with t.Fori(lo + SLOTS, hi) as b:
                        t.wait_ge(more_made, t.snap(n))
                        for c in range(NT):
                            ins = t.matmul(ps[:, c * 128:(c + 1) * 128], S_more[:, c * 128:(c + 1) * 128],
                                           g.D_flat[:, bass.ds(b * 128, 128)],
                                           start=False, stop=False, skip_group_check=True)
                        ins.then_inc(more_used, 1)
                        t.reg_add(n, n, 1)
                    t.matmul(ps[:, 0:128], g.zeros[0:EB, :], g.zeros[0:EB, :], start=False, stop=True,
                             skip_group_check=True).then_inc(summed, 1)

        @block.scalar
        def _(a):
            with a.Fori(0, NW // 2) as w2:
                for par in range(2):
                    w = w2 * 2 + par
                    ps = banks(par).rearrange("p (c a w) -> p c a w", c=NT, a=4)
                    a.wait_ge(summed, w + 1)
                    a.wait_ge(parts_free, w + 1)
                    a.activation(WP[:, par], ps[:, :, 1:4, :], ACT.Copy).then_inc(copied, 1)
                    a.activation(g.A0T[:, :, bass.ds(w * WIN, WIN)], ps[:, :, 0, :],
                                 ACT.Copy).then_inc(drained, 1)

        @block.gpsimd
        def _(q):
            q.sem_inc(parts_free, 2)
            with q.Fori(0, NW // 2) as w2:
                for par in range(2):
                    w = w2 * 2 + par
                    q.wait_ge(copied, w + 1)
                    q.wait_ge(parts_free, w + 2)
                    q.tensor_tensor(T[:, :, :], WP[:, par, :, 0, :], WP[:, par, :, 1, :],
                                    ALU.add).then_inc(added, 1)
                    q.wait_ge(added, w + 1)
                    q.tensor_tensor(g.A1T[:, :, bass.ds(w * WIN, WIN)], T[:, :, :], WP[:, par, :, 2, :],
                                    ALU.add).then_inc(parts_free, 1)


def norm_sems(sem, name):
    n = Record()
    n.own = sem(name + "_own")
    n.var = sem(name + "_var")
    n.dev = sem(name + "_dev")
    n.normed = sem(name + "_normed")
    return n


def norm_vector(v, g, to, n):
    s = Steps(v, n.own)
    for t in range(NT):
        s.mark(v.bn_stats(g.stats[:, t, :], g.x_rows[:, t, :]))
    s.wait()
    for t in range(NT):
        s.mark(v.bn_aggr(g.meanvar[:, t, :], g.stats[:, t, :]))
    s.wait()
    v.tensor_scalar(g.dev[:, :], g.meanvar[:, :, 1], EPS, None, ALU.add).then_inc(n.var, 1)
    v.wait_ge(n.dev, 1)
    s.then(v.reciprocal(g.rstd[:, :], g.dev2[:, :]))
    for t in range(NT):
        v.tensor_scalar(to[:, t, :], g.x_rows[:, t, :], g.meanvar[:, t, 0:1], g.rstd[:, t:t + 1],
                        ALU.subtract, ALU.mult).then_inc(n.normed, 1)
    return s


def norm_scalar(a, g, n):
    a.wait_ge(n.var, 1)
    a.activation(g.dev2[:, :], g.dev[:, :], ACT.Sqrt).then_inc(n.dev, 1)


def phase_norm0(nc, sem, g):
    n = norm_sems(sem, "n0")
    hi_cut = sem("n0_hi")
    lo_cut = sem("n0_lo")
    xed = sem("n0_x")

    with nc.Block() as block:
        @block.vector
        def _(v):
            v.wait_ge(g.x_loaded, 16)
            s = norm_vector(v, g, g.xn, n)
            s.then(v.tensor_scalar(g.eps0[:, :], g.eps0[:, :], 1.0, None, ALU.add))
            for t in range(NT):
                v.wait_ge(hi_cut, t + 1)
                v.tensor_tensor(g.rlo[:, t, :], g.xn[:, t, :], g.rhi[:, t, :].bitcast(F32),
                                ALU.subtract).then_inc(lo_cut, 1)
            for t in range(NT):
                v.wait_ge(lo_cut, t + 1)
                v.wait_ge(xed, t + 1)
                s.mark(v.tensor_scalar(g.xn[:, t, :], g.xn[:, t, :], g.eps0[0:TR, :], None, ALU.mult))

        @block.scalar
        def _(a):
            norm_scalar(a, g, n)
            for t in range(NT):
                a.wait_ge(n.normed, t + 1)
                a.activation(g.rhi[:, t, :], g.xn[:, t, :], ACT.Copy).then_inc(hi_cut, 1)

        @block.gpsimd
        def _(q):
            for t in range(NT):
                q.wait_ge(n.normed, t + 1)
                q.tensor_tensor(g.x_rows[:, t, :], g.x_rows[:, t, :], g.xn[:, t, :],
                                ALU.add).then_inc(xed, 1)


def cut_products(t, out, stat, mov, start, stop):
    t.matmul(out, stat[0], mov[0], start=start, stop=False)
    t.matmul(out, stat[0], mov[1], start=False, stop=False)
    return t.matmul(out, stat[1], mov[0], start=False, stop=stop)


def phase_gather0(nc, sem, g):
    RING = 2
    chunk = g.a0chunk
    cut = sem("g0_cut")
    used = sem("g0_used")
    summed = sem("g0_summed")
    hi_cut = sem("g0_hi")
    lo_cut = sem("g0_lo")
    order = [(b, k) for b in range(3) for k in range(NT)]

    with nc.Block() as block:
        @block.scalar
        def _(a):
            def drain(b):
                lo, hi = BLOCKS[b]
                a.wait_ge(summed, b + 1)
                for d in range(KD):
                    a.activation(g.thi[:, d, lo:hi], g.psum[:, b % 2 * 4 + d, 0:hi - lo],
                                 ACT.Copy).then_inc(hi_cut, 1)

            for i, (b, k) in enumerate(order):
                if k == 2 and b:
                    drain(b - 1)
                lo, hi = BLOCKS[b]
                if i >= RING:
                    a.wait_ge(used, i - RING + 1)
                a.activation(chunk[:, i % RING, 0:hi - lo], g.A0T[0:TR, k, lo:hi], ACT.Copy).then_inc(cut, 1)
            drain(2)

        @block.tensor
        def _(t):
            for i, (b, k) in enumerate(order):
                lo, hi = BLOCKS[b]
                if k == 0 and b == 2:
                    t.wait_ge(lo_cut, KD)
                t.wait_ge(cut, i + 1)
                for d in range(KD):
                    ps = g.psum[:, b % 2 * 4 + d, 0:hi - lo]
                    t.matmul(ps, g.rhi[:, k, d * 128:(d + 1) * 128], chunk[:, i % RING, 0:hi - lo],
                             start=k == 0, stop=False)
                    ins = t.matmul(ps, g.rlo[:, k, d * 128:(d + 1) * 128], chunk[:, i % RING, 0:hi - lo],
                                   start=False, stop=False)
                ins.then_inc(used, 1)
                if k == NT - 1:
                    for tile, p0, p1 in pieces(lo, hi):
                        o = tile * TR + p0 - lo
                        for d in range(KD):
                            ins = t.matmul(g.psum[:, b % 2 * 4 + d, o:o + p1 - p0],
                                           g.xn[:, tile, d * 128:(d + 1) * 128], g.ident[0:TR, p0:p1],
                                           start=False, stop=tile * TR + p1 >= hi)
                    ins.then_inc(summed, 1)

        @block.vector
        def _(v):
            for b, (lo, hi) in enumerate(BLOCKS):
                for d in range(KD):
                    v.wait_ge(hi_cut, b * KD + d + 1)
                    v.tensor_tensor(g.tlo[:, d, lo:hi], g.psum[:, b % 2 * 4 + d, 0:hi - lo],
                                    g.thi[:, d, lo:hi].bitcast(F32), ALU.subtract).then_inc(lo_cut, 1)


def bn_scale_shift(v, s, g, var, dev, n, mean, var_ap, bias, gamma, beta, scale, shift, scratch):
    v.tensor_scalar(scratch[0], var_ap, EPS, None, ALU.add).then_inc(var, 1)
    s.then(v.tensor_tensor(scratch[1], mean, bias, ALU.add))
    s.then(v.tensor_tensor(scratch[1], bias, scratch[1], ALU.subtract))
    v.wait_ge(dev, n)
    s.then(v.reciprocal(scratch[3], scratch[2]))
    s.then(v.tensor_tensor(scale, scratch[3], gamma, ALU.mult))
    s.then(v.tensor_tensor(scratch[1], scratch[1], scale, ALU.mult))


def phase_mlp1(nc, sem, g):
    room = Room(nc, g.w1_at)
    raw = room("W1_raw", [128, 2, KD, 256], F32)
    whi = room("W1_hi", [128, 2, KD, 128], F32R)
    wlo = room("W1_lo", [128, 2, KD, 128], F32R)

    loaded = [sem("m1_loaded0"), sem("m1_loaded1")]
    hi_cut = sem("m1_hi")
    lo_cut = sem("m1_lo")
    summed = sem("m1_summed")
    own = sem("m1_own")
    var = sem("m1_var")
    dev = sem("m1_dev")
    scaled = sem("m1_scaled")
    drained = sem("m1_drained")
    bn = g.bn

    with nc.Block() as block:
        @block.sync
        def _(sp):
            for p in range(KH0 // 2):
                if p >= 2:
                    sp.wait_ge(lo_cut, 2 * (p - 1))
                sp.dma_start(raw[:, p % 2], g.gnn0_W1.rearrange("(k p) h -> p k h", p=128)[
                    :, :, p * 256:(p + 1) * 256]).then_inc(loaded[p % 2], 16)
            sp.dma_start(g.W2_raw[:, :, :], g.gnn0_W2.rearrange("(k p) d -> p k d", p=128)).then_inc(
                g.W2_loaded, 16)

        @block.vector
        def _(v):
            s = Steps(v, own)

            def cut(m):
                p = m // 2
                v.wait_ge(loaded[p % 2], 16 * (p // 2 + 1))
                if m >= 2:
                    v.wait_ge(summed, m - 1)
                of = raw[:, p % 2, :, m % 2 * 128:(m % 2 + 1) * 128]
                v.tensor_copy(whi[:, m % 2], of).then_inc(hi_cut, 1)
                v.wait_ge(hi_cut, m + 1)
                v.tensor_tensor(wlo[:, m % 2], of, whi[:, m % 2].bitcast(F32), ALU.subtract).then_inc(lo_cut, 1)

            cut(0)
            cut(1)
            for m in range(KH0):
                v.wait_ge(summed, m + 1)
                for b, (lo, hi) in enumerate(BLOCKS):
                    s.mark(v.bn_stats(bn.stats[:, b, :], g.psum[:, m % 2 * 3 + b, 0:hi - lo]))
                s.wait()
                s.then(v.bn_aggr(bn.mv[:, :], bn.stats[:, 0:3, :]))
                c = slice(m, m + 1)
                bn_scale_shift(v, s, g, var, dev, m + 1, bn.mv[:, 0:1], bn.mv[:, 1:2], g.b1v[:, c], g.g1v[:, c],
                               g.be1v[:, c], bn.scale[:, c], None,
                               [bn.a[:, c], bn.b[:, c], bn.c[:, c], bn.d[:, c]])
                v.tensor_tensor(bn.shift[:, c], bn.b[:, c], g.be1v[:, c], ALU.add).then_inc(scaled, 1)
                if m + 2 < KH0:
                    cut(m + 2)

        @block.scalar
        def _(a):
            for m in range(KH0):
                a.wait_ge(var, m + 1)
                a.activation(bn.c[:, m:m + 1], bn.a[:, m:m + 1], ACT.Sqrt).then_inc(dev, 1)
                a.wait_ge(scaled, m + 1)
                for b, (lo, hi) in enumerate(BLOCKS):
                    a.activation(g.h1[:, m, lo:hi], g.psum[:, m % 2 * 3 + b, 0:hi - lo], ACT.Relu,
                                 bias=bn.shift[:, m:m + 1], scale=bn.scale[:, m:m + 1]).then_inc(drained, 1)

        @block.tensor
        def _(t):
            for m in range(KH0):
                t.wait_ge(lo_cut, m + 1)
                if m >= 2:
                    t.wait_ge(drained, 3 * (m - 1))
                for b, (lo, hi) in enumerate(BLOCKS):
                    for k in range(KD):
                        ins = cut_products(t, g.psum[:, m % 2 * 3 + b, 0:hi - lo],
                                           (whi[:, m % 2, k, :], wlo[:, m % 2, k, :]),
                                           (g.thi[:, k, lo:hi], g.tlo[:, k, lo:hi]), k == 0, k == KD - 1)
                ins.then_inc(summed, 1)


def phase_mlp2(nc, sem, g):
    RING = 3
    room = Room(nc, g.w2_cut_at)
    whi = room("W2_hi", [128, KH0, D], F32R)
    wlo = room("W2_lo", [128, KH0, D], F32R)
    hhi = room("h1_hi", [128, RING, BW], F32R)
    hlo = room("h1_lo", [128, RING, BW], F32R)

    w_hi = sem("m2_whi")
    w_lo = sem("m2_wlo")
    hi_cut = sem("m2_hi")
    lo_cut = sem("m2_lo")
    used = sem("m2_used")
    summed = sem("m2_summed")
    drained = sem("m2_drained")
    own = sem("m2_own")
    var = sem("m2_var")
    dev = sem("m2_dev")
    scaled = sem("m2_scaled")
    done = sem("m2_done")
    order = [(b, k) for b in range(3) for k in range(KH0)]
    bn = g.bn

    with nc.Block() as block:
        @block.scalar
        def _(a):
            def drain(b):
                lo, hi = BLOCKS[b]
                a.wait_ge(summed, b + 1)
                for d in range(KD):
                    a.activation(g.yT[:, d, lo:hi], g.psum[:, b % 2 * 4 + d, 0:hi - lo],
                                 ACT.Copy).then_inc(drained, 1)

            for i, (b, k) in enumerate(order):
                if k == 2 and b:
                    drain(b - 1)
                lo, hi = BLOCKS[b]
                if i >= RING:
                    a.wait_ge(used, i - RING + 1)
                a.activation(hhi[:, i % RING, 0:hi - lo], g.h1[:, k, lo:hi], ACT.Copy).then_inc(hi_cut, 1)
            drain(2)
            a.wait_ge(var, 1)
            a.activation(bn.c[:, 0:KD], bn.a[:, 0:KD], ACT.Sqrt).then_inc(dev, 1)
            a.wait_ge(scaled, 1)
            for d in range(KD):
                a.activation(g.yT[:, d, :], g.yT[:, d, :], ACT.Relu, bias=bn.shift[:, d:d + 1],
                             scale=bn.scale[:, d:d + 1]).then_inc(done, 1)

        @block.vector
        def _(v):
            s = Steps(v, own)
            v.wait_ge(g.W2_loaded, 16)
            for i, (b, k) in enumerate(order):
                lo, hi = BLOCKS[b]
                if b == 0:
                    v.tensor_copy(whi[:, k, :], g.W2_raw[:, k, :]).then_inc(w_hi, 1)
                    v.wait_ge(w_hi, k + 1)
                    v.tensor_tensor(wlo[:, k, :], g.W2_raw[:, k, :], whi[:, k, :].bitcast(F32),
                                    ALU.subtract).then_inc(w_lo, 1)
                v.wait_ge(hi_cut, i + 1)
                if i >= RING:
                    v.wait_ge(used, i - RING + 1)
                v.tensor_tensor(hlo[:, i % RING, 0:hi - lo], g.h1[:, k, lo:hi],
                                hhi[:, i % RING, 0:hi - lo].bitcast(F32), ALU.subtract).then_inc(lo_cut, 1)
            for b, (lo, hi) in enumerate(BLOCKS):
                v.wait_ge(drained, KD * (b + 1))
                for d in range(KD):
                    s.mark(v.bn_stats(bn.stats[:, d * 3 + b, :], g.yT[:, d, lo:hi]))
            s.wait()
            for d in range(KD):
                s.mark(v.bn_aggr(bn.mv4[:, d, :], bn.stats[:, 3 * d:3 * d + 3, :]))
            s.wait()
            bn_scale_shift(v, s, g, var, dev, 1, bn.mv4[:, :, 0], bn.mv4[:, :, 1], g.b2v[:, :], g.g2v[:, :],
                           g.be2v[:, :], bn.scale[:, 0:KD], None,
                           [bn.a[:, 0:KD], bn.b[:, 0:KD], bn.c[:, 0:KD], bn.d[:, 0:KD]])
            v.tensor_tensor(bn.shift[:, 0:KD], bn.b[:, 0:KD], g.be2v[:, :], ALU.add).then_inc(scaled, 1)

        @block.tensor
        def _(t):
            for i, (b, k) in enumerate(order):
                lo, hi = BLOCKS[b]
                if b == 0:
                    t.wait_ge(w_lo, k + 1)
                if b == 2 and k == 0:
                    t.wait_ge(drained, KD)
                t.wait_ge(lo_cut, i + 1)
                for d in range(KD):
                    f = slice(d * 128, (d + 1) * 128)
                    ins = cut_products(t, g.psum[:, b % 2 * 4 + d, 0:hi - lo], (whi[:, k, f], wlo[:, k, f]),
                                       (hhi[:, i % RING, 0:hi - lo], hlo[:, i % RING, 0:hi - lo]),
                                       k == 0, k == KH0 - 1)
                ins.then_inc(used, 1)
                if k == KH0 - 1:
                    t.matmul(g.psum[:, b % 2 * 4 + 3, 0:2], g.zeros[:, :], g.zeros[:, 0:2], start=False,
                             stop=True, skip_group_check=True).then_inc(summed, 1)


def add_turned(nc, sem, g, name, cols):
    turned = sem(name + "_turned")
    added = sem(name + "_added")
    with nc.Block() as block:
        @block.tensor
        def _(t):
            for i in range(NT):
                if i >= 8:
                    t.wait_ge(added, i - 7)
                for d in range(KD):
                    ins = t.transpose(g.psum[0:TR, i % 8, d * 128:(d + 1) * 128],
                                      cols[:, d, i * TR:(i + 1) * TR], g.ident[:, :])
                ins.then_inc(turned, 1)

        @block.vector
        def _(v):
            for i in range(NT):
                v.wait_ge(turned, i + 1)
                v.tensor_tensor(g.x_rows[:, i, :], g.x_rows[:, i, :], g.psum[0:TR, i % 8, :],
                                ALU.add).then_inc(added, 1)


def norm_and_turn(nc, sem, g, name, rows, thi, tlo):
    n = norm_sems(sem, name)
    turned = sem(name + "_turned")
    hi_cut = sem(name + "_hi")
    lo_cut = sem(name + "_lo")

    def cols(i):
        return g.psum[:, i % 8, 0:KD * TR].rearrange("p (k c) -> p k c", k=KD)

    with nc.Block() as block:
        @block.vector
        def _(v):
            norm_vector(v, g, rows, n)
            for i in range(NT):
                v.wait_ge(hi_cut, i + 1)
                v.tensor_tensor(tlo[:, :, i * TR:(i + 1) * TR], cols(i),
                                thi[:, :, i * TR:(i + 1) * TR].bitcast(F32), ALU.subtract).then_inc(lo_cut, 1)

        @block.scalar
        def _(a):
            norm_scalar(a, g, n)
            for i in range(NT):
                a.wait_ge(turned, i + 1)
                a.activation(thi[:, :, i * TR:(i + 1) * TR], cols(i), ACT.Copy).then_inc(hi_cut, 1)

        @block.tensor
        def _(t):
            for i in range(NT):
                t.wait_ge(n.normed, i + 1)
                if i >= 8:
                    t.wait_ge(lo_cut, i - 7)
                for k in range(KD):
                    ins = t.transpose(g.psum[:, i % 8, k * TR:(k + 1) * TR], rows[:, i, k * 128:(k + 1) * 128],
                                      g.ident[0:TR, 0:TR])
                ins.then_inc(turned, 1)


def phase_route(nc, sem, g):
    room = Room(nc, g.route_at)
    ghi = room("gate_hi", [128, KD, 128], F32R)
    glo = room("gate_lo", [128, KD, 128], F32R)
    gT = room("gates_T", [NE, N], F32)
    P = room("plan", [TR, NT, 128], F32)
    V = room("plan_T", [128, N], F32)
    above = room("above", [128, N], F32)
    equal = room("equal", [128, N], F32)
    cum = room("equal_so_far", [128, N], F32)
    zero_rows = room("zero_rows", [128, D], F32)
    small = Room(nc, g.route_small)
    colsum = small("colsum", [TR, NE], F32)
    rcol = small("rcol", [TR, NE], F32)
    rowsum = small("rowsum", [TR, NT], F32)
    rrow = small("rrow", [TR, NT], F32)
    bits = small("threshold_bits", [128, 1], I32)
    cand = small("candidate_bits", [128, 1], I32)
    count = small("count", [128, 1], F32)
    enough = small("enough", [128, 1], F32)
    nth = small("nth", [128, 1], I32)
    nths = small("nth_shifted", [128, 1], I32)
    need = small("need", [128, 1], F32)
    chosen_by = small("chosen_by", [TR, NT], F32)
    place = small("place", [TR, NT], F32)
    is_out = small("is_out", [TR, NT], F32)

    own = sem("r_own")
    cut = sem("r_cut")
    gated = sem("r_gated")
    copied = sem("r_copied")
    turned = sem("r_turned")
    to_sum = sem("r_to_sum")
    cols_summed = sem("r_cols_summed")
    planned = sem("r_planned")
    plan_turned = sem("r_plan_turned")
    spread = sem("r_spread")
    to_count = sem("r_to_count")
    counted = sem("r_counted")
    selected = sem("r_selected")
    back = sem("r_back")
    zeroed = sem("r_zeroed")
    w_hi = sem("r_w_hi")
    w_lo = sem("r_w_lo")
    plan = P[:, :, 0:NE]

    with nc.Block() as block:
        @block.vector
        def _(v):
            s = Steps(v, own)
            s.mark(v.memset(ghi[:, :, :].bitcast(F32), 0.0))
            s.mark(v.memset(glo[:, :, :].bitcast(F32), 0.0))
            s.mark(v.memset(bits[:, :], 0))
            s.then(v.memset(P[:, :, :], 0.0))
            s.then(v.tensor_copy(ghi[:, :, 0:NE], g.gate[:, :, :]))
            v.tensor_tensor(glo[:, :, 0:NE], g.gate[:, :, :], ghi[:, :, 0:NE].bitcast(F32),
                            ALU.subtract).then_inc(cut, 1)
            v.wait_ge(turned, 1)
            s.then(v.tensor_scalar(plan, g.psum[0:TR, 3, 0:NT * NE].rearrange("p (t e) -> p t e", t=NT),
                                   FLOOR, None, ALU.max))
            for i in range(SINKHORN):
                v.tensor_reduce(colsum[:, :], plan.rearrange("p t e -> p e t"), X, ALU.add).then_inc(to_sum, 1)
                v.wait_ge(cols_summed, i + 1)
                s.then(v.reciprocal(rcol[:, :], g.psum[0:TR, 4, 0:NE]))
                s.then(v.tensor_tensor(plan, plan, rcol[:, :].unsqueeze(1).to_broadcast([TR, NT, NE]), ALU.mult))
                s.then(v.tensor_reduce(rowsum[:, :], plan, X, ALU.add))
                s.then(v.reciprocal(rrow[:, :], rowsum[:, :]))
                s.then(v.tensor_tensor(plan, plan, rrow[:, :].unsqueeze(2).to_broadcast([TR, NT, NE]), ALU.mult))
            v.sem_inc(planned, 1)
            v.wait_ge(spread, 3)
            for r, shift in enumerate(SHIFTS):
                s.then(v.tensor_tensor(cand[:, :], bits[:, :], g.kshift[:, r:r + 1], ALU.bitwise_or))
                s.then(v.tensor_scalar(above[:, :], V[:, :], cand[:, :].bitcast(F32), 0.0, ALU.is_ge, ALU.add,
                                       accum_out=count[:, :]))
                v.tensor_scalar(enough[:, :], count[:, :], float(TOP), None, ALU.is_ge).then_inc(to_count, 1)
                v.wait_ge(counted, r + 1)
                s.then(v.tensor_scalar(nth[:, :], g.psum[:, 4, 16:17], -1.0, None, ALU.add))
                s.then(v.tensor_single_scalar(nths[:, :], nth[:, :], shift, ALU.logical_shift_left))
                s.then(v.tensor_tensor(bits[:, :], bits[:, :], nths[:, :], ALU.bitwise_or))
            least = bits[:, :].bitcast(F32)
            s.mark(v.tensor_scalar(above[:, :], V[:, :], least, 0.0, ALU.is_gt, ALU.add, accum_out=count[:, :]))
            s.then(v.tensor_scalar(equal[:, :], V[:, :], least, None, ALU.is_equal))
            s.mark(v.tensor_scalar(need[:, :], count[:, :], -1.0, float(TOP), ALU.mult, ALU.add))
            s.then(v.tensor_tensor_scan(cum[:, :], equal[:, :], equal[:, :], 0.0, ALU.add, ALU.max))
            s.then(v.scalar_tensor_tensor(out=equal[:, :], in0=cum[:, :], scalar=need[:, :], in1=equal[:, :],
                                          op0=ALU.is_le, op1=ALU.mult))
            s.then(v.tensor_tensor(above[:, :], above[:, :], equal[:, :], ALU.add))
            s.then(v.scalar_tensor_tensor(out=equal[:, :], in0=V[:, :], scalar=0.5, in1=above[:, :],
                                          op0=ALU.is_gt, op1=ALU.mult))
            s.then(v.tensor_tensor_scan(cum[:, :], equal[:, :], equal[:, :], 0.0, ALU.add, ALU.max))
            s.then(v.scalar_tensor_tensor(out=equal[:, :], in0=cum[:, :], scalar=g.place0[:, :], in1=equal[:, :],
                                          op0=ALU.add, op1=ALU.mult))
            v.sem_inc(selected, 1)
            v.wait_ge(back, 1)

            def by_token(bank):
                flat = g.psum[0:TR, bank:bank + 3, :].rearrange("p a b -> p (a b)")
                return flat[:, 0:NT * 128].rearrange("p (t e c) -> p t e c", t=NT, e=NE)[:, :, :, 0]

            s.then(v.tensor_reduce(chosen_by[:, :], by_token(0), X, ALU.add))
            s.then(v.tensor_scalar(chosen_by[:, :], chosen_by[:, :], 1.0, None, ALU.add))
            s.mark(v.reciprocal(is_out[:, :], chosen_by[:, :]))
            s.then(v.tensor_reduce(place[:, :], by_token(3), X, ALU.max))
            s.then(v.scalar_tensor_tensor(out=g.share[:, :], in0=place[:, :], scalar=1.0, in1=is_out[:, :],
                                          op0=ALU.min, op1=ALU.mult))
            s.mark(v.tensor_scalar(g.place_from[:, :], place[:, :], -1.0, 0.0, ALU.add, ALU.max))
            s.then(v.tensor_scalar(is_out[:, :], place[:, :], 1.0, g.far[0:TR, :], ALU.is_lt, ALU.mult))
            s.then(v.scalar_tensor_tensor(out=g.place_to[:, :], in0=place[:, :], scalar=-1.0, in1=is_out[:, :],
                                          op0=ALU.add, op1=ALU.add))

        @block.tensor
        def _(t):
            t.wait_ge(cut, 1)
            for b, (lo, hi) in enumerate(BLOCKS):
                for k in range(KD):
                    ins = cut_products(t, g.psum[:, b, 0:hi - lo], (ghi[:, k, :], glo[:, k, :]),
                                       (g.cthi[:, k, lo:hi], g.ctlo[:, k, lo:hi]), k == 0, k == KD - 1)
            ins.then_inc(gated, 1)
            t.wait_ge(copied, 3)
            for i in range(NT):
                ins = t.transpose(g.psum[0:TR, 3, i * NE:(i + 1) * NE], gT[:, i * TR:(i + 1) * TR],
                                  g.ident[0:NE, 0:NE])
            ins.then_inc(turned, 1)
            for i in range(SINKHORN):
                t.wait_ge(to_sum, i + 1)
                t.matmul(g.psum[0:TR, 4, 0:NE], g.ones[0:TR, 0:TR], colsum[:, :], start=True,
                         stop=True).then_inc(cols_summed, 1)
            t.wait_ge(planned, 1)
            for i in range(NT):
                ins = t.transpose(g.psum[:, 5 + i // 4, i % 4 * TR:(i % 4 + 1) * TR], P[:, i, :],
                                  g.ident[0:TR, 0:TR])
            ins.then_inc(plan_turned, 1)
            t.wait_ge(copied, 6)
            for b, (lo, hi) in enumerate(BLOCKS):
                t.matmul(g.psum[:, b, 0:hi - lo], g.sel16[0:NE, :], gT[:, lo:hi], start=True,
                         stop=True).then_inc(gated, 1)
            for r in range(len(SHIFTS)):
                t.wait_ge(to_count, r + 1)
                t.matmul(g.psum[:, 4, 16:17], g.blk16[:, :], enough[:, :], start=True, stop=True).then_inc(counted, 1)
            t.wait_ge(selected, 1)
            for bank, of in ((0, above), (3, equal)):
                for i in range(NT):
                    ins = t.transpose(g.psum[0:TR, bank + i // 4, i % 4 * 128:(i % 4 + 1) * 128],
                                      of[:, i * TR:(i + 1) * TR], g.ident[:, :])
            ins.then_inc(back, 1)

        @block.scalar
        def _(a):
            a.wait_ge(gated, 1)
            for b, (lo, hi) in enumerate(BLOCKS):
                a.activation(gT[:, lo:hi], g.psum[0:NE, b, 0:hi - lo], ACT.Copy).then_inc(copied, 1)
            a.wait_ge(plan_turned, 1)
            for i in range(3):
                n = min(4, NT - 4 * i) * TR
                a.activation(gT[:, 4 * i * TR:4 * i * TR + n], g.psum[0:NE, 5 + i, 0:n],
                             ACT.Copy).then_inc(copied, 1)
            for b, (lo, hi) in enumerate(BLOCKS):
                a.wait_ge(gated, b + 2)
                a.activation(V[:, lo:hi], g.psum[:, b, 0:hi - lo], ACT.Copy).then_inc(spread, 1)

        @block.gpsimd
        def _(q):
            q.memset(zero_rows[:, :], 0.0).then_inc(zeroed, 1)
            q.wait_ge(g.w_loaded[0], 16)
            q.tensor_copy(g.ewhi0[:, :, :], g.eraw[:, 0]).then_inc(w_hi, 1)
            q.wait_ge(w_hi, 1)
            q.tensor_tensor(g.ewlo0[:, :, :], g.eraw[:, 0], g.ewhi0[:, :, :].bitcast(F32),
                            ALU.subtract).then_inc(w_lo, 1)

        @block.sync
        def _(sp):
            for e in range(2):
                sp.dma_start(g.eraw[:, e], g.experts[e].rearrange("(k p) d -> p k d", p=128)).then_inc(
                    g.w_loaded[e], 16)
            sp.wait_ge(zeroed, 1)
            sp.dma_start(g.placed_d.rearrange("(t p) d -> p t d", p=128),
                         zero_rows[:, :].unsqueeze(1).to_broadcast([128, NG, D])).then_inc(g.placed_zero, 16)
            sp.wait_ge(w_lo, 1)
            sp.dma_start(g.eraw[:, 0], g.experts[2].rearrange("(k p) d -> p k d", p=128)).then_inc(
                g.w_loaded[0], 16)


def turn_groups():
    return [(t, c, min(4, NT - c)) for t in range(NT) for c in range(t, NT, 4)]


def turn_tensor(t, g, turned, moved):
    A = g.A1T
    for i, (r, c0, n) in enumerate(turn_groups()):
        if i >= 4:
            t.wait_ge(moved, 2 * (i - 3))
        for j in range(n):
            t.transpose(g.psum[0:TR, i % 4 * 2, j * TR:(j + 1) * TR],
                        A[0:TR, c0 + j, r * TR:(r + 1) * TR], g.ident[0:TR, 0:TR])
            ins = t.transpose(g.psum[0:TR, i % 4 * 2 + 1, j * TR:(j + 1) * TR],
                              A[0:TR, r, (c0 + j) * TR:(c0 + j + 1) * TR], g.ident[0:TR, 0:TR])
        ins.then_inc(turned, 1)


def turn_scalar(a, g, turned, moved):
    A = g.A1T
    for i, (r, c0, n) in enumerate(turn_groups()):
        a.wait_ge(turned, i + 1)
        a.activation(A[0:TR, r, c0 * TR:(c0 + n) * TR], g.psum[0:TR, i % 4 * 2, 0:n * TR],
                     ACT.Copy).then_inc(moved, 1)
        a.wait_ge(moved, 2 * i + 1)
        a.activation(A[0:TR, c0:c0 + n, r * TR:(r + 1) * TR],
                     g.psum[0:TR, i % 4 * 2 + 1, 0:n * TR].rearrange("p (c w) -> p c w", c=n),
                     ACT.Copy).then_inc(moved, 1)


def phase_experts(nc, sem, g):
    sent = sem("x_sent")
    back = sem("x_back")
    turned_a = sem("x_turned_a")
    moved_a = sem("x_moved_a")
    turned = sem("x_turned")
    x_hi = sem("x_hi")
    x_lo = sem("x_lo")
    w_hi = sem("x_whi")
    w_lo = sem("x_wlo")
    summed = sem("x_summed")
    copied = sem("x_copied")
    stored = [sem("x_stored0"), sem("x_stored1"), sem("x_stored2"), sem("x_stored3")]
    fetched = [sem(f"x_fetched{i}") for i in range(NT // 2)]

    def cut_buffers(e):
        return (g.ewhi0, g.ewlo0) if e % 2 == 0 else (g.ewhi1, g.ewlo1)

    with nc.Block() as block:
        @block.gpsimd
        def _(q):
            q.wait_ge(g.placed_zero, 16)
            for t in range(NT):
                q.indirect_dma_start(g.placed_d[:, :], bass.IndirectOffsetOnAxis(ap=g.place_to[:, t:t + 1], axis=0),
                                     g.c_rows[:, t, :], None, bounds_check=NP - 1, oob_is_err=False
                                     ).then_inc(sent, 16)
            for i in range(4):
                q.wait_ge(stored[i], 16 * 4)
            q.wait_ge(x_lo, NG)
            for t in range(NT):
                q.indirect_dma_start(g.fetched_rows[:, t, :], None, g.results_d[:, :],
                                     bass.IndirectOffsetOnAxis(ap=g.place_from[:, t:t + 1], axis=0),
                                     bounds_check=NP - 1, oob_is_err=False).then_inc(fetched[t // 2], 16)

        @block.sync
        def _(sp):
            sp.wait_ge(sent, 16 * NT)
            sp.dma_start(g.g_rows[:, :, :], g.placed_d.rearrange("(t p) d -> p t d", p=128)).then_inc(back, 16)
            for c in range(2 * NE):
                if c % 2 == 0 and c // 2 + 3 < NE:
                    e = c // 2 + 3
                    sp.wait_ge(w_lo, e - 2)
                    sp.dma_start(g.eraw[:, e % 2], g.experts[e].rearrange("(k p) d -> p k d", p=128)).then_inc(
                        g.w_loaded[e % 2], 16)
                sp.wait_ge(copied, c + 1)
                sp.dma_start(g.results_d[c * CH:(c + 1) * CH, :], g.y_rows[:, c % 4, :]).then_inc(stored[c % 4], 16)

        @block.scalar
        def _(a):
            def cut_w(e):
                a.wait_ge(g.w_loaded[e % 2], 16 * (e // 2 + 1))
                if e >= 2:
                    a.wait_ge(summed, 2 * (e - 1))
                else:
                    a.wait_ge(sent, 16 * NT)
                a.activation(cut_buffers(e)[0][:, :, :], g.eraw[:, e % 2], ACT.Copy).then_inc(w_hi, 1)

            turn_scalar(a, g, turned_a, moved_a)
            cut_w(1)
            for i in range(NG):
                a.wait_ge(turned, i + 1)
                a.activation(g.gxhi[:, :, i * 128:(i + 1) * 128],
                             g.psum[:, i % 4, :].rearrange("p (k c) -> p k c", k=KD), ACT.Copy).then_inc(x_hi, 1)
            for e in range(NE):
                if 1 <= e < NE - 1:
                    cut_w(e + 1)
                for h in range(2):
                    c = 2 * e + h
                    a.wait_ge(summed, c + 1)
                    if c >= 4:
                        a.wait_ge(stored[c % 4], 16 * (c // 4))
                    a.activation(g.y_rows[:, c % 4, :], g.psum[0:CH, 4 + c % 4, :], ACT.Copy).then_inc(copied, 1)

        @block.vector
        def _(v):
            def cut_w(e):
                hi, lo = cut_buffers(e)
                v.wait_ge(w_hi, e)
                v.tensor_tensor(lo[:, :, :], g.eraw[:, e % 2], hi[:, :, :].bitcast(F32),
                                ALU.subtract).then_inc(w_lo, 1)

            cut_w(1)
            for i in range(NG):
                v.wait_ge(x_hi, i + 1)
                c = slice(i * 128, (i + 1) * 128)
                v.tensor_tensor(g.gxlo[:, :, c], g.psum[:, i % 4, :].rearrange("p (k c) -> p k c", k=KD),
                                g.gxhi[:, :, c].bitcast(F32), ALU.subtract).then_inc(x_lo, 1)
            for e in range(2, NE):
                cut_w(e)
            for t in range(NT):
                v.wait_ge(fetched[t // 2], 32)
                v.scalar_tensor_tensor(out=g.x_rows[:, t, :], in0=g.fetched_rows[:, t, :],
                                       scalar=g.share[:, t:t + 1], in1=g.x_rows[:, t, :],
                                       op0=ALU.mult, op1=ALU.add)

        @block.tensor
        def _(t):
            turn_tensor(t, g, turned_a, moved_a)
            t.wait_ge(moved_a, 2 * len(turn_groups()))
            t.wait_ge(back, 16)
            for i in range(NG):
                if i >= 4:
                    t.wait_ge(x_lo, i - 3)
                for k in range(KD):
                    ins = t.transpose(g.psum[:, i % 4, k * 128:(k + 1) * 128],
                                      g.g_rows[:, i, k * 128:(k + 1) * 128], g.ident[:, :])
                ins.then_inc(turned, 1)
            for e in range(NE):
                hi, lo = cut_buffers(e)
                if e:
                    t.wait_ge(w_lo, e)
                for h in range(2):
                    c = 2 * e + h
                    if h == 0:
                        t.wait_ge(x_lo, -(-(e + 1) * PLACES // 128))
                    if c >= 4:
                        t.wait_ge(copied, c - 3)
                    at = slice(c * CH, (c + 1) * CH)
                    for k in range(KD):
                        ins = cut_products(t, g.psum[0:CH, 4 + c % 4, :], (g.gxhi[:, k, at], g.gxlo[:, k, at]),
                                           (hi[:, k, :], lo[:, k, :]), k == 0, k == KD - 1)
                    ins.then_inc(summed, 1)


def phase_norm1(nc, sem, g):
    n = norm_sems(sem, "n1")
    hi_cut = sem("n1_hi")
    lo_cut = sem("n1_lo")
    w_loaded = sem("n1_w")
    turned = sem("n1_turned")
    w_hi = sem("n1_whi")
    w_lo = sem("n1_wlo")

    with nc.Block() as block:
        @block.sync
        def _(sp):
            sp.dma_start(g.W_rows[:, :, :], g.gnn1_weight.rearrange("(o p) d -> p o d", p=128)).then_inc(w_loaded, 16)

        @block.vector
        def _(v):
            norm_vector(v, g, g.xn1, n)
            for t in range(NT):
                v.wait_ge(hi_cut, t + 1)
                v.tensor_tensor(g.r1lo[:, t, :], g.xn1[:, t, :], g.r1hi[:, t, :].bitcast(F32),
                                ALU.subtract).then_inc(lo_cut, 1)
            for k in range(KD):
                v.wait_ge(w_hi, k + 1)
                v.tensor_tensor(g.WTlo[:, k, :], g.psum[:, k, :], g.WThi[:, k, :].bitcast(F32),
                                ALU.subtract).then_inc(w_lo, 1)

        @block.scalar
        def _(a):
            for k in range(KD):
                a.wait_ge(turned, k + 1)
                a.activation(g.WThi[:, k, :], g.psum[:, k, :], ACT.Copy).then_inc(w_hi, 1)
            norm_scalar(a, g, n)
            for t in range(NT):
                a.wait_ge(n.normed, t + 1)
                a.activation(g.r1hi[:, t, :], g.xn1[:, t, :], ACT.Copy).then_inc(hi_cut, 1)

        @block.tensor
        def _(t):
            t.wait_ge(w_loaded, 16)
            for k in range(KD):
                for o in range(KD):
                    ins = t.transpose(g.psum[:, k, o * 128:(o + 1) * 128],
                                      g.W_rows[:, o, k * 128:(k + 1) * 128], g.ident[:, :])
                ins.then_inc(turned, 1)


def phase_gather1(nc, sem, g):
    RING = 3
    hi_cut = sem("g1_hi")
    lo_cut = sem("g1_lo")
    used = sem("g1_used")
    summed = sem("g1_summed")
    t_hi = sem("g1_thi")
    t_lo = sem("g1_tlo")
    order = [(b, k) for b in range(3) for k in range(NT)]
    chi, clo = g.a1hi, g.a1lo

    with nc.Block() as block:
        @block.scalar
        def _(a):
            def drain(b):
                lo, hi = BLOCKS[b]
                a.wait_ge(summed, b + 1)
                for d in range(KD):
                    a.activation(g.gthi[:, d, lo:hi], g.psum[:, b % 2 * 4 + d, 0:hi - lo],
                                 ACT.Copy).then_inc(t_hi, 1)

            for i, (b, k) in enumerate(order):
                if k == 2 and b:
                    drain(b - 1)
                lo, hi = BLOCKS[b]
                if i >= RING:
                    a.wait_ge(used, i - RING + 1)
                a.activation(chi[:, i % RING, 0:hi - lo], g.A1T[0:TR, k, lo:hi], ACT.Copy).then_inc(hi_cut, 1)
            drain(2)

        @block.vector
        def _(v):
            def drain(b):
                lo, hi = BLOCKS[b]
                for d in range(KD):
                    v.wait_ge(t_hi, b * KD + d + 1)
                    v.tensor_tensor(g.gtlo[:, d, lo:hi], g.psum[:, b % 2 * 4 + d, 0:hi - lo],
                                    g.gthi[:, d, lo:hi].bitcast(F32), ALU.subtract).then_inc(t_lo, 1)

            for i, (b, k) in enumerate(order):
                if k == 3 and b:
                    drain(b - 1)
                lo, hi = BLOCKS[b]
                v.wait_ge(hi_cut, i + 1)
                v.tensor_tensor(clo[:, i % RING, 0:hi - lo], g.A1T[0:TR, k, lo:hi],
                                chi[:, i % RING, 0:hi - lo].bitcast(F32), ALU.subtract).then_inc(lo_cut, 1)
            drain(2)

        @block.tensor
        def _(t):
            for i, (b, k) in enumerate(order):
                lo, hi = BLOCKS[b]
                if k == 0 and b == 2:
                    t.wait_ge(t_lo, KD)
                t.wait_ge(lo_cut, i + 1)
                for d in range(KD):
                    f = slice(d * 128, (d + 1) * 128)
                    ins = cut_products(t, g.psum[:, b % 2 * 4 + d, 0:hi - lo],
                                       (g.r1hi[:, k, f], g.r1lo[:, k, f]),
                                       (chi[:, i % RING, 0:hi - lo], clo[:, i % RING, 0:hi - lo]),
                                       k == 0, k == NT - 1)
                ins.then_inc(used, 1)
                if k == NT - 1:
                    t.matmul(g.psum[:, b % 2 * 4 + 3, 0:2], g.zeros[:, :], g.zeros[:, 0:2], start=False,
                             stop=True, skip_group_check=True).then_inc(summed, 1)


def phase_project(nc, sem, g):
    summed = sem("p_summed")
    added = sem("p_added")
    with nc.Block() as block:
        @block.tensor
        def _(t):
            for i in range(NT):
                if i >= 8:
                    t.wait_ge(added, i - 7)
                c = slice(i * TR, (i + 1) * TR)
                for k in range(KD):
                    ins = cut_products(t, g.psum[0:TR, i % 8, :], (g.gthi[:, k, c], g.gtlo[:, k, c]),
                                       (g.WThi[:, k, :], g.WTlo[:, k, :]), k == 0, k == KD - 1)
                ins.then_inc(summed, 1)

        @block.vector
        def _(v):
            for i in range(NT):
                v.wait_ge(summed, i + 1)
                v.tensor_tensor(g.x_rows[:, i, :], g.x_rows[:, i, :], g.psum[0:TR, i % 8, :],
                                ALU.add).then_inc(added, 1)


def phase_leaves(nc, sem, g):
    room = Room(nc, g.leaves_at)
    rhi = room("rw_hi", [128, KD, 128], F32R)
    rlo = room("rw_lo", [128, KD, 128], F32R)
    p7 = room("node_p", [7, N], F32)
    f = [room(f"factor{d}", [NE, N], F32) for d in range(3)]
    leaf = room("leaf", [NE, N], F32)

    own = sem("l_own")
    cut = sem("l_cut")
    summed = sem("l_summed")
    nodes = sem("l_nodes")
    spread = sem("l_spread")
    factors = sem("l_factors")
    ready = sem("l_ready")

    with nc.Block() as block:
        @block.vector
        def _(v):
            s = Steps(v, own)
            s.mark(v.memset(rhi[:, :, :].bitcast(F32), 0.0))
            s.mark(v.memset(rlo[:, :, :].bitcast(F32), 0.0))
            s.mark(v.tensor_scalar(g.b2half[:, :], g.vecs[:, 36:68], 0.5, None, ALU.mult))
            s.mark(v.memset(g.acc[:, :, :], 0.0))
            s.wait()
            rw = g.vecs[:, 68:96].rearrange("p (n k) -> p k n", n=7)
            s.then(v.tensor_copy(rhi[:, :, 0:7], rw))
            v.tensor_tensor(rlo[:, :, 0:7], rw, rhi[:, :, 0:7].bitcast(F32), ALU.subtract).then_inc(cut, 1)
            v.wait_ge(factors, 9)
            s.then(v.tensor_tensor(f[0][:, :], f[0][:, :], f[1][:, :], ALU.mult))
            v.tensor_tensor(leaf[:, :], f[0][:, :], f[2][:, :], ALU.mult).then_inc(ready, 1)

        @block.tensor
        def _(t):
            t.wait_ge(cut, 1)
            for b, (lo, hi) in enumerate(BLOCKS):
                for k in range(KD):
                    ins = cut_products(t, g.psum[:, b, 0:hi - lo], (rhi[:, k, :], rlo[:, k, :]),
                                       (g.fthi[:, k, lo:hi], g.ftlo[:, k, lo:hi]), k == 0, k == KD - 1)
                ins.then_inc(summed, 1)
            t.wait_ge(nodes, 3)
            for b, (lo, hi) in enumerate(BLOCKS):
                if b == 2:
                    t.wait_ge(factors, 3)
                for d in range(3):
                    t.matmul(g.psum[0:NE, b % 2 * 3 + d, 0:hi - lo], g.leafsel[0:7, 8 * d:8 * d + 8],
                             p7[:, lo:hi], start=True, stop=True).then_inc(spread, 1)

        @block.scalar
        def _(a):
            for b, (lo, hi) in enumerate(BLOCKS):
                a.wait_ge(summed, b + 1)
                a.activation(p7[:, lo:hi], g.psum[0:7, b, 0:hi - lo], ACT.Sigmoid,
                             bias=g.rb_col[0:7, :]).then_inc(nodes, 1)
            for b, (lo, hi) in enumerate(BLOCKS):
                for d in range(3):
                    a.wait_ge(spread, b * 3 + d + 1)
                    a.activation(f[d][:, lo:hi], g.psum[0:NE, b % 2 * 3 + d, 0:hi - lo], ACT.Identity,
                                 bias=g.leafone[0:NE, d:d + 1]).then_inc(factors, 1)

        @block.sync
        def _(sp):
            sp.wait_ge(ready, 1)
            sp.dma_start(g.leaf_dram, leaf[:, :]).then_inc(g.leaf_stored, 16)
            sp.wait_ge(g.leaf_stored, 16)


def phase_tree(nc, sem, g):
    PAIRS = HID1 // 256
    STEPS = 48
    room = Room(nc, g.tree_at)
    w1hi = room("w1_hi", [128, 4, KD, 256], F32R)
    w1lo = room("w1_lo", [128, 4, KD, 256], F32R)
    w2hi = room("w2_hi", [128, 4, 2, D], F32R)
    w2lo = room("w2_lo", [128, 4, 2, D], F32R)
    raw1 = room("w1_raw", [128, 2, KD, 256], F32)
    raw2 = room("w2_raw", [128, 2, 2, D], F32)
    room.next += COLS
    leafb = room("leaf_all", [128, N], F32)
    G = room("gelu", [128, 3, BW], F32)
    hhi = room("hidden_hi", [128, 4, BW], F32R)
    hlo = room("hidden_lo", [128, 4, BW], F32R)
    ytmp = room("y_scaled", [128, KD, BW], F32)

    loaded = [sem("t_loaded0"), sem("t_loaded1")]
    w_hi = sem("t_whi")
    cut = sem("t_cut")
    hidden = sem("t_hidden")
    begun = sem("t_begun")
    active = sem("t_active")
    hi_cut = sem("t_hi")
    lo_cut = sem("t_lo")
    used = sem("t_used")
    y_sum = sem("t_ysum")
    y_free = sem("t_yfree")
    acc_done = sem("t_acc")
    leaf_in = sem("t_leaf")

    w1_d = g.w1.rearrange("e (k p) h -> e p k h", p=128)
    w2_d = g.w2.rearrange("e (j p) d -> e p j d", p=128)

    def where(s):
        return s // 24, s % 24 // 8, s % 8 // 2, s % 2

    with nc.Block() as block:
        @block.sync
        def _(sp):
            with sp.Fori(0, NE) as e:
                for p in range(PAIRS):
                    if p == 4:
                        sp.wait_ge(y_free, e * 24 + 4)
                        sp.dma_start(leafb[:, :], g.leaf_dram[bass.ds(e, 1), :].partition_broadcast(128)
                                     ).then_inc(leaf_in, 16)
                    sp.wait_ge(cut, e * PAIRS + p + 1)
                    sp.dma_start(raw1[:, p % 2], w1_d[bass.ds(e, 1), :, :, p * 256:(p + 1) * 256].rearrange(
                        "e p k h -> p (e k) h")).then_inc(loaded[p % 2], 16)
                    sp.dma_start(raw2[:, p % 2], w2_d[bass.ds(e, 1), :, 2 * p:2 * p + 2, :].rearrange(
                        "e p j d -> p (e j) d")).then_inc(loaded[p % 2], 16)

        @block.vector
        def _(v):
            v.sem_inc(cut, 2)
            v.sem_inc(lo_cut, 3)
            v.sem_inc(y_free, 4)

            def cut1(e, p):
                q = p % 4
                v.wait_ge(loaded[p % 2], e * (16 * PAIRS) + 32 * (p // 2 + 1))
                v.wait_ge(used, (e * 2 + p // 4) * 24 + 18 + 2 * q)
                v.tensor_copy(w1hi[:, q], raw1[:, p % 2]).then_inc(w_hi, 1)
                v.wait_ge(w_hi, e * (2 * PAIRS) + 2 * p + 1)
                v.tensor_tensor(w1lo[:, q], raw1[:, p % 2], w1hi[:, q].bitcast(F32), ALU.subtract)

            def cut2(e, p):
                q = p % 4
                v.tensor_copy(w2hi[:, q], raw2[:, p % 2]).then_inc(w_hi, 1)
                v.wait_ge(w_hi, e * (2 * PAIRS) + 2 * p + 2)
                v.tensor_tensor(w2lo[:, q], raw2[:, p % 2], w2hi[:, q].bitcast(F32),
                                ALU.subtract).then_inc(cut, 1)

            def cuts(e, s, last):
                r = (s - 20) % 24
                if r < 8:
                    p = (s - 20) // 24 * 4 + 4 + r // 2
                    at = e
                    if p >= PAIRS:
                        if last:
                            return
                        at, p = e + 1, p - PAIRS
                    (cut2 if r % 2 else cut1)(at, p)

            def drain(e, m):
                lo, hi = BLOCKS[m % 3]
                if m == 0:
                    v.wait_ge(leaf_in, e * 16 + 16)
                for d in range(KD):
                    if d < 3:
                        v.wait_ge(y_sum, e * 18 + 3 * m + d + 1)
                    else:
                        v.wait_ge(used, e * STEPS + 24 + 8 * m + 8)
                    v.wait_ge(acc_done, e * 24 + 4 * m + d + 1)
                    v.scalar_tensor_tensor(out=ytmp[:, d, 0:hi - lo], in0=g.psum[:, d, 0:hi - lo],
                                           scalar=g.b2half[:, bass.ds(e * 4 + d, 1)], in1=leafb[:, lo:hi],
                                           op0=ALU.add, op1=ALU.mult).then_inc(y_free, 1)

            def expert(e, last):
                for s in range(STEPS):
                    half, b, _, _ = where(s)
                    w = BLOCKS[b][1] - BLOCKS[b][0]
                    v.wait_ge(hi_cut, e * STEPS + s + 1)
                    v.tensor_tensor(hlo[:, s % 4, 0:w], G[:, s % 3, 0:w], hhi[:, s % 4, 0:w].bitcast(F32),
                                    ALU.subtract).then_inc(lo_cut, 1)
                    if s % 8 == 0 and s:
                        drain(e, s // 8 - 1)
                    cuts(e, s, last)
                drain(e, 5)

            for p in range(2):
                cut1(0, p)
                cut2(0, p)
            with v.Fori(0, NE - 1) as e:
                expert(e, False)
            expert(NE - 1, True)

        @block.gpsimd
        def _(q):
            q.sem_inc(acc_done, 4)
            with q.Fori(0, NE) as e:
                for m in range(6):
                    lo, hi = BLOCKS[m % 3]
                    for d in range(KD):
                        q.wait_ge(y_free, e * 24 + 4 * m + d + 5)
                        q.tensor_tensor(g.acc[:, d, lo:hi], g.acc[:, d, lo:hi], ytmp[:, d, 0:hi - lo],
                                        ALU.add).then_inc(acc_done, 1)

        @block.scalar
        def _(a):
            a.sem_inc(active, 4)
            with a.Fori(0, NE) as e:
                for s in range(STEPS):
                    half, b, q, j = where(s)
                    w = BLOCKS[b][1] - BLOCKS[b][0]
                    a.wait_ge(hidden, e * STEPS + s + 1)
                    a.wait_ge(lo_cut, e * STEPS + s + 1)
                    a.sem_inc(begun, 1)
                    a.activation(G[:, s % 3, 0:w], g.psum[:, 4 + s % 4, 0:w], ACT.Gelu,
                                 bias=g.b1cols[:, bass.ds(e * 16 + half * 8 + 2 * q + j, 1)]).then_inc(active, 1)
                    a.wait_ge(active, e * STEPS + s + 5)
                    a.wait_ge(used, e * STEPS + s + 21)
                    a.activation(hhi[:, s % 4, 0:w], G[:, s % 3, 0:w], ACT.Copy).then_inc(hi_cut, 1)

        @block.tensor
        def _(t):
            t.sem_inc(used, 24)

            def first(e, s):
                half, b, q, j = where(s)
                lo, hi = BLOCKS[b]
                if b == 0 and j == 0:
                    t.wait_ge(cut, e * PAIRS + half * 4 + q + 3)
                t.wait_ge(active, e * STEPS + s + 1)
                c = slice(j * 128, (j + 1) * 128)
                for k in range(KD):
                    ins = cut_products(t, g.psum[:, 4 + s % 4, 0:hi - lo], (w1hi[:, q, k, c], w1lo[:, q, k, c]),
                                       (g.fthi[:, k, lo:hi], g.ftlo[:, k, lo:hi]), k == 0, k == KD - 1)
                ins.then_inc(hidden, 1)

            def second(e, s):
                half, b, q, j = where(s)
                w = BLOCKS[b][1] - BLOCKS[b][0]
                t.wait_ge(lo_cut, e * STEPS + s + 4)
                for d in range(KD):
                    if s % 8 == 0:
                        t.wait_ge(y_free, e * 24 + 4 * (s // 8) + d + 1)
                    c = slice(d * 128, (d + 1) * 128)
                    ins = cut_products(t, g.psum[:, d, 0:w], (w2hi[:, q, j, c], w2lo[:, q, j, c]),
                                       (hhi[:, s % 4, 0:w], hlo[:, s % 4, 0:w]), s % 8 == 0, s % 8 == 7)
                    if d == 3:
                        ins.then_inc(used, 1)
                    elif s % 8 == 7:
                        ins.then_inc(y_sum, 1)

            first(0, 0)
            first(0, 1)
            with t.Fori(0, NE - 1) as e:
                for s in range(STEPS):
                    second(e, s)
                    if s + 2 < STEPS:
                        first(e, s + 2)
                    else:
                        first(e + 1, s + 2 - STEPS)
            for s in range(STEPS):
                second(NE - 1, s)
                if s + 2 < STEPS:
                    first(NE - 1, s + 2)


def phase_out(nc, sem, g):
    turned = sem("o_turned")
    added = sem("o_added")
    stored = sem("o_stored")
    with nc.Block() as block:
        @block.tensor
        def _(t):
            for i in range(NT):
                if i >= 8:
                    t.wait_ge(added, i - 7)
                for d in range(KD):
                    ins = t.transpose(g.psum[0:TR, i % 8, d * 128:(d + 1) * 128],
                                      g.acc[:, d, i * TR:(i + 1) * TR], g.ident[:, :])
                ins.then_inc(turned, 1)

        @block.vector
        def _(v):
            for i in range(NT):
                v.wait_ge(turned, i + 1)
                v.tensor_tensor(g.x_rows[:, i, :], g.x_rows[:, i, :], g.psum[0:TR, i % 8, :],
                                ALU.add).then_inc(added, 1)

        @block.sync
        def _(sp):
            for i in range(NT):
                sp.wait_ge(added, i + 1)
                sp.dma_start(g.out[i * TR:(i + 1) * TR, :], g.x_rows[:, i, :]).then_inc(stored, 16)
            sp.wait_ge(stored, 16 * NT)


INPUTS = ["x", "src", "dst", "edge_weight", "gnn0_eps", "gnn0_W1", "gnn0_b1", "gnn0_g1", "gnn0_be1",
          "gnn0_W2", "gnn0_b2", "gnn0_g2", "gnn0_be2", "gate_w", "experts", "gnn1_weight", "rw", "rb",
          "w1", "b1", "w2", "b2", "consts_d", "bits_d"]


def gnn_ffn_kernel(nc, x, src, dst, edge_weight, gnn0_eps, gnn0_W1, gnn0_b1, gnn0_g1, gnn0_be1, gnn0_W2,
                   gnn0_b2, gnn0_g2, gnn0_be2, gate_w, experts, gnn1_weight, rw, rb, w1, b1, w2, b2,
                   consts_d, bits_d, out):
    with ExitStack() as ctx:
        def sem(name):
            return ctx.enter_context(nc.semaphore(name))

        g = Record()
        g.x, g.src, g.dst, g.edge_weight, g.out = x, src, dst, edge_weight, out
        g.gnn0_eps, g.gnn0_W1, g.gnn0_b1, g.gnn0_g1, g.gnn0_be1 = gnn0_eps, gnn0_W1, gnn0_b1, gnn0_g1, gnn0_be1
        g.gnn0_W2, g.gnn0_b2, g.gnn0_g2, g.gnn0_be2 = gnn0_W2, gnn0_b2, gnn0_g2, gnn0_be2
        g.gate_w, g.experts, g.gnn1_weight = gate_w, experts, gnn1_weight
        g.rw, g.rb, g.w1, g.b1, g.w2, g.b2 = rw, rb, w1, b1, w2, b2
        g.consts_d, g.bits_d = consts_d, bits_d
        g.psum = ctx.enter_context(nc.psum_tensor("psum", [128, 8, 512], F32))
        g.leaf_dram = nc.dram_tensor("leaf_rows", (NE, N), F32).ap()
        g.x_loaded, g.W2_loaded, g.leaf_stored = sem("x_loaded"), sem("W2_loaded"), sem("leaf_stored")

        keep = Room(nc, 0)
        g.small = keep("small_consts", [128, C_I10], F32)
        g.ident = g.small[:, C_ID:C_ID + 128]
        g.ones = g.small[:, C_ONE:C_ONE + 128]
        g.blk16 = g.small[:, C_BLK:C_BLK + 128]
        g.sel16 = g.small[:, C_SEL:C_SEL + 128]
        g.leafsel = g.small[:, C_LSEL:C_LSEL + 24]
        g.leafone = g.small[:, C_LONE:C_LONE + 3]
        g.rowno = g.small[:, C_ROW:C_ROW + 1]
        g.iota32 = g.small[:, C_I32:C_I32 + WIN]
        g.w2k = g.small[:, C_W2K:C_W2K + NW]
        g.blkno = g.small[:, C_BLKNO:C_BLKNO + NB]
        g.place0 = g.small[:, C_PLACE:C_PLACE + 1]
        g.far = g.small[:, C_FAR:C_FAR + 1]
        g.kshift = keep("kshift", [128, len(SHIFTS)], I32)
        g.eps0 = keep("eps0", [128, 1], F32)
        g.vecrows = keep("vecrows", [96, 128], F32)
        g.b1rows = keep("b1rows", [128, 128], F32)
        g.gate = keep("gate", [128, KD, NE], F32)
        g.rb_col = keep("rb_col", [7, 1], F32)
        g.vecs = keep("vecs", [128, 96], F32)
        g.b1v, g.g1v, g.be1v = g.vecs[:, 0:8], g.vecs[:, 8:16], g.vecs[:, 16:24]
        g.b2v, g.g2v, g.be2v = g.vecs[:, 24:28], g.vecs[:, 28:32], g.vecs[:, 32:36]
        g.b1cols = keep("b1cols", [128, 128], F32)
        g.b2half = keep("b2half", [128, 32], F32)
        g.zeros = keep("zeros", [128, 128], BF16)
        g.bounds = keep("bounds", [1, 2 * NW], I32)
        g.key = keep("key", [EB, NB + SLOTS], F32)
        g.share = keep("share", [TR, NT], F32)
        g.place_to = keep("place_to", [TR, NT], I32)
        g.place_from = keep("place_from", [TR, NT], I32)
        g.stats = keep("stats", [TR, NT, 6], F32)
        g.meanvar = keep("meanvar", [TR, NT, 2], F32)
        g.dev = keep("dev", [TR, NT], F32)
        g.dev2 = keep("dev2", [TR, NT], F32)
        g.rstd = keep("rstd", [TR, NT], F32)
        bn = g.bn = Record()
        bn.stats = keep("bn_stats", [128, 12, 6], F32)
        bn.mv = keep("bn_mv", [128, 2], F32)
        bn.mv4 = keep("bn_mv4", [128, KD, 2], F32)
        bn.a = keep("bn_var", [128, KH0], F32)
        bn.b = keep("bn_mean", [128, KH0], F32)
        bn.c = keep("bn_dev", [128, KH0], F32)
        bn.d = keep("bn_rdev", [128, KH0], F32)
        bn.scale = keep("bn_scale", [128, KH0], F32)
        bn.shift = keep("bn_shift", [128, KH0], F32)
        g.route_small = keep.next
        assert keep.next + 32 * 16 <= X_AT, keep.next
        g.x_rows = Room(nc, X_AT)("x_rows", [TR, NT, D], F32)

        room = Room(nc, REG)
        g.A1T = room("A1T", [128, NT, ND], F32)
        g.A0T = room("A0T", [128, NT, ND], BF16)
        g.D_all = room("dst_onehot", [EB, NB + SLOTS, 4, WIN], BF16)
        g.D_flat = g.D_all[:, :, :, :].rearrange("p b a w -> p (b a w)")
        g.i10 = room("i10", [EB, NC], F16)
        g.scratch_at = room.next
        phase_edges(nc, sem, g)
        phase_adjacency(nc, sem, g)

        room = Room(nc, A1_END + NT * ND * 2)
        g.rhi = room("xn_hi", [TR, NT, D], F32R)
        g.rlo = room("xn_lo", [TR, NT, D], F32R)
        g.xn = room("xn", [TR, NT, D], F32)
        g.a0chunk = room("A0_chunk", [TR, 2, BW], F32R)
        g.thi = room("hT_hi", [128, KD, N], F32R)
        g.tlo = room("hT_lo", [128, KD, N], F32R)
        phase_norm0(nc, sem, g)
        phase_gather0(nc, sem, g)
        room = Room(nc, A1_END)
        g.h1 = room("h1", [128, KH0, N], F32)
        g.w1_at = room.next
        g.yT = room("yT", [128, KD, N], F32)
        g.W2_raw = room("W2_raw", [128, KH0, D], F32)
        g.w2_cut_at = room.next
        phase_mlp1(nc, sem, g)
        phase_mlp2(nc, sem, g)
        add_turned(nc, sem, g, "y0", g.yT)

        room = Room(nc, A1_END)
        g.eraw = room("expert_raw", [128, 2, KD, D], F32)
        g.ewhi0 = room("expert_hi0", [128, KD, D], F32R)
        g.ewlo0 = room("expert_lo0", [128, KD, D], F32R)
        sent_at = room.next
        rows = g.c_rows = room("c_rows", [TR, NT, D], F32)
        cols_at = room.next
        g.cthi = room("c_xT_hi", [128, KD, N], F32R)
        g.ctlo = room("c_xT_lo", [128, KD, N], F32R)
        g.route_at = room.next
        room = Room(nc, sent_at)
        g.ewhi1 = room("expert_hi1", [128, KD, D], F32R)
        g.ewlo1 = room("expert_lo1", [128, KD, D], F32R)
        room = Room(nc, cols_at)
        g.g_rows = room("rows_by_place", [128, NG, D], F32)
        g.gxhi = room("xT_by_place_hi", [128, KD, NP], F32R)
        g.gxlo = room("xT_by_place_lo", [128, KD, NP], F32R)
        g.y_rows = room("expert_results", [CH, 4, D], F32)
        g.fetched_rows = Room(nc, cols_at)("fetched_rows", [TR, NT, D], F32)
        g.placed_d = nc.dram_tensor("rows_by_place_d", (NP, D), F32).ap()
        g.results_d = nc.dram_tensor("expert_results_d", (NP, D), F32).ap()
        g.w_loaded = [sem("expert_loaded0"), sem("expert_loaded1")]
        g.placed_zero = sem("placed_zero")
        norm_and_turn(nc, sem, g, "c", rows, g.cthi, g.ctlo)
        phase_route(nc, sem, g)
        phase_experts(nc, sem, g)

        room = Room(nc, A1_END)
        g.r1hi = room("d_rows_hi", [TR, NT, D], F32R)
        g.r1lo = room("d_rows_lo", [TR, NT, D], F32R)
        g.W_rows = room("W_rows", [128, KD, D], F32)
        g.WThi = room("WT_hi", [128, KD, D], F32R)
        g.WTlo = room("WT_lo", [128, KD, D], F32R)
        g.xn1 = Room(nc, room.next)("d_rows", [TR, NT, D], F32)
        g.gthi = room("aggT_hi", [128, KD, N], F32R)
        g.gtlo = room("aggT_lo", [128, KD, N], F32R)
        g.a1hi = room("A1_hi", [TR, 3, BW], F32R)
        g.a1lo = room("A1_lo", [TR, 3, BW], F32R)
        phase_norm1(nc, sem, g)
        phase_gather1(nc, sem, g)
        phase_project(nc, sem, g)

        room = Room(nc, REG)
        g.fthi = room("f_xT_hi", [128, KD, N], F32R)
        g.ftlo = room("f_xT_lo", [128, KD, N], F32R)
        g.tree_at = room.next
        acc_at = g.tree_at + 5 * 16384
        rows = Room(nc, acc_at)("f_rows", [TR, NT, D], F32)
        g.acc = Room(nc, acc_at)("acc", [128, KD, N], F32)
        norm_and_turn(nc, sem, g, "f", rows, g.fthi, g.ftlo)
        g.leaves_at = g.tree_at
        phase_leaves(nc, sem, g)
        phase_tree(nc, sem, g)
        phase_out(nc, sem, g)


def kernel(**inputs):
    import concourse.bacc as bacc
    from concourse.bass_utils import run_bass_kernel_spmd

    nc = bacc.Bacc("TRN2", target_bir_lowering=False, num_devices=1)
    names = {
        "gnn0_eps": "L0_gnn_eps", "gnn0_W1": "L0_gnn_W1", "gnn0_b1": "L0_gnn_b1", "gnn0_g1": "L0_gnn_g1",
        "gnn0_be1": "L0_gnn_be1", "gnn0_W2": "L0_gnn_W2", "gnn0_b2": "L0_gnn_b2", "gnn0_g2": "L0_gnn_g2",
        "gnn0_be2": "L0_gnn_be2", "gate_w": "L0_ffn_gate_w", "experts": "L0_ffn_experts",
        "gnn1_weight": "L1_gnn_weight", "rw": "L1_ffn_rw", "rb": "L1_ffn_rb", "w1": "L1_ffn_w1",
        "b1": "L1_ffn_b1", "w2": "L1_ffn_w2", "b2": "L1_ffn_b2",
    }
    consts, bits = shape_constants()
    arrays, drams = {}, {}
    for name in INPUTS:
        a = {"consts_d": consts, "bits_d": bits}.get(name)
        if a is None:
            a = np.ascontiguousarray(inputs[names.get(name, name)])
            a = a.reshape(1) if a.ndim == 0 else a
        arrays["in_" + name] = a
        drams[name] = nc.dram_tensor("in_" + name, a.shape, mybir.dt.from_np(a.dtype), kind="ExternalInput").ap()
    drams["out"] = nc.dram_tensor("out_rows", (N, D), F32, kind="ExternalOutput").ap()
    gnn_ffn_kernel(nc, **drams)
    got = run_bass_kernel_spmd(nc, [arrays], core_ids=[0])
    return got.results[0]["out_rows"]
```

```python
from contextlib import ExitStack

import numpy as np

import concourse.bass as bass
from concourse import mybir

F32 = mybir.dt.float32
F32R = mybir.dt.float32r
F16 = mybir.dt.float16
BF16 = mybir.dt.bfloat16
I32 = mybir.dt.int32
ACT = mybir.ActivationFunctionType
ALU = mybir.AluOpType
X = mybir.AxisListType.X

N = 1250
D = 512
TR = 125
NT = N // TR
KD = D // 128
EDGES = 20000
EB = 125
NB = EDGES // EB
EQ = NB // 2
WIN = 32
NW = -(-N // WIN)
NC = NT * 128
ND = NW * WIN
SLOTS = 6
GROUP = NW // NT
KEY = 2048
HID0 = 1024
KH0 = HID0 // 128
NE = 8
TOP = N // NE
PLACES = 160
NP = NE * PLACES
CH = PLACES // 2
NG = NP // 128
FAR = 3000
HID1 = 2048
EPS = 1e-5
FLOOR = 1e-10
SINKHORN = 8
BLOCKS = [(0, 418), (418, 834), (834, 1250)]
BW = 418
SHIFTS = [26, 22, 18, 14, 10, 6, 2, 0]

C_ID, C_ONE, C_BLK, C_TRI, C_LSEL, C_LONE, C_ROW = 0, 128, 256, 384, 512, 536, 539
C_I32, C_W2K, C_BLKNO, C_PLACE, C_FIRST, C_MASK, C_FAR, C_I10 = 540, 572, 612, 772, 780, 788, 868, 869
C_END = C_I10 + NC


def shape_constants():
    c = np.zeros((128, C_END), np.float32)
    p = np.arange(128)
    c[:, C_ID:C_ID + 128] = np.eye(128)
    c[:, C_ONE:C_ONE + 128] = 1
    c[:, C_BLK:C_BLK + 128] = p[:, None] // 16 == p[None] // 16
    c[:, C_TRI:C_TRI + 128] = p[:, None] <= p[None]
    for depth in range(3):
        for e in range(NE):
            node, bit = 2**depth - 1 + (e >> (3 - depth)), (e >> (2 - depth)) & 1
            c[node, C_LSEL + 8 * depth + e] = 1 if bit else -1
            c[e, C_LONE + depth] = 0 if bit else 1
    c[:, C_ROW] = p
    c[:, C_I32:C_I32 + WIN] = np.arange(WIN)
    c[:, C_W2K:C_W2K + NW] = KEY * np.arange(NW)
    c[:, C_BLKNO:C_BLKNO + NB] = (2 * np.arange(EQ)[None] + np.arange(2)[:, None]).reshape(-1)
    c[:, C_PLACE:C_PLACE + NE] = PLACES * np.arange(NE)
    c[:, C_FIRST:C_FIRST + NE] = p[:, None] == 16 * np.arange(NE)
    c[:, C_MASK:C_MASK + NE * NT] = np.arange(NE * NT) % NT != 0
    c[:, C_FAR] = FAR + p
    i10 = np.full((NT, 128), -1.0)
    i10[:, :TR] = np.arange(N).reshape(NT, TR)
    c[:, C_I10:] = i10.reshape(-1)
    bits = np.zeros((128, len(SHIFTS)), np.int32)
    for r, s in enumerate(SHIFTS):
        limit = 4 if r == len(SHIFTS) - 1 else 16
        bits[:, r] = np.where(p % 16 < limit - 1, (p % 16 + 1) << s, 0x40000000)
    return c, bits


X_AT = 8960
REG = X_AT + NT * D * 4
A1_END = REG + NT * ND * 4
XN_AT = REG + 6 * NT * ND + 2 * NT * D * 4 + 2 * KD * N * 4 + 4096
ROWS = NT * D * 4
COLS = KD * N * 4


class Record:
    pass


class Room:

    def __init__(self, nc, start):
        self.nc, self.next = nc, start

    def __call__(self, name, shape, dtype):
        width = {F32: 4, F32R: 4, I32: 4, F16: 2, BF16: 2}[dtype]
        start = -(-self.nc.sbuf_base // 32) * 32
        buffer = self.nc.alloc_sbuf_tensor_at(name, shape, dtype, offset=start + self.next)
        self.next += -(-int(np.prod(shape[1:])) * width // 32) * 32
        return buffer


class Steps:

    def __init__(self, semaphore):
        self.engine, self.semaphore, self.n = None, semaphore, 0

    def on(self, engine):
        self.engine = engine
        return self

    def mark(self, ins):
        ins.then_inc(self.semaphore, 1)
        self.n += 1
        return self.n

    def wait(self, n=None):
        self.engine.wait_ge(self.semaphore, self.n if n is None else n)

    def then(self, ins):
        self.mark(ins)
        self.wait()


def pieces(lo, hi):
    return [(t, max(lo, t * TR) - t * TR, min(hi, (t + 1) * TR) - t * TR)
            for t in range(NT) if t * TR < hi and (t + 1) * TR > lo]


def halves(ap):
    return ap.rearrange("p (q h) -> p q h", h=2)


def phase_edges(nc, sem, g):
    room = Room(nc, g.scratch_at)
    raw_i = room("edge_ints", [EQ, 2, 2 * EB], I32)
    wraw = room("edge_w", [EQ, 2 * EB], F32)
    win_i = room("edge_win", [EQ, 2 * EB], I32)
    rem_i = room("edge_rem", [EQ, 2 * EB], I32)
    keyrem = room("edge_keyrem", [EQ, 2, 2 * EB], F32)
    extent = room("edge_extent", [EQ, 4], F32)
    spread = room("edge_spread", [EQ, 4, NW], F32)
    rem = room("rem", [EB, NB], F32)
    wcol = room("wcol", [EB, NB], F32)
    wres = room("wres", [EB, NB], F32)
    wres2 = room("wres2", [EB, NB], F32)
    parts = room("parts", [EB, NB, 3], BF16)
    meets1 = room("meets1", [NW, NB], F32)
    meets = room("meets", [NW, NB], F32)
    pick = room("pick", [NW, 2, NB], F32)
    ends = room("ends", [NW, 2], F32)
    lohi = room("lohi", [NW, 2], F32)
    i10f = room("i10f", [128, NC], F32)

    at = Record()
    loaded = sem("e_loaded")
    later_loaded = sem("e_later_loaded")
    one_hot = sem("e_one_hot")
    turned = sem("e_turned")

    loads = [
        (g.small[:, :], g.consts_d[:, 0:C_I10]), (raw_i[:, 0, :], g.src.rearrange("(q e) -> q e", q=EQ)),
        (raw_i[:, 1, :], g.dst.rearrange("(q e) -> q e", q=EQ)),
        (wraw[:, :], g.edge_weight.rearrange("(q e) -> q e", q=EQ)), (i10f[:, :], g.consts_d[:, C_I10:C_END]),
    ]
    later_loads = [
        (g.kshift[:, :], g.bits_d), (g.eps0[:, :], g.gnn0_eps.partition_broadcast(128)),
        (g.vecrows[0:8, :], g.gnn0_b1.rearrange("(t p) -> t p", p=128)),
        (g.vecrows[8:16, :], g.gnn0_g1.rearrange("(t p) -> t p", p=128)),
        (g.vecrows[16:24, :], g.gnn0_be1.rearrange("(t p) -> t p", p=128)),
        (g.vecrows[24:28, :], g.gnn0_b2.rearrange("(t p) -> t p", p=128)),
        (g.vecrows[28:32, :], g.gnn0_g2.rearrange("(t p) -> t p", p=128)),
        (g.vecrows[32:36, :], g.gnn0_be2.rearrange("(t p) -> t p", p=128)),
        (g.vecrows[36:68, :], g.b2.rearrange("e (t p) -> (e t) p", p=128)),
        (g.vecrows[68:96, :], g.rw.rearrange("n (t p) -> (n t) p", p=128)),
        (g.b1rows[:, :], g.b1.rearrange("e (t p) -> (e t) p", p=128)),
        (g.gate[:, :, :], g.gate_w[0].rearrange("(k p) e -> p k e", p=128)),
        (g.rb_col[0:7, :], g.rb.rearrange("(n a) -> n a", a=1)),
    ]

    NB_V = NB * 5 // 8

    def weighted_rows(eng, mark, b0, b1):
        d = g.D_all[:, b0:b1, :, :]
        for c in range(3):
            mark(eng.tensor_tensor(d[:, :, 1 + c, :], d[:, :, 0, :],
                                   parts[:, b0:b1, c:c + 1].to_broadcast([EB, b1 - b0, WIN]), ALU.mult))

    with nc.Block() as block:
        @block.sync
        def _(sp):
            for to, of in loads:
                sp.dma_start(to, of).then_inc(loaded, 16)
            for to, of in later_loads:
                sp.dma_start(to, of).then_inc(later_loaded, 16)
            sp.dma_start(g.x_rows[:, :, :], g.x.rearrange("(t p) d -> p t d", p=TR)).then_inc(g.x_loaded, 16)

        @block.vector
        def _(v):
            s = g.steps.on(v)
            v.wait_ge(loaded, 16 * len(loads))
            s.mark(v.tensor_copy(g.i10[:, :], i10f[0:EB, :]))
            s.mark(v.memset(g.zeros[:, :], 0.0))
            s.mark(v.memset(g.eps_col[:, :], EPS))
            s.mark(v.memset(g.key[:, :], -1.0))
            s.mark(v.memset(g.D_all[:, NB:NB + SLOTS, :, :], 0.0))
            s.mark(v.tensor_single_scalar(win_i[:, :], raw_i[:, 1, :], 5, ALU.logical_shift_right))
            s.then(v.tensor_single_scalar(rem_i[:, :], raw_i[:, 1, :], WIN - 1, ALU.bitwise_and))
            s.mark(v.scalar_tensor_tensor(out=keyrem[:, 0, :], in0=win_i[:, :], scalar=float(KEY),
                                          in1=raw_i[:, 0, :], op0=ALU.mult, op1=ALU.add))
            at.keyed = s.mark(v.tensor_copy(keyrem[:, 1, :], rem_i[:, :]))
            by_block = win_i[:, :].rearrange("q (h e) -> q h e", h=2)
            s.mark(v.tensor_reduce(extent[:, 0:2], by_block, X, ALU.min))
            s.then(v.tensor_reduce(extent[:, 2:4], by_block, X, ALU.max))
            for a in range(4):
                at.spread = s.mark(v.tensor_scalar(spread[:, a, :], g.ones[0:EQ, 0:NW], extent[:, a:a + 1], None,
                                                   ALU.mult))
            v.wait_ge(turned, 1)
            table = g.psum[0:EB, 0, 0:6 * EQ].rearrange("p (a h q) -> p a q h", a=3, h=2)
            s.mark(v.tensor_copy(halves(g.key[:, 0:NB]), table[:, 0]))
            s.mark(v.tensor_copy(halves(rem[:, :]), table[:, 1]))
            s.then(v.tensor_copy(halves(wcol[:, :]), table[:, 2]))
            s.then(v.tensor_copy(parts[:, :, 0], wcol[:, :]))
            s.then(v.tensor_tensor(wres[:, :], wcol[:, :], parts[:, :, 0], ALU.subtract))
            s.then(v.tensor_copy(parts[:, :, 1], wres[:, :]))
            s.then(v.tensor_tensor(wres2[:, :], wres[:, :], parts[:, :, 1], ALU.subtract))
            s.then(v.tensor_copy(parts[:, :, 2], wres2[:, :]))
            v.wait_ge(turned, 2)
            ext = g.psum[0:NW, 1, 0:2 * NB].rearrange("w (a b) -> w a b", a=2)
            s.then(v.tensor_scalar(meets1[:, :], ext[:, 0], g.rowno[0:NW, :], None, ALU.is_le))
            s.then(v.scalar_tensor_tensor(out=meets[:, :], in0=ext[:, 1], scalar=g.rowno[0:NW, :],
                                          in1=meets1[:, :], op0=ALU.is_ge, op1=ALU.mult))
            s.mark(v.scalar_tensor_tensor(out=pick[:, 0, :], in0=meets[:, :], scalar=-256.0,
                                          in1=g.blkno[0:NW, :], op0=ALU.mult, op1=ALU.add))
            s.then(v.tensor_tensor(pick[:, 1, :], meets[:, :], g.blkno[0:NW, :], ALU.mult))
            s.mark(v.tensor_reduce(ends[:, 0:1], pick[:, 0, :], X, ALU.min))
            s.then(v.tensor_reduce(ends[:, 1:2], pick[:, 1, :], X, ALU.max))
            s.mark(v.tensor_scalar(lohi[:, 0:1], ends[:, 0:1], 256.0, float(NB - 1), ALU.add, ALU.min))
            at.bounded = s.mark(v.tensor_scalar(lohi[:, 1:2], ends[:, 1:2], 1.0, None, ALU.add))
            d, shape = g.D_all[:, 0:NB, :, :], [EB, NB, WIN]
            s.then(v.tensor_tensor(d[:, :, 0, :], rem[:, :].unsqueeze(2).to_broadcast(shape),
                                   g.iota32[0:EB, :].unsqueeze(1).to_broadcast(shape), ALU.is_equal))
            v.sem_inc(one_hot, 1)
            weighted_rows(v, s.mark, 0, NB_V)
            v.wait_ge(turned, 3)
            s.mark(v.tensor_copy(g.bounds[:, :].rearrange("o (w a) -> o a w", a=2),
                                 g.psum[0:1, 2, 0:2 * NW].rearrange("o (a w) -> o a w", a=2)))
            v.wait_ge(turned, 4)
            s.mark(v.tensor_copy(g.vecs[:, :], g.psum[:, 3, 0:96]))
            s.mark(v.tensor_copy(g.b1cols[:, :], g.psum[:, 3, 128:256]))

        @block.gpsimd
        def _(q):
            q.wait_ge(one_hot, 1)
            weighted_rows(q, lambda ins: ins.then_inc(one_hot, 1), NB_V, NB)

        @block.tensor
        def _(t):
            t.wait_ge(loaded, 16 * len(loads))
            t.wait_ge(g.steps.semaphore, at.keyed)
            for a, of in enumerate([keyrem[:, 0, :], keyrem[:, 1, :], wraw[:, :]]):
                for h in range(2):
                    o = (2 * a + h) * EQ
                    ins = t.transpose(g.psum[0:EB, 0, o:o + EQ], of[:, h * EB:(h + 1) * EB],
                                      g.ident[0:EQ, 0:EQ])
            ins.then_inc(turned, 1)
            t.wait_ge(g.steps.semaphore, at.spread)
            for a in range(4):
                ins = t.matmul(g.psum[0:NW, 1, a * EQ:(a + 1) * EQ], spread[:, a, :], g.ident[0:EQ, 0:EQ],
                               start=True, stop=True)
            ins.then_inc(turned, 1)
            t.wait_ge(g.steps.semaphore, at.bounded)
            for a in range(2):
                ins = t.transpose(g.psum[0:1, 2, a * NW:(a + 1) * NW], lohi[:, a:a + 1],
                                  g.ident[0:NW, 0:NW])
            ins.then_inc(turned, 1)
            t.wait_ge(later_loaded, 16 * len(later_loads))
            t.transpose(g.psum[:, 3, 0:96], g.vecrows[0:96, :], g.ident[0:96, 0:96])
            t.transpose(g.psum[:, 3, 128:256], g.b1rows[:, :], g.ident[:, :]).then_inc(turned, 1)


def phase_adjacency(nc, sem, g):
    room = Room(nc, g.scratch_at)
    S = room("src_onehot", [EB, SLOTS, NC], BF16)
    rkey = room("rkey", [EB, GROUP, SLOTS], F32)
    S_more = room("src_onehot_more", [EB, NC], BF16)
    rkey_more = room("rkey_more", [EB, 1], F32)
    WP = room("weight_parts", [128, 2, NT, 3, WIN], F32)
    T = room("weight_sum", [128, NT, WIN], F32)
    PAIRS = SLOTS // 2

    keyed = sem("a_keyed")
    made = sem("a_made")
    used = sem("a_used")
    more_keyed = sem("a_more_keyed")
    more_made = sem("a_more_made")
    more_used = sem("a_more_used")
    summed = sem("a_summed")
    drained = sem("a_drained")
    copied = sem("a_copied")
    parts_free = sem("a_parts_free")
    added = sem("a_added")
    stat = sem("a_stat")

    def banks(par):
        return g.psum[:, 3 * par:3 * par + 3, :].rearrange("p a b -> p (a b)")[:, 0:NC]

    def group_bounds(eng, regs, i):
        eng.load(regs, g.bounds[0:1, bass.ds(i * (2 * GROUP), 2 * GROUP)])
        return [(eng.snap(regs[2 * j], min_val=0, max_val=NB - 1), eng.snap(regs[2 * j + 1], min_val=1, max_val=NB))
                for j in range(GROUP)]

    with nc.Block() as block:
        @block.vector
        def _(v):
            regs = [v.alloc_register(f"v_bound{i}") for i in range(2 * GROUP)]
            n = v.alloc_register("more_made_blocks")
            v.reg_mov(n, 1)
            v.wait_ge(g.x_loaded, 16)
            with v.Fori(0, NT) as i:
                bounds = group_bounds(v, regs, i)
                tile = bass.ds(i, 1)
                v.bn_stats(g.stats[:, tile, :], g.x_rows[:, tile, :]).then_inc(stat, 1)
                v.wait_ge(made, i * (GROUP * PAIRS))
                for par, (lo, hi) in enumerate(bounds):
                    v.tensor_scalar(rkey[:, par, :], g.key[:, bass.ds(lo, SLOTS)],
                                    g.w2k[0:EB, bass.ds(i * GROUP + par, 1)], None, ALU.subtract).then_inc(keyed, 1)
                for par, (lo, hi) in enumerate(bounds):
                    v.wait_ge(keyed, i * GROUP + par + 1)
                    for p in range(PAIRS):
                        v.wait_ge(used, i * (GROUP * PAIRS) + par * PAIRS + p + 1)
                        for u in (2 * p, 2 * p + 1):
                            ins = v.tensor_scalar(S[:, u, :], g.i10[:, :], rkey[:, par, u:u + 1], None, ALU.is_equal)
                        ins.then_inc(made, 1)
                    with v.Fori(lo + SLOTS, hi) as b:
                        v.wait_ge(more_used, v.snap(n))
                        v.tensor_scalar(rkey_more[:, :], g.key[:, bass.ds(b, 1)],
                                        g.w2k[0:EB, bass.ds(i * GROUP + par, 1)], None,
                                        ALU.subtract).then_inc(more_keyed, 1)
                        v.wait_ge(more_keyed, v.snap(n))
                        v.tensor_scalar(S_more[:, :], g.i10[:, :], rkey_more[:, :], None,
                                        ALU.is_equal).then_inc(more_made, 1)
                        v.reg_add(n, n, 1)

        @block.tensor
        def _(t):
            t.sem_inc(used, PAIRS)
            t.sem_inc(more_used, 1)
            t.sem_inc(drained, 2)
            regs = [t.alloc_register(f"t_bound{i}") for i in range(2 * GROUP)]
            n = t.alloc_register("more_used_blocks")
            t.reg_mov(n, 1)
            with t.Fori(0, NT) as i:
                for par, (lo, hi) in enumerate(group_bounds(t, regs, i)):
                    ps = banks(par % 2)
                    t.wait_ge(drained, i * GROUP + par + 1)
                    for p in range(PAIRS):
                        t.wait_ge(made, i * (GROUP * PAIRS) + par * PAIRS + p + 1)
                        for u in (2 * p, 2 * p + 1):
                            for c in range(NT):
                                ins = t.matmul(ps[:, c * 128:(c + 1) * 128], S[:, u, c * 128:(c + 1) * 128],
                                               g.D_flat[:, bass.ds((lo + u) * 128, 128)],
                                               start=u == 0 and c % 4 == 0, stop=False, skip_group_check=True)
                        ins.then_inc(used, 1)
                    with t.Fori(lo + SLOTS, hi) as b:
                        t.wait_ge(more_made, t.snap(n))
                        for c in range(NT):
                            ins = t.matmul(ps[:, c * 128:(c + 1) * 128], S_more[:, c * 128:(c + 1) * 128],
                                           g.D_flat[:, bass.ds(b * 128, 128)],
                                           start=False, stop=False, skip_group_check=True)
                        ins.then_inc(more_used, 1)
                        t.reg_add(n, n, 1)
                    t.matmul(ps[:, 0:128], g.zeros[0:EB, :], g.zeros[0:EB, :], start=False, stop=True,
                             skip_group_check=True).then_inc(summed, 1)

        @block.scalar
        def _(a):
            with a.Fori(0, NT) as tile:
                for j in range(GROUP):
                    w, par = tile * GROUP + j, j % 2
                    ps = banks(par).rearrange("p (c a w) -> p c a w", c=NT, a=4)
                    a.wait_ge(summed, w + 1)
                    a.wait_ge(parts_free, w + 1)
                    a.activation(WP[:, par], ps[:, :, 1:4, :], ACT.Copy).then_inc(copied, 1)
                    a.activation(g.A0T[:, :, bass.ds(w * WIN, WIN)], ps[:, :, 0, :],
                                 ACT.Copy).then_inc(drained, 1)

        @block.gpsimd
        def _(q):
            q.sem_inc(parts_free, 2)
            with q.Fori(0, NT) as tile:
                for j in range(GROUP):
                    w, par = tile * GROUP + j, j % 2
                    q.wait_ge(copied, w + 1)
                    q.wait_ge(parts_free, w + 2)
                    q.tensor_tensor(T[:, :, :], WP[:, par, :, 0, :], WP[:, par, :, 1, :],
                                    ALU.add).then_inc(added, 1)
                    q.wait_ge(added, w + 1)
                    q.tensor_tensor(g.A1T[:, :, bass.ds(w * WIN, WIN)], T[:, :, :], WP[:, par, :, 2, :],
                                    ALU.add).then_inc(parts_free, 1)


class NormSteps:
    LAG = 2

    def __init__(self, v, s, g, sems):
        self.v, self.s, self.g, self.sems = v, s, g, sems
        self.stat = {}

    def step(self, i):
        v, s, g = self.v, self.s, self.g
        if i < NT:
            self.stat[i] = s.mark(v.bn_stats(g.stats[:, i, :], g.x_rows[:, i, :]))
        if 0 <= i - 1 < NT:
            s.wait(self.stat[i - 1])
            v.bn_aggr(g.meanvar[:, i - 1, :], g.stats[:, i - 1, :]).then_inc(self.sems.var, 1)
        if 0 <= i - self.LAG < NT:
            t = i - self.LAG
            v.wait_ge(self.sems.dev, t + 1)
            v.reciprocal(g.rstd[:, t:t + 1], g.dev[:, t:t + 1]).then_inc(self.sems.inverse, 1)
            v.wait_ge(self.sems.inverse, t + 1)
            v.scalar_tensor_tensor(out=g.shift[:, t:t + 1], in0=g.meanvar[:, t, 0:1], scalar=-1.0,
                                   in1=g.rstd[:, t:t + 1], op0=ALU.mult, op1=ALU.mult).then_inc(self.sems.ready, 1)


def norm_sems(sem, name):
    n = Record()
    n.var = sem(name + "_var")
    n.dev = sem(name + "_dev")
    n.inverse = sem(name + "_inverse")
    n.ready = sem(name + "_ready")
    return n


def deviation(a, g, sems, t):
    a.wait_ge(sems.var, t + 1)
    a.activation(g.dev[:, t:t + 1], g.meanvar[:, t, 1:2], ACT.Sqrt, bias=g.eps_col[0:TR, :]).then_inc(sems.dev, 1)


def norm_rows(a, g, to, t):
    return a.activation(to[:, t, :], g.x_rows[:, t, :], ACT.Identity, bias=g.shift[:, t:t + 1],
                        scale=g.rstd[:, t:t + 1])


def cut_products(t, out, stat, mov, start, stop):
    t.matmul(out, stat[0], mov[0], start=start, stop=False)
    t.matmul(out, stat[0], mov[1], start=False, stop=False)
    return t.matmul(out, stat[1], mov[0], start=False, stop=stop)


def phase_gather0(nc, sem, g):
    RING = 2
    chunk = g.a0chunk
    cut = sem("g0_cut")
    used = sem("g0_used")
    summed = sem("g0_summed")
    hi_cut = sem("g0_hi")
    lo_cut = sem("g0_lo")
    r_hi = sem("g0_rhi")
    r_lo = sem("g0_rlo")
    residual = sem("g0_residual")
    scaled = sem("g0_scaled")
    var = sem("g0_var")
    dev = sem("g0_dev")
    shifted = sem("g0_shifted")
    normed = sem("g0_normed")
    order = [(b, k) for b in range(3) for k in range(NT)]

    with nc.Block() as block:
        @block.gpsimd
        def _(q):
            for t in range(NT):
                q.wait_ge(normed, t + 1)
                q.tensor_tensor(g.x_rows[:, t, :], g.x_rows[:, t, :], g.xn[:, t, :], ALU.add).then_inc(residual, 1)

        @block.scalar
        def _(a):
            def drain(b):
                lo, hi = BLOCKS[b]
                a.wait_ge(summed, b + 1)
                for d in range(KD):
                    a.activation(g.thi[:, d, lo:hi], g.psum[:, b % 2 * 4 + d, 0:hi - lo],
                                 ACT.Identity).then_inc(hi_cut, 1)

            a.wait_ge(var, NT)
            a.activation(g.dev[:, :], g.meanvar[:, :, 1], ACT.Sqrt, bias=g.eps_col[0:TR, :]).then_inc(dev, 1)
            a.wait_ge(shifted, 1)
            for i, (b, k) in enumerate(order):
                if k == 2 and b:
                    drain(b - 1)
                lo, hi = BLOCKS[b]
                if b == 0:
                    norm_rows(a, g, g.xn, k).then_inc(normed, 1)
                    a.wait_ge(normed, k + 1)
                    a.activation(g.rhi[:, k, :], g.xn[:, k, :], ACT.Identity).then_inc(r_hi, 1)
                if i >= RING:
                    a.wait_ge(used, i - RING + 1)
                a.activation(chunk[:, i % RING, 0:hi - lo], g.A0T[0:TR, k, lo:hi], ACT.Identity).then_inc(cut, 1)
            drain(2)

        @block.tensor
        def _(t):
            for i, (b, k) in enumerate(order):
                lo, hi = BLOCKS[b]
                if k == 0 and b == 2:
                    t.wait_ge(lo_cut, KD)
                if b == 0:
                    t.wait_ge(r_lo, k + 1)
                t.wait_ge(cut, i + 1)
                for d in range(KD):
                    ps = g.psum[:, b % 2 * 4 + d, 0:hi - lo]
                    t.matmul(ps, g.rhi[:, k, d * 128:(d + 1) * 128], chunk[:, i % RING, 0:hi - lo],
                             start=k == 0, stop=False)
                    ins = t.matmul(ps, g.rlo[:, k, d * 128:(d + 1) * 128], chunk[:, i % RING, 0:hi - lo],
                                   start=False, stop=False)
                ins.then_inc(used, 1)
                if k == NT - 1:
                    t.wait_ge(scaled, NT)
                    for tile, p0, p1 in pieces(lo, hi):
                        o = tile * TR + p0 - lo
                        for d in range(KD):
                            ins = t.matmul(g.psum[:, b % 2 * 4 + d, o:o + p1 - p0],
                                           g.xn[:, tile, d * 128:(d + 1) * 128], g.ident[0:TR, p0:p1],
                                           start=False, stop=tile * TR + p1 >= hi)
                    ins.then_inc(summed, 1)

        @block.vector
        def _(v):
            s = g.steps.on(v)
            s.mark(v.tensor_scalar(g.eps0[:, :], g.eps0[:, :], 1.0, None, ALU.add))
            for t in range(NT):
                v.bn_aggr(g.meanvar[:, t, :], g.stats[:, t, :]).then_inc(var, 1)
            v.wait_ge(dev, 1)
            s.then(v.reciprocal(g.rstd[:, :], g.dev[:, :]))
            v.scalar_tensor_tensor(out=g.shift[:, :], in0=g.meanvar[:, :, 0], scalar=-1.0, in1=g.rstd[:, :],
                                   op0=ALU.mult, op1=ALU.mult).then_inc(shifted, 1)
            for t in range(NT):
                v.wait_ge(r_hi, t + 1)
                v.tensor_tensor(g.rlo[:, t, :], g.xn[:, t, :], g.rhi[:, t, :].bitcast(F32),
                                ALU.subtract).then_inc(r_lo, 1)
            for t in range(NT):
                v.wait_ge(r_lo, t + 1)
                v.wait_ge(residual, t + 1)
                v.tensor_scalar(g.xn[:, t, :], g.xn[:, t, :], g.eps0[0:TR, :], None, ALU.mult).then_inc(scaled, 1)
            for b, (lo, hi) in enumerate(BLOCKS):
                for d in range(KD):
                    v.wait_ge(hi_cut, b * KD + d + 1)
                    v.tensor_tensor(g.tlo[:, d, lo:hi], g.psum[:, b % 2 * 4 + d, 0:hi - lo],
                                    g.thi[:, d, lo:hi].bitcast(F32), ALU.subtract).then_inc(lo_cut, 1)


def bn_scale_shift(v, s, g, var, dev, n, mean, var_ap, bias, gamma, beta, scale, shift, scratch):
    v.tensor_scalar(scratch[0], var_ap, EPS, None, ALU.add).then_inc(var, 1)
    s.then(v.tensor_tensor(scratch[1], mean, bias, ALU.add))
    s.then(v.tensor_tensor(scratch[1], bias, scratch[1], ALU.subtract))
    v.wait_ge(dev, n)
    s.then(v.reciprocal(scratch[3], scratch[2]))
    s.then(v.tensor_tensor(scale, scratch[3], gamma, ALU.mult))
    s.then(v.tensor_tensor(scratch[1], scratch[1], scale, ALU.mult))


def phase_mlp1(nc, sem, g):
    room = Room(nc, g.w1_at)
    raw = room("W1_raw", [128, 2, KD, 256], F32)
    whi = room("W1_hi", [128, 2, KD, 128], F32R)
    wlo = room("W1_lo", [128, 2, KD, 128], F32R)

    loaded = [sem("m1_loaded0"), sem("m1_loaded1")]
    hi_cut = sem("m1_hi")
    lo_cut = sem("m1_lo")
    summed = sem("m1_summed")
    var = sem("m1_var")
    dev = sem("m1_dev")
    scaled = sem("m1_scaled")
    drained = sem("m1_drained")
    bn = g.bn

    with nc.Block() as block:
        @block.sync
        def _(sp):
            for p in range(KH0 // 2):
                if p >= 2:
                    sp.wait_ge(lo_cut, 2 * (p - 1))
                sp.dma_start(raw[:, p % 2], g.gnn0_W1.rearrange("(k p) h -> p k h", p=128)[
                    :, :, p * 256:(p + 1) * 256]).then_inc(loaded[p % 2], 16)
            sp.dma_start(g.W2_raw[:, :, :], g.gnn0_W2.rearrange("(k p) d -> p k d", p=128)).then_inc(
                g.W2_loaded, 16)

        @block.vector
        def _(v):
            s = g.steps.on(v)

            def cut(m):
                p = m // 2
                v.wait_ge(loaded[p % 2], 16 * (p // 2 + 1))
                if m >= 2:
                    v.wait_ge(summed, m - 1)
                of = raw[:, p % 2, :, m % 2 * 128:(m % 2 + 1) * 128]
                v.tensor_copy(whi[:, m % 2], of).then_inc(hi_cut, 1)
                v.wait_ge(hi_cut, m + 1)
                v.tensor_tensor(wlo[:, m % 2], of, whi[:, m % 2].bitcast(F32), ALU.subtract).then_inc(lo_cut, 1)

            cut(0)
            cut(1)
            for m in range(KH0):
                v.wait_ge(summed, m + 1)
                for b, (lo, hi) in enumerate(BLOCKS):
                    s.mark(v.bn_stats(bn.stats[:, b, :], g.psum[:, m % 2 * 3 + b, 0:hi - lo]))
                s.wait()
                s.then(v.bn_aggr(bn.mv[:, :], bn.stats[:, 0:3, :]))
                c = slice(m, m + 1)
                bn_scale_shift(v, s, g, var, dev, m + 1, bn.mv[:, 0:1], bn.mv[:, 1:2], g.b1v[:, c], g.g1v[:, c],
                               g.be1v[:, c], bn.scale[:, c], None,
                               [bn.a[:, c], bn.b[:, c], bn.c[:, c], bn.d[:, c]])
                v.tensor_tensor(bn.shift[:, c], bn.b[:, c], g.be1v[:, c], ALU.add).then_inc(scaled, 1)
                if m + 2 < KH0:
                    cut(m + 2)

        @block.scalar
        def _(a):
            for m in range(KH0):
                a.wait_ge(var, m + 1)
                a.activation(bn.c[:, m:m + 1], bn.a[:, m:m + 1], ACT.Sqrt).then_inc(dev, 1)
                a.wait_ge(scaled, m + 1)
                for b, (lo, hi) in enumerate(BLOCKS):
                    a.activation(g.h1[:, m, lo:hi], g.psum[:, m % 2 * 3 + b, 0:hi - lo], ACT.Relu,
                                 bias=bn.shift[:, m:m + 1], scale=bn.scale[:, m:m + 1]).then_inc(drained, 1)

        @block.tensor
        def _(t):
            for m in range(KH0):
                t.wait_ge(lo_cut, m + 1)
                if m >= 2:
                    t.wait_ge(drained, 3 * (m - 1))
                for b, (lo, hi) in enumerate(BLOCKS):
                    for k in range(KD):
                        ins = cut_products(t, g.psum[:, m % 2 * 3 + b, 0:hi - lo],
                                           (whi[:, m % 2, k, :], wlo[:, m % 2, k, :]),
                                           (g.thi[:, k, lo:hi], g.tlo[:, k, lo:hi]), k == 0, k == KD - 1)
                ins.then_inc(summed, 1)


def phase_mlp2(nc, sem, g):
    RING = 3
    room = Room(nc, g.w2_cut_at)
    whi = room("W2_hi", [128, KH0, D], F32R)
    wlo = room("W2_lo", [128, KH0, D], F32R)
    hhi = room("h1_hi", [128, RING, BW], F32R)
    hlo = room("h1_lo", [128, RING, BW], F32R)

    w_hi = sem("m2_whi")
    w_lo = sem("m2_wlo")
    hi_cut = sem("m2_hi")
    lo_cut = sem("m2_lo")
    used = sem("m2_used")
    summed = sem("m2_summed")
    drained = sem("m2_drained")
    var = sem("m2_var")
    dev = sem("m2_dev")
    scaled = sem("m2_scaled")
    done = sem("m2_done")
    order = [(b, k) for b in range(3) for k in range(KH0)]
    bn = g.bn

    with nc.Block() as block:
        @block.scalar
        def _(a):
            def drain(b):
                lo, hi = BLOCKS[b]
                a.wait_ge(summed, b + 1)
                for d in range(KD):
                    a.activation(g.yT[:, d, lo:hi], g.psum[:, b % 2 * 4 + d, 0:hi - lo],
                                 ACT.Copy).then_inc(drained, 1)

            for i, (b, k) in enumerate(order):
                if k == 2 and b:
                    drain(b - 1)
                lo, hi = BLOCKS[b]
                if i >= RING:
                    a.wait_ge(used, i - RING + 1)
                a.activation(hhi[:, i % RING, 0:hi - lo], g.h1[:, k, lo:hi], ACT.Copy).then_inc(hi_cut, 1)
            drain(2)
            a.wait_ge(var, 1)
            a.activation(bn.c[:, 0:KD], bn.a[:, 0:KD], ACT.Sqrt).then_inc(dev, 1)
            a.wait_ge(scaled, 1)
            for d in range(KD // 2):
                a.activation(g.yT[:, d, :], g.yT[:, d, :], ACT.Relu, bias=bn.shift[:, d:d + 1],
                             scale=bn.scale[:, d:d + 1]).then_inc(done, 1)

        @block.vector
        def _(v):
            s = g.steps.on(v)
            v.wait_ge(g.W2_loaded, 16)
            for i, (b, k) in enumerate(order):
                lo, hi = BLOCKS[b]
                if b == 0:
                    v.tensor_copy(whi[:, k, :], g.W2_raw[:, k, :]).then_inc(w_hi, 1)
                    v.wait_ge(w_hi, k + 1)
                    v.tensor_tensor(wlo[:, k, :], g.W2_raw[:, k, :], whi[:, k, :].bitcast(F32),
                                    ALU.subtract).then_inc(w_lo, 1)
                v.wait_ge(hi_cut, i + 1)
                if i >= RING:
                    v.wait_ge(used, i - RING + 1)
                v.tensor_tensor(hlo[:, i % RING, 0:hi - lo], g.h1[:, k, lo:hi],
                                hhi[:, i % RING, 0:hi - lo].bitcast(F32), ALU.subtract).then_inc(lo_cut, 1)
            for b, (lo, hi) in enumerate(BLOCKS):
                for d in range(KD):
                    v.wait_ge(drained, KD * b + d + 1)
                    s.mark(v.bn_stats(bn.stats[:, d * 3 + b, :], g.yT[:, d, lo:hi]))
            s.wait()
            for d in range(KD):
                s.mark(v.bn_aggr(bn.mv4[:, d, :], bn.stats[:, 3 * d:3 * d + 3, :]))
            s.wait()
            bn_scale_shift(v, s, g, var, dev, 1, bn.mv4[:, :, 0], bn.mv4[:, :, 1], g.b2v[:, :], g.g2v[:, :],
                           g.be2v[:, :], bn.scale[:, 0:KD], None,
                           [bn.a[:, 0:KD], bn.b[:, 0:KD], bn.c[:, 0:KD], bn.d[:, 0:KD]])
            v.tensor_tensor(bn.shift[:, 0:KD], bn.b[:, 0:KD], g.be2v[:, :], ALU.add).then_inc(scaled, 1)
            v.wait_ge(scaled, 1)
            for d in range(KD // 2, KD):
                s.mark(v.tensor_scalar(g.yT[:, d, :], g.yT[:, d, :], bn.scale[:, d:d + 1], bn.shift[:, d:d + 1],
                                       ALU.mult, ALU.add))
            for d in range(KD // 2, KD):
                s.wait(s.n - (KD // 2 - 1))
                s.mark(v.tensor_scalar(g.yT[:, d, :], g.yT[:, d, :], 0.0, None, ALU.max))

        @block.tensor
        def _(t):
            for i, (b, k) in enumerate(order):
                lo, hi = BLOCKS[b]
                if b == 0:
                    t.wait_ge(w_lo, k + 1)
                if b == 2 and k == 0:
                    t.wait_ge(drained, KD)
                t.wait_ge(lo_cut, i + 1)
                for d in range(KD):
                    f = slice(d * 128, (d + 1) * 128)
                    ins = cut_products(t, g.psum[:, b % 2 * 4 + d, 0:hi - lo], (whi[:, k, f], wlo[:, k, f]),
                                       (hhi[:, i % RING, 0:hi - lo], hlo[:, i % RING, 0:hi - lo]),
                                       k == 0, k == KH0 - 1)
                ins.then_inc(used, 1)
                if k == KH0 - 1:
                    t.matmul(g.psum[:, b % 2 * 4 + 3, 0:2], g.zeros[:, :], g.zeros[:, 0:2], start=False,
                             stop=True, skip_group_check=True).then_inc(summed, 1)


def add_norm_turn(nc, sem, g, name, produce, rows, thi, tlo, loads=()):
    LAG = 3
    produced = sem(name + "_produced")
    added = sem(name + "_added")
    stats = norm_sems(sem, name)
    normed = sem(name + "_normed")
    turned = sem(name + "_turned")
    hi_cut = sem(name + "_hi")
    lo_cut = sem(name + "_lo")

    def cols(i):
        return g.psum[:, 4 + i % 4, 0:KD * TR].rearrange("p (k c) -> p k c", k=KD)

    def lo_part(v, i):
        v.wait_ge(hi_cut, i + 1)
        v.tensor_tensor(tlo[:, :, i * TR:(i + 1) * TR], cols(i),
                        thi[:, :, i * TR:(i + 1) * TR].bitcast(F32), ALU.subtract).then_inc(lo_cut, 1)

    with nc.Block() as block:
        @block.sync
        def _(sp):
            for to, of, semaphore in loads:
                sp.dma_start(to, of).then_inc(semaphore, 16)

        @block.vector
        def _(v):
            s = g.steps.on(v)
            norm = NormSteps(v, s, g, stats)
            for i in range(NT + LAG + 1):
                if i < NT:
                    v.wait_ge(produced, i + 1)
                    v.tensor_tensor(g.x_rows[:, i, :], g.x_rows[:, i, :], g.psum[0:TR, i % 4, :],
                                    ALU.add).then_inc(added, 1)
                    v.wait_ge(added, i + 1)
                norm.step(i)
                if i > LAG:
                    lo_part(v, i - LAG - 1)

        @block.scalar
        def _(a):
            for i in range(NT + 3):
                j = i - 2
                if 0 <= j < NT:
                    a.wait_ge(stats.ready, j + 1)
                    norm_rows(a, g, rows, j).then_inc(normed, 1)
                j = i - 3
                if 0 <= j < NT:
                    a.wait_ge(turned, j + 1)
                    a.activation(thi[:, :, j * TR:(j + 1) * TR], cols(j), ACT.Copy).then_inc(hi_cut, 1)
                if i < NT:
                    deviation(a, g, stats, i)

        @block.tensor
        def _(t):
            for i in range(NT + LAG):
                if i < NT:
                    if i >= 4:
                        t.wait_ge(added, i - 3)
                    produce(t, i, g.psum[0:TR, i % 4, :]).then_inc(produced, 1)
                j = i - LAG
                if j >= 0:
                    t.wait_ge(normed, j + 1)
                    if j >= 4:
                        t.wait_ge(lo_cut, j - 3)
                    for k in range(KD):
                        ins = t.transpose(g.psum[:, 4 + j % 4, k * TR:(k + 1) * TR],
                                          rows[:, j, k * 128:(k + 1) * 128], g.ident[0:TR, 0:TR])
                    ins.then_inc(turned, 1)


def turn_y(g):
    def produce(t, i, out):
        for d in range(KD):
            ins = t.transpose(out[:, d * 128:(d + 1) * 128], g.yT[:, d, i * TR:(i + 1) * TR], g.ident[:, :])
        return ins
    return produce


def project(g):
    def produce(t, i, out):
        c = slice(i * TR, (i + 1) * TR)
        for k in range(KD):
            ins = cut_products(t, out, (g.gthi[:, k, c], g.gtlo[:, k, c]),
                               (g.WThi[:, k, :], g.WTlo[:, k, :]), k == 0, k == KD - 1)
        return ins
    return produce


def phase_route(nc, sem, g):
    room = Room(nc, g.route_at)
    gT = room("gates_T", [NE, N], F32)
    P16 = room("plan_sixteen_times", [TR, NT, NE, 16], F32)
    above_c = room("above_candidate", [128, N], F32)
    assert room.next <= g.route_end
    room = Room(nc, g.route_at2)
    ghi = room("gate_hi", [128, KD, 128], F32R)
    glo = room("gate_lo", [128, KD, 128], F32R)
    zero_rows = room("zero_rows", [128, D], F32)
    plan = room("plan", [TR, NT, NE], F32)
    above, equal, rank, chosen, active = (room(name, [TR, NE, NT], F32) for name in (
        "above", "equal", "rank", "chosen", "active"))
    small = Room(nc, g.route_small)
    colsum = small("colsum", [TR, NE], F32)
    rcol = small("rcol", [TR, NE], F32)
    rowsum = small("rowsum", [TR, NT], F32)
    rrow = small("rrow", [TR, NT], F32)
    bits = small("threshold_bits", [128, 1], I32)
    cand = small("candidate_bits", [128, 1], I32)
    count = small("count", [128, 1], F32)
    enough = small("enough", [128, 1], F32)
    digit = small("digit_bits", [128, 1], I32)
    diag = small("threshold_diag", [128, NE], F32)
    need = small("need", [TR, NE], F32)
    place = small("place", [TR, NT], F32)
    is_out = small("is_out", [TR, NT], F32)

    at = Record()
    gated = sem("r_gated")
    copied = sem("r_copied")
    turned = sem("r_turned")
    to_sum = sem("r_to_sum")
    cols_summed = sem("r_cols_summed")
    plan_turned = sem("r_plan_turned")
    to_count = sem("r_to_count")
    counted = sem("r_counted")
    back = sem("r_back")
    zeroed = sem("r_zeroed")
    w_hi = sem("r_w_hi")
    w_lo = sem("r_w_lo")
    V = g.psum[:, 0:5, 0:2 * TR]
    by_expert = plan[:, :, :].rearrange("p t e -> p e t")

    def flat(ap):
        return ap.rearrange("p e t -> p (e t)")

    with nc.Block() as block:
        @block.vector
        def _(v):
            s = g.steps.on(v)
            s.mark(v.memset(ghi[:, :, :].bitcast(F32), 0.0))
            s.mark(v.memset(glo[:, :, :].bitcast(F32), 0.0))
            s.then(v.memset(bits[:, :], 0))
            s.then(v.tensor_copy(ghi[:, :, 0:NE], g.gate[:, :, :]))
            at.cut = s.mark(v.tensor_tensor(glo[:, :, 0:NE], g.gate[:, :, :], ghi[:, :, 0:NE].bitcast(F32),
                                            ALU.subtract))
            v.wait_ge(turned, 1)
            s.then(v.tensor_scalar(plan[:, :, :], g.psum[0:TR, 5, 0:NT * NE].rearrange("p (t e) -> p t e", t=NT),
                                   FLOOR, None, ALU.max))
            for i in range(SINKHORN):
                v.tensor_reduce(colsum[:, :], by_expert, X, ALU.add).then_inc(to_sum, 1)
                v.wait_ge(cols_summed, i + 1)
                s.then(v.reciprocal(rcol[:, :], g.psum[0:TR, 6, 0:NE]))
                s.then(v.tensor_tensor(plan[:, :, :], plan[:, :, :], rcol[:, :].unsqueeze(1).to_broadcast([TR, NT, NE]),
                                       ALU.mult))
                s.then(v.tensor_reduce(rowsum[:, :], plan[:, :, :], X, ALU.add))
                s.then(v.reciprocal(rrow[:, :], rowsum[:, :]))
                s.then(v.tensor_tensor(plan[:, :, :], plan[:, :, :], rrow[:, :].unsqueeze(2).to_broadcast([TR, NT, NE]),
                                       ALU.mult))
            at.planned = s.mark(v.tensor_copy(P16[:, :, :, :], plan[:, :, :].unsqueeze(3).to_broadcast(
                [TR, NT, NE, 16])))
            v.wait_ge(plan_turned, 1)
            for r, shift in enumerate(SHIFTS):
                s.then(v.tensor_tensor(cand[:, :], bits[:, :], g.kshift[:, r:r + 1], ALU.bitwise_or))
                s.then(v.tensor_scalar(above_c[:, :].rearrange("p (b c) -> p b c", b=5), V, cand[:, :].bitcast(F32),
                                       0.0, ALU.is_ge, ALU.add, accum_out=count[:, :]))
                v.tensor_scalar(enough[:, :], count[:, :], float(TOP), float(2**shift), ALU.is_ge,
                                ALU.mult).then_inc(to_count, 1)
                v.wait_ge(counted, r + 1)
                s.then(v.tensor_copy(digit[:, :], g.psum[:, 6, 16:17]))
                s.then(v.tensor_tensor(bits[:, :], bits[:, :], digit[:, :], ALU.bitwise_or))
            at.threshold = s.mark(v.tensor_scalar(diag[:, :], g.first16[:, :], bits[:, :].bitcast(F32), None, ALU.mult))
            v.wait_ge(back, 1)
            least = g.psum[0:TR, 7, 0:NE].unsqueeze(2).to_broadcast([TR, NE, NT])
            s.mark(v.tensor_tensor(above[:, :, :], by_expert, least, ALU.is_gt))
            at.compared = s.mark(v.tensor_tensor(equal[:, :, :], by_expert, least, ALU.is_equal))
            v.wait_ge(back, 2)
            s.mark(v.tensor_reduce(need[:, :], g.psum[0:TR, 7, 0:NE * NT].rearrange("p (e t) -> p e t", e=NE),
                                   X, ALU.add))

            def running():
                s.then(v.tensor_tensor_scan(flat(rank[:, :, :]), g.not_first_tile[0:TR, :],
                                            g.psum[0:TR, 6, 0:NE * NT], 0.0, ALU.mult, ALU.add))
                s.then(v.tensor_tensor(flat(rank[:, :, :]), flat(rank[:, :, :]), g.psum[0:TR, 6, 0:NE * NT],
                                       ALU.subtract))
                s.then(v.tensor_tensor(flat(rank[:, :, :]), flat(rank[:, :, :]), g.psum[0:TR, 5, 0:NE * NT],
                                       ALU.add))

            running()
            s.then(v.tensor_scalar(need[:, :], need[:, :], -1.0, float(TOP), ALU.mult, ALU.add))
            s.then(v.tensor_tensor(rank[:, :, :], rank[:, :, :], need[:, :].unsqueeze(2).to_broadcast([TR, NE, NT]),
                                   ALU.is_le))
            s.then(v.tensor_tensor(rank[:, :, :], rank[:, :, :], equal[:, :, :], ALU.mult))
            s.then(v.tensor_tensor(chosen[:, :, :], above[:, :, :], rank[:, :, :], ALU.add))
            at.active = s.mark(v.scalar_tensor_tensor(out=active[:, :, :], in0=by_expert, scalar=0.5,
                                                      in1=chosen[:, :, :], op0=ALU.is_gt, op1=ALU.mult))
            s.then(v.tensor_reduce(is_out[:, :], chosen[:, :, :].rearrange("p e t -> p t e"), X, ALU.add))
            s.then(v.tensor_scalar(is_out[:, :], is_out[:, :], 1.0, None, ALU.add))
            s.then(v.reciprocal(is_out[:, :], is_out[:, :]))
            v.wait_ge(back, 3)
            running()
            s.then(v.tensor_tensor(rank[:, :, :], rank[:, :, :],
                                   g.place0[0:TR, :].unsqueeze(2).to_broadcast([TR, NE, NT]), ALU.add))
            s.then(v.tensor_tensor(rank[:, :, :], rank[:, :, :], active[:, :, :], ALU.mult))
            s.then(v.tensor_reduce(place[:, :], rank[:, :, :].rearrange("p e t -> p t e"), X, ALU.max))
            s.then(v.scalar_tensor_tensor(out=g.share[:, :], in0=place[:, :], scalar=1.0, in1=is_out[:, :],
                                          op0=ALU.min, op1=ALU.mult))
            s.mark(v.tensor_scalar(g.place_from[:, :], place[:, :], -1.0, 0.0, ALU.add, ALU.max))
            s.then(v.tensor_scalar(is_out[:, :], place[:, :], 1.0, g.far[0:TR, :], ALU.is_lt, ALU.mult))
            s.then(v.scalar_tensor_tensor(out=g.place_to[:, :], in0=place[:, :], scalar=-1.0, in1=is_out[:, :],
                                          op0=ALU.add, op1=ALU.add))

        @block.tensor
        def _(t):
            t.wait_ge(g.steps.semaphore, at.cut)
            for b, (lo, hi) in enumerate(BLOCKS):
                for k in range(KD):
                    ins = cut_products(t, g.psum[:, b, 0:hi - lo], (ghi[:, k, :], glo[:, k, :]),
                                       (g.cthi[:, k, lo:hi], g.ctlo[:, k, lo:hi]), k == 0, k == KD - 1)
                ins.then_inc(gated, 1)
            done = 0
            for b, (lo, hi) in enumerate(BLOCKS):
                t.wait_ge(copied, b + 1)
                while done < NT and (done + 1) * TR <= hi:
                    ins = t.transpose(g.psum[0:TR, 5, done * NE:(done + 1) * NE], gT[:, done * TR:(done + 1) * TR],
                                      g.ident[0:NE, 0:NE])
                    done += 1
            ins.then_inc(turned, 1)
            for i in range(SINKHORN):
                t.wait_ge(to_sum, i + 1)
                t.matmul(g.psum[0:TR, 6, 0:NE], g.ones[0:TR, 0:TR], colsum[:, :], start=True,
                         stop=True).then_inc(cols_summed, 1)
            t.wait_ge(g.steps.semaphore, at.planned)
            for i in range(NT):
                ins = t.transpose(g.psum[:, i // 2, i % 2 * TR:(i % 2 + 1) * TR],
                                  P16[:, i, :, :].rearrange("p e c -> p (e c)"), g.ident[0:TR, 0:TR])
            ins.then_inc(plan_turned, 1)
            for r in range(len(SHIFTS)):
                t.wait_ge(to_count, r + 1)
                t.matmul(g.psum[:, 6, 16:17], g.blk16[:, :], enough[:, :], start=True, stop=True).then_inc(counted, 1)

            def over_tokens(bank, weights, of):
                return t.matmul(g.psum[0:TR, bank, 0:NE * NT], weights[0:TR, 0:TR], flat(of[:, :, :]), start=True,
                                stop=True)

            t.wait_ge(g.steps.semaphore, at.threshold)
            t.matmul(g.psum[0:TR, 7, 0:NE], g.ones[:, 0:TR], diag[:, :], start=True, stop=True).then_inc(back, 1)
            t.wait_ge(g.steps.semaphore, at.compared)
            over_tokens(7, g.ones, above)
            over_tokens(6, g.ones, equal)
            over_tokens(5, g.upto, equal).then_inc(back, 1)
            t.wait_ge(g.steps.semaphore, at.active)
            over_tokens(6, g.ones, active)
            over_tokens(5, g.upto, active).then_inc(back, 1)

        @block.scalar
        def _(a):
            for b, (lo, hi) in enumerate(BLOCKS):
                a.wait_ge(gated, b + 1)
                a.activation(gT[:, lo:hi], g.psum[0:NE, b, 0:hi - lo], ACT.Copy).then_inc(copied, 1)

        @block.gpsimd
        def _(q):
            q.memset(zero_rows[:, :], 0.0).then_inc(zeroed, 1)
            q.wait_ge(g.w_loaded[0], 16)
            q.tensor_copy(g.ewhi0[:, :, :], g.eraw[:, 0]).then_inc(w_hi, 1)
            q.wait_ge(w_hi, 1)
            q.tensor_tensor(g.ewlo0[:, :, :], g.eraw[:, 0], g.ewhi0[:, :, :].bitcast(F32),
                            ALU.subtract).then_inc(w_lo, 1)

        @block.sync
        def _(sp):
            for e in range(2):
                sp.dma_start(g.eraw[:, e], g.experts[e].rearrange("(k p) d -> p k d", p=128)).then_inc(
                    g.w_loaded[e], 16)
            sp.wait_ge(zeroed, 1)
            sp.dma_start(g.placed_d.rearrange("(t p) d -> p t d", p=128),
                         zero_rows[:, :].unsqueeze(1).to_broadcast([128, NG, D])).then_inc(g.placed_zero, 16)
            sp.wait_ge(w_lo, 1)
            sp.dma_start(g.eraw[:, 0], g.experts[2].rearrange("(k p) d -> p k d", p=128)).then_inc(
                g.w_loaded[0], 16)


class Gather1:
    RING = 3

    def __init__(self, sem, g):
        self.g = g
        self.hi_cut = sem("g1_hi")
        self.lo_cut = sem("g1_lo")
        self.used = sem("g1_used")
        self.summed = sem("g1_summed")
        self.t_hi = sem("g1_thi")
        self.t_lo = sem("g1_tlo")
        self.order = [(b, k) for b in range(3) for k in range(NT)]

    def scalar_chunk(self, a, i):
        g, (b, k) = self.g, self.order[i]
        lo, hi = BLOCKS[b]
        if i >= self.RING:
            a.wait_ge(self.used, i - self.RING + 1)
        a.activation(g.a1hi[:, i % self.RING, 0:hi - lo], g.A1T[0:TR, k, lo:hi], ACT.Copy).then_inc(self.hi_cut, 1)

    def scalar_drain(self, a, b):
        g, (lo, hi) = self.g, BLOCKS[b]
        a.wait_ge(self.summed, b + 1)
        for d in range(KD):
            a.activation(g.gthi[:, d, lo:hi], g.psum[:, b % 2 * 4 + d, 0:hi - lo], ACT.Copy).then_inc(self.t_hi, 1)

    def scalar_rest(self, a):
        for i in range(NT, 3 * NT):
            if i % NT == 2:
                self.scalar_drain(a, i // NT - 1)
            self.scalar_chunk(a, i)
        self.scalar_drain(a, 2)

    def vector_chunk(self, v, i):
        g, (b, k) = self.g, self.order[i]
        lo, hi = BLOCKS[b]
        v.wait_ge(self.hi_cut, i + 1)
        v.tensor_tensor(g.a1lo[:, i % self.RING, 0:hi - lo], g.A1T[0:TR, k, lo:hi],
                        g.a1hi[:, i % self.RING, 0:hi - lo].bitcast(F32), ALU.subtract).then_inc(self.lo_cut, 1)

    def vector_drain(self, v, b):
        g, (lo, hi) = self.g, BLOCKS[b]
        for d in range(KD):
            v.wait_ge(self.t_hi, b * KD + d + 1)
            v.tensor_tensor(g.gtlo[:, d, lo:hi], g.psum[:, b % 2 * 4 + d, 0:hi - lo],
                            g.gthi[:, d, lo:hi].bitcast(F32), ALU.subtract).then_inc(self.t_lo, 1)

    def vector_rest(self, v):
        for i in range(NT, 3 * NT):
            if i % NT == 3:
                self.vector_drain(v, i // NT - 1)
            self.vector_chunk(v, i)
        self.vector_drain(v, 2)

    def tensor(self, t, rows_cut):
        g = self.g
        for i, (b, k) in enumerate(self.order):
            lo, hi = BLOCKS[b]
            if b == 0:
                t.wait_ge(rows_cut, k + 1)
            if k == 0 and b == 2:
                t.wait_ge(self.t_lo, KD)
            t.wait_ge(self.lo_cut, i + 1)
            for d in range(KD):
                f = slice(d * 128, (d + 1) * 128)
                ins = cut_products(t, g.psum[:, b % 2 * 4 + d, 0:hi - lo], (g.r1hi[:, k, f], g.r1lo[:, k, f]),
                                   (g.a1hi[:, i % self.RING, 0:hi - lo], g.a1lo[:, i % self.RING, 0:hi - lo]),
                                   k == 0, k == NT - 1)
            ins.then_inc(self.used, 1)
            if k == NT - 1:
                t.matmul(g.psum[:, b % 2 * 4 + 3, 0:2], g.zeros[:, :], g.zeros[:, 0:2], start=False,
                         stop=True, skip_group_check=True).then_inc(self.summed, 1)


def turn_groups():
    return [(t, c, min(4, NT - c)) for t in range(NT) for c in range(t, NT, 4)]


def turn_tensor(t, g, turned, moved):
    A = g.A1T
    for i, (r, c0, n) in enumerate(turn_groups()):
        if i >= 4:
            t.wait_ge(moved, 2 * (i - 3))
        for j in range(n):
            t.transpose(g.psum[0:TR, i % 4 * 2, j * TR:(j + 1) * TR],
                        A[0:TR, c0 + j, r * TR:(r + 1) * TR], g.ident[0:TR, 0:TR])
            ins = t.transpose(g.psum[0:TR, i % 4 * 2 + 1, j * TR:(j + 1) * TR],
                              A[0:TR, r, (c0 + j) * TR:(c0 + j + 1) * TR], g.ident[0:TR, 0:TR])
        ins.then_inc(turned, 1)


def turn_scalar(a, g, turned, moved):
    A = g.A1T
    for i, (r, c0, n) in enumerate(turn_groups()):
        a.wait_ge(turned, i + 1)
        a.activation(A[0:TR, r, c0 * TR:(c0 + n) * TR], g.psum[0:TR, i % 4 * 2, 0:n * TR],
                     ACT.Copy).then_inc(moved, 1)
        a.wait_ge(moved, 2 * i + 1)
        a.activation(A[0:TR, c0:c0 + n, r * TR:(r + 1) * TR],
                     g.psum[0:TR, i % 4 * 2 + 1, 0:n * TR].rearrange("p (c w) -> p c w", c=n),
                     ACT.Copy).then_inc(moved, 1)


def phase_experts(nc, sem, g):
    sent = sem("x_sent")
    turned_a = sem("x_turned_a")
    moved_a = sem("x_moved_a")
    turned = sem("x_turned")
    x_hi = sem("x_hi")
    x_lo = sem("x_lo")
    w_hi = sem("x_whi")
    w_lo = sem("x_wlo")
    summed = sem("x_summed")
    copied = sem("x_copied")
    stored = [sem("x_stored0"), sem("x_stored1"), sem("x_stored2"), sem("x_stored3")]
    fetched = [sem(f"x_fetched{i}") for i in range(NT // 2)]
    back = [sem(f"x_back{i}") for i in range(NG // 2)]

    added = sem("x_added")
    stats = norm_sems(sem, "x")
    normed = sem("x_normed")
    r_hi = sem("x_rhi")
    r_lo = sem("x_rlo")
    w2_in = sem("x_w")
    wt = sem("x_wt")
    wt_hi = sem("x_wt_hi")
    wt_lo = sem("x_wt_lo")

    gather = Gather1(sem, g)

    def cut_buffers(e):
        return (g.ewhi0, g.ewlo0) if e % 2 == 0 else (g.ewhi1, g.ewlo1)

    with nc.Block() as block:
        @block.gpsimd
        def _(q):
            q.wait_ge(g.placed_zero, 16)
            for t in range(NT):
                q.indirect_dma_start(g.placed_d[:, :], bass.IndirectOffsetOnAxis(ap=g.place_to[:, t:t + 1], axis=0),
                                     g.c_rows[:, t, :], None, bounds_check=NP - 1, oob_is_err=False
                                     ).then_inc(sent, 16)
            for i in range(4):
                q.wait_ge(stored[i], 16 * 4)
            q.wait_ge(x_lo, NG)
            for t in range(NT):
                q.indirect_dma_start(g.fetched_rows[:, t, :], None, g.results_d[:, :],
                                     bass.IndirectOffsetOnAxis(ap=g.place_from[:, t:t + 1], axis=0),
                                     bounds_check=NP - 1, oob_is_err=False).then_inc(fetched[t // 2], 16)

        @block.sync
        def _(sp):
            sp.wait_ge(sent, 16 * NT)
            for i in range(NG // 2):
                sp.dma_start(g.g_rows[:, 2 * i:2 * i + 2, :],
                             g.placed_d[i * 256:(i + 1) * 256, :].rearrange("(t p) d -> p t d", p=128)
                             ).then_inc(back[i], 16)
            sp.wait_ge(x_lo, NG)
            sp.dma_start(g.W_rows[:, :, :], g.gnn1_weight.rearrange("(o p) d -> p o d", p=128)).then_inc(w2_in, 16)
            for c in range(2 * NE):
                if c % 2 == 0 and c // 2 + 3 < NE:
                    e = c // 2 + 3
                    sp.wait_ge(w_lo, e - 2)
                    sp.dma_start(g.eraw[:, e % 2], g.experts[e].rearrange("(k p) d -> p k d", p=128)).then_inc(
                        g.w_loaded[e % 2], 16)
                sp.wait_ge(copied, c + 1)
                sp.dma_start(g.results_d[c * CH:(c + 1) * CH, :], g.y_rows[:, c % 4, :]).then_inc(stored[c % 4], 16)

        @block.scalar
        def _(a):
            def cut_w(e):
                a.wait_ge(g.w_loaded[e % 2], 16 * (e // 2 + 1))
                if e >= 2:
                    a.wait_ge(summed, 2 * (e - 1))
                else:
                    a.wait_ge(sent, 16 * NT)
                a.activation(cut_buffers(e)[0][:, :, :], g.eraw[:, e % 2], ACT.Copy).then_inc(w_hi, 1)

            turn_scalar(a, g, turned_a, moved_a)
            cut_w(1)
            for i in range(NG):
                a.wait_ge(turned, i + 1)
                a.activation(g.gxhi[:, :, i * 128:(i + 1) * 128],
                             g.psum[:, i % 4, :].rearrange("p (k c) -> p k c", k=KD), ACT.Copy).then_inc(x_hi, 1)
            for e in range(NE):
                if 1 <= e < NE - 1:
                    cut_w(e + 1)
                for h in range(2):
                    c = 2 * e + h
                    a.wait_ge(summed, c + 1)
                    if c >= 4:
                        a.wait_ge(stored[c % 4], 16 * (c // 4))
                    a.activation(g.y_rows[:, c % 4, :], g.psum[0:CH, 4 + c % 4, :], ACT.Copy).then_inc(copied, 1)
            for k in range(KD):
                a.wait_ge(wt, k + 1)
                a.activation(g.WThi[:, k, :], g.psum[:, k, :], ACT.Copy).then_inc(wt_hi, 1)
            for t in range(NT + 2):
                if t >= 2:
                    a.wait_ge(stats.ready, t - 1)
                    norm_rows(a, g, g.xn1, t - 2).then_inc(normed, 1)
                    a.wait_ge(normed, t - 1)
                    a.activation(g.r1hi[:, t - 2, :], g.xn1[:, t - 2, :], ACT.Copy).then_inc(r_hi, 1)
                    gather.scalar_chunk(a, t - 2)
                if t < NT:
                    deviation(a, g, stats, t)
            gather.scalar_rest(a)

        @block.vector
        def _(v):
            def cut_w(e):
                hi, lo = cut_buffers(e)
                v.wait_ge(w_hi, e)
                v.tensor_tensor(lo[:, :, :], g.eraw[:, e % 2], hi[:, :, :].bitcast(F32),
                                ALU.subtract).then_inc(w_lo, 1)

            s = g.steps.on(v)
            cut_w(1)
            for i in range(NG):
                v.wait_ge(x_hi, i + 1)
                c = slice(i * 128, (i + 1) * 128)
                v.tensor_tensor(g.gxlo[:, :, c], g.psum[:, i % 4, :].rearrange("p (k c) -> p k c", k=KD),
                                g.gxhi[:, :, c].bitcast(F32), ALU.subtract).then_inc(x_lo, 1)
            for e in range(2, NE):
                cut_w(e)
            for k in range(KD):
                v.wait_ge(wt_hi, k + 1)
                v.tensor_tensor(g.WTlo[:, k, :], g.psum[:, k, :], g.WThi[:, k, :].bitcast(F32),
                                ALU.subtract).then_inc(wt_lo, 1)
            norm = NormSteps(v, s, g, stats)
            for t in range(NT + 3):
                if t < NT:
                    v.wait_ge(fetched[t // 2], 32)
                    v.scalar_tensor_tensor(out=g.x_rows[:, t, :], in0=g.fetched_rows[:, t, :],
                                           scalar=g.share[:, t:t + 1], in1=g.x_rows[:, t, :],
                                           op0=ALU.mult, op1=ALU.add).then_inc(added, 1)
                    v.wait_ge(added, t + 1)
                norm.step(t)
                if t >= 3:
                    v.wait_ge(r_hi, t - 2)
                    v.tensor_tensor(g.r1lo[:, t - 3, :], g.xn1[:, t - 3, :], g.r1hi[:, t - 3, :].bitcast(F32),
                                    ALU.subtract).then_inc(r_lo, 1)
                    gather.vector_chunk(v, t - 3)
            gather.vector_rest(v)

        @block.tensor
        def _(t):
            turn_tensor(t, g, turned_a, moved_a)
            t.wait_ge(moved_a, 2 * len(turn_groups()))
            for i in range(NG):
                t.wait_ge(back[i // 2], 16)
                if i >= 4:
                    t.wait_ge(x_lo, i - 3)
                for k in range(KD):
                    ins = t.transpose(g.psum[:, i % 4, k * 128:(k + 1) * 128],
                                      g.g_rows[:, i, k * 128:(k + 1) * 128], g.ident[:, :])
                ins.then_inc(turned, 1)
            for e in range(NE):
                hi, lo = cut_buffers(e)
                if e:
                    t.wait_ge(w_lo, e)
                for h in range(2):
                    c = 2 * e + h
                    if h == 0:
                        t.wait_ge(x_lo, -(-(e + 1) * PLACES // 128))
                    if c >= 4:
                        t.wait_ge(copied, c - 3)
                    at = slice(c * CH, (c + 1) * CH)
                    for k in range(KD):
                        ins = cut_products(t, g.psum[0:CH, 4 + c % 4, :], (g.gxhi[:, k, at], g.gxlo[:, k, at]),
                                           (hi[:, k, :], lo[:, k, :]), k == 0, k == KD - 1)
                    ins.then_inc(summed, 1)
            t.wait_ge(w2_in, 16)
            for k in range(KD):
                for o in range(KD):
                    ins = t.transpose(g.psum[:, k, o * 128:(o + 1) * 128],
                                      g.W_rows[:, o, k * 128:(k + 1) * 128], g.ident[:, :])
                ins.then_inc(wt, 1)
            t.wait_ge(wt_lo, KD)
            t.wait_ge(copied, 2 * NE)
            gather.tensor(t, r_lo)


PAIRS = HID1 // 256
STEPS = 48


def tree_buffers(nc, g, room):
    g.w1hi = room("w1_hi", [128, 4, KD, 256], F32R)
    g.w1lo = room("w1_lo", [128, 4, KD, 256], F32R)
    g.w2hi = room("w2_hi", [128, 4, 2, D], F32R)
    g.w2lo = room("w2_lo", [128, 4, 2, D], F32R)
    acc_at = room.next
    g.factors = room("leaf_factors", [NE, 3, N], F32)
    assert room.next <= acc_at + COLS
    g.acc = Room(nc, acc_at)("acc", [128, KD, N], F32)
    room.next = acc_at + COLS
    g.leafb = room("leaf_all", [128, N], F32)
    g.G = room("gelu", [128, 3, BW], F32)
    g.hhi = room("hidden_hi", [128, 4, BW], F32R)
    g.hlo = room("hidden_lo", [128, 4, BW], F32R)
    g.ytmp = room("y_scaled", [128, KD, BW], F32)
    g.raw_at = room.next
    g.raw1 = room("w1_raw", [128, 2, KD, 256], F32)
    g.raw2 = room("w2_raw", [128, 2, 2, D], F32)
    g.rwhi = room("rw_hi", [128, KD, 128], F32R)
    g.rwlo = room("rw_lo", [128, KD, 128], F32R)
    g.node_p = room("node_p", [7, N], F32)


def tree_sources(g):
    return g.w1.rearrange("e (k p) h -> e p k h", p=128), g.w2.rearrange("e (j p) d -> e p j d", p=128)


def tree_first_loads(g, sem):
    g.t_loaded = [sem("t_loaded0"), sem("t_loaded1")]
    w1_d, w2_d = tree_sources(g)
    return [load for p in range(2) for load in (
        (g.raw1[:, p], w1_d[0, :, :, p * 256:(p + 1) * 256], g.t_loaded[p]),
        (g.raw2[:, p], w2_d[0, :, 2 * p:2 * p + 2, :], g.t_loaded[p]))]


def phase_tree(nc, sem, g):
    w1hi, w1lo, w2hi, w2lo, raw1, raw2 = g.w1hi, g.w1lo, g.w2hi, g.w2lo, g.raw1, g.raw2
    leafb, G, hhi, hlo, ytmp = g.leafb, g.G, g.hhi, g.hlo, g.ytmp
    loaded = g.t_loaded
    w_hi = sem("t_whi")
    cut = sem("t_cut")
    hidden = sem("t_hidden")
    begun = sem("t_begun")
    active = sem("t_active")
    hi_cut = sem("t_hi")
    lo_cut = sem("t_lo")
    used = sem("t_used")
    y_sum = sem("t_ysum")
    y_free = sem("t_yfree")
    acc_done = sem("t_acc")
    leaf_in = sem("t_leaf")
    rw_cut = sem("t_rw_cut")
    noded = sem("t_noded")
    node_done = sem("t_node_done")
    spread = sem("t_spread")
    factor = sem("t_factor")
    zeroed = sem("t_zeroed")

    w1_d, w2_d = tree_sources(g)

    BANKS = [(0, 1, 2), (3, 6, 7), (0, 1, 2)]

    def where(s):
        return s // 24, s % 24 // 8, s % 8 // 2, s % 2

    with nc.Block() as block:
        @block.sync
        def _(sp):
            def load(e, p):
                if p == 4:
                    sp.wait_ge(y_free, e * 24 + 4)
                    sp.dma_start(leafb[:, :], g.leaf_dram[bass.ds(e, 1), :].partition_broadcast(128)
                                 ).then_inc(leaf_in, 16)
                sp.wait_ge(cut, e * PAIRS + p + 1)
                sp.dma_start(raw1[:, p % 2], w1_d[bass.ds(e, 1), :, :, p * 256:(p + 1) * 256].rearrange(
                    "e p k h -> p (e k) h")).then_inc(loaded[p % 2], 16)
                sp.dma_start(raw2[:, p % 2], w2_d[bass.ds(e, 1), :, 2 * p:2 * p + 2, :].rearrange(
                    "e p j d -> p (e j) d")).then_inc(loaded[p % 2], 16)

            for p in range(2, PAIRS):
                if p == 4:
                    sp.wait_ge(factor, 9)
                    sp.dma_start(g.leaf_dram, g.factors[:, 2, :]).then_inc(g.leaf_stored, 16)
                    sp.wait_ge(g.leaf_stored, 16)
                load(0, p)
            with sp.Fori(1, NE) as e:
                for p in range(PAIRS):
                    load(e, p)

        @block.vector
        def _(v):
            v.sem_inc(cut, 2)
            v.sem_inc(lo_cut, 3)
            v.sem_inc(y_free, 4)

            def cut1(e, p):
                q = p % 4
                v.wait_ge(loaded[p % 2], e * (16 * PAIRS) + 32 * (p // 2 + 1))
                v.wait_ge(used, (e * 2 + p // 4) * 24 + 18 + 2 * q)
                v.tensor_copy(w1hi[:, q], raw1[:, p % 2]).then_inc(w_hi, 1)
                v.wait_ge(w_hi, e * (2 * PAIRS) + 2 * p + 1)
                v.tensor_tensor(w1lo[:, q], raw1[:, p % 2], w1hi[:, q].bitcast(F32), ALU.subtract)

            def cut2(e, p):
                q = p % 4
                v.tensor_copy(w2hi[:, q], raw2[:, p % 2]).then_inc(w_hi, 1)
                v.wait_ge(w_hi, e * (2 * PAIRS) + 2 * p + 2)
                v.tensor_tensor(w2lo[:, q], raw2[:, p % 2], w2hi[:, q].bitcast(F32),
                                ALU.subtract).then_inc(cut, 1)

            def cuts(e, s, last):
                r = (s - 20) % 24
                if r < 8:
                    p = (s - 20) // 24 * 4 + 4 + r // 2
                    at = e
                    if p >= PAIRS:
                        if last:
                            return
                        at, p = e + 1, p - PAIRS
                    (cut2 if r % 2 else cut1)(at, p)

            def drain(e, m):
                lo, hi = BLOCKS[m % 3]
                if m == 0:
                    v.wait_ge(leaf_in, e * 16 + 16)
                for d in range(KD):
                    if d < 3:
                        v.wait_ge(y_sum, e * 18 + 3 * m + d + 1)
                    else:
                        v.wait_ge(used, e * STEPS + 24 + 8 * m + 8)
                    v.wait_ge(acc_done, e * 24 + 4 * m + d + 1)
                    v.scalar_tensor_tensor(out=ytmp[:, d, 0:hi - lo], in0=g.psum[:, d, 0:hi - lo],
                                           scalar=g.b2half[:, bass.ds(e * 4 + d, 1)], in1=leafb[:, lo:hi],
                                           op0=ALU.add, op1=ALU.mult).then_inc(y_free, 1)

            def expert(e, last):
                for s in range(STEPS):
                    half, b, _, _ = where(s)
                    w = BLOCKS[b][1] - BLOCKS[b][0]
                    v.wait_ge(hi_cut, e * STEPS + s + 1)
                    v.tensor_tensor(hlo[:, s % 4, 0:w], G[:, s % 3, 0:w], hhi[:, s % 4, 0:w].bitcast(F32),
                                    ALU.subtract).then_inc(lo_cut, 1)
                    if s % 8 == 0 and s:
                        drain(e, s // 8 - 1)
                    cuts(e, s, last)
                drain(e, 5)

            s = g.steps.on(v)
            s.mark(v.memset(g.rwhi[:, :, :].bitcast(F32), 0.0))
            s.mark(v.memset(g.rwlo[:, :, :].bitcast(F32), 0.0))
            s.then(v.tensor_scalar(g.b2half[:, :], g.vecs[:, 36:68], 0.5, None, ALU.mult))
            rw = g.vecs[:, 68:96].rearrange("p (n k) -> p k n", n=7)
            s.then(v.tensor_copy(g.rwhi[:, :, 0:7], rw))
            v.tensor_tensor(g.rwlo[:, :, 0:7], rw, g.rwhi[:, :, 0:7].bitcast(F32), ALU.subtract).then_inc(rw_cut, 1)
            cut1(0, 0)
            cut2(0, 0)
            for b, (lo, hi) in enumerate(BLOCKS):
                for d in range(3):
                    v.wait_ge(spread, b * 3 + d + 1)
                    of, one = g.psum[0:NE, BANKS[b][d], 0:hi - lo], g.leafone[0:NE, d:d + 1]
                    if d == 0:
                        ins = v.tensor_scalar(g.factors[:, 0, lo:hi], of, one, None, ALU.add)
                    else:
                        v.wait_ge(factor, b * 3 + d)
                        ins = v.scalar_tensor_tensor(out=g.factors[:, d, lo:hi], in0=of, scalar=one,
                                                     in1=g.factors[:, d - 1, lo:hi], op0=ALU.add, op1=ALU.mult)
                    ins.then_inc(factor, 1)
                if b == 1:
                    cut1(0, 1)
                    cut2(0, 1)
            with v.Fori(0, NE - 1) as e:
                expert(e, False)
            expert(NE - 1, True)

        @block.gpsimd
        def _(q):
            q.wait_ge(g.leaf_stored, 16)
            q.memset(g.acc[:, :, :], 0.0).then_inc(zeroed, 1)
            q.wait_ge(zeroed, 1)
            q.sem_inc(acc_done, 4)
            with q.Fori(0, NE) as e:
                for m in range(6):
                    lo, hi = BLOCKS[m % 3]
                    for d in range(KD):
                        q.wait_ge(y_free, e * 24 + 4 * m + d + 5)
                        q.tensor_tensor(g.acc[:, d, lo:hi], g.acc[:, d, lo:hi], ytmp[:, d, 0:hi - lo],
                                        ALU.add).then_inc(acc_done, 1)

        @block.scalar
        def _(a):
            for b, (lo, hi) in enumerate(BLOCKS):
                a.wait_ge(noded, b + 1)
                a.activation(g.node_p[:, lo:hi], g.psum[0:7, b, 0:hi - lo], ACT.Sigmoid,
                             bias=g.rb_col[0:7, :]).then_inc(node_done, 1)
            a.sem_inc(active, 4)
            with a.Fori(0, NE) as e:
                for s in range(STEPS):
                    half, b, q, j = where(s)
                    w = BLOCKS[b][1] - BLOCKS[b][0]
                    a.wait_ge(hidden, e * STEPS + s + 1)
                    a.wait_ge(lo_cut, e * STEPS + s + 1)
                    a.sem_inc(begun, 1)
                    a.activation(G[:, s % 3, 0:w], g.psum[:, 4 + s % 4, 0:w], ACT.Gelu,
                                 bias=g.b1cols[:, bass.ds(e * 16 + half * 8 + 2 * q + j, 1)]).then_inc(active, 1)
                    a.wait_ge(active, e * STEPS + s + 5)
                    a.wait_ge(used, e * STEPS + s + 21)
                    a.activation(hhi[:, s % 4, 0:w], G[:, s % 3, 0:w], ACT.Copy).then_inc(hi_cut, 1)

        @block.tensor
        def _(t):
            t.sem_inc(used, 24)

            def first(e, s):
                half, b, q, j = where(s)
                lo, hi = BLOCKS[b]
                if b == 0 and j == 0:
                    t.wait_ge(cut, e * PAIRS + half * 4 + q + 3)
                t.wait_ge(active, e * STEPS + s + 1)
                c = slice(j * 128, (j + 1) * 128)
                for k in range(KD):
                    ins = cut_products(t, g.psum[:, 4 + s % 4, 0:hi - lo], (w1hi[:, q, k, c], w1lo[:, q, k, c]),
                                       (g.fthi[:, k, lo:hi], g.ftlo[:, k, lo:hi]), k == 0, k == KD - 1)
                ins.then_inc(hidden, 1)

            def second(e, s):
                half, b, q, j = where(s)
                w = BLOCKS[b][1] - BLOCKS[b][0]
                t.wait_ge(lo_cut, e * STEPS + s + 4)
                for d in range(KD):
                    if s % 8 == 0:
                        t.wait_ge(y_free, e * 24 + 4 * (s // 8) + d + 1)
                    c = slice(d * 128, (d + 1) * 128)
                    ins = cut_products(t, g.psum[:, d, 0:w], (w2hi[:, q, j, c], w2lo[:, q, j, c]),
                                       (hhi[:, s % 4, 0:w], hlo[:, s % 4, 0:w]), s % 8 == 0, s % 8 == 7)
                    if d == 3:
                        ins.then_inc(used, 1)
                    elif s % 8 == 7:
                        ins.then_inc(y_sum, 1)

            t.wait_ge(rw_cut, 1)
            for b, (lo, hi) in enumerate(BLOCKS):
                for k in range(KD):
                    ins = cut_products(t, g.psum[:, b, 0:hi - lo], (g.rwhi[:, k, :], g.rwlo[:, k, :]),
                                       (g.fthi[:, k, lo:hi], g.ftlo[:, k, lo:hi]), k == 0, k == KD - 1)
                ins.then_inc(noded, 1)
            first(0, 0)
            t.wait_ge(node_done, 3)
            for b, (lo, hi) in enumerate(BLOCKS):
                if b == 2:
                    first(0, 1)
                    t.wait_ge(factor, 3)
                for d in range(3):
                    t.matmul(g.psum[0:NE, BANKS[b][d], 0:hi - lo], g.leafsel[0:7, 8 * d:8 * d + 8],
                             g.node_p[:, lo:hi], start=True, stop=True).then_inc(spread, 1)
            t.wait_ge(factor, 9)
            with t.Fori(0, NE - 1) as e:
                for s in range(STEPS):
                    second(e, s)
                    if s + 2 < STEPS:
                        first(e, s + 2)
                    else:
                        first(e + 1, s + 2 - STEPS)
            for s in range(STEPS):
                second(NE - 1, s)
                if s + 2 < STEPS:
                    first(NE - 1, s + 2)


def phase_out(nc, sem, g):
    turned = sem("o_turned")
    added = sem("o_added")
    stored = sem("o_stored")
    with nc.Block() as block:
        @block.tensor
        def _(t):
            for i in range(NT):
                if i >= 8:
                    t.wait_ge(added, i - 7)
                for d in range(KD):
                    ins = t.transpose(g.psum[0:TR, i % 8, d * 128:(d + 1) * 128],
                                      g.acc[:, d, i * TR:(i + 1) * TR], g.ident[:, :])
                ins.then_inc(turned, 1)

        @block.vector
        def _(v):
            for i in range(NT):
                v.wait_ge(turned, i + 1)
                v.tensor_tensor(g.x_rows[:, i, :], g.x_rows[:, i, :], g.psum[0:TR, i % 8, :],
                                ALU.add).then_inc(added, 1)

        @block.sync
        def _(sp):
            for i in range(NT):
                sp.wait_ge(added, i + 1)
                sp.dma_start(g.out[i * TR:(i + 1) * TR, :], g.x_rows[:, i, :]).then_inc(stored, 16)
            sp.wait_ge(stored, 16 * NT)


INPUTS = ["x", "src", "dst", "edge_weight", "gnn0_eps", "gnn0_W1", "gnn0_b1", "gnn0_g1", "gnn0_be1",
          "gnn0_W2", "gnn0_b2", "gnn0_g2", "gnn0_be2", "gate_w", "experts", "gnn1_weight", "rw", "rb",
          "w1", "b1", "w2", "b2", "consts_d", "bits_d"]


def gnn_ffn_kernel(nc, x, src, dst, edge_weight, gnn0_eps, gnn0_W1, gnn0_b1, gnn0_g1, gnn0_be1, gnn0_W2,
                   gnn0_b2, gnn0_g2, gnn0_be2, gate_w, experts, gnn1_weight, rw, rb, w1, b1, w2, b2,
                   consts_d, bits_d, out):
    with ExitStack() as ctx:
        def sem(name):
            return ctx.enter_context(nc.semaphore(name))

        g = Record()
        g.x, g.src, g.dst, g.edge_weight, g.out = x, src, dst, edge_weight, out
        g.gnn0_eps, g.gnn0_W1, g.gnn0_b1, g.gnn0_g1, g.gnn0_be1 = gnn0_eps, gnn0_W1, gnn0_b1, gnn0_g1, gnn0_be1
        g.gnn0_W2, g.gnn0_b2, g.gnn0_g2, g.gnn0_be2 = gnn0_W2, gnn0_b2, gnn0_g2, gnn0_be2
        g.gate_w, g.experts, g.gnn1_weight = gate_w, experts, gnn1_weight
        g.rw, g.rb, g.w1, g.b1, g.w2, g.b2 = rw, rb, w1, b1, w2, b2
        g.consts_d, g.bits_d = consts_d, bits_d
        g.psum = ctx.enter_context(nc.psum_tensor("psum", [128, 8, 512], F32))
        g.leaf_dram = nc.dram_tensor("leaf_rows", (NE, N), F32).ap()
        g.x_loaded, g.W2_loaded, g.leaf_stored = sem("x_loaded"), sem("W2_loaded"), sem("leaf_stored")

        g.steps = Steps(sem("vector_steps"))

        keep = Room(nc, 0)
        g.small = keep("small_consts", [128, C_I10], F32)
        g.ident = g.small[:, C_ID:C_ID + 128]
        g.ones = g.small[:, C_ONE:C_ONE + 128]
        g.blk16 = g.small[:, C_BLK:C_BLK + 128]
        g.upto = g.small[:, C_TRI:C_TRI + 128]
        g.leafsel = g.small[:, C_LSEL:C_LSEL + 24]
        g.leafone = g.small[:, C_LONE:C_LONE + 3]
        g.rowno = g.small[:, C_ROW:C_ROW + 1]
        g.iota32 = g.small[:, C_I32:C_I32 + WIN]
        g.w2k = g.small[:, C_W2K:C_W2K + NW]
        g.blkno = g.small[:, C_BLKNO:C_BLKNO + NB]
        g.place0 = g.small[:, C_PLACE:C_PLACE + NE]
        g.first16 = g.small[:, C_FIRST:C_FIRST + NE]
        g.not_first_tile = g.small[:, C_MASK:C_MASK + NE * NT]
        g.far = g.small[:, C_FAR:C_FAR + 1]
        g.kshift = keep("kshift", [128, len(SHIFTS)], I32)
        g.eps0 = keep("eps0", [128, 1], F32)
        g.vecrows = keep("vecrows", [96, 128], F32)
        g.b1rows = keep("b1rows", [128, 128], F32)
        g.gate = keep("gate", [128, KD, NE], F32)
        g.rb_col = keep("rb_col", [7, 1], F32)
        g.vecs = keep("vecs", [128, 96], F32)
        g.b1v, g.g1v, g.be1v = g.vecs[:, 0:8], g.vecs[:, 8:16], g.vecs[:, 16:24]
        g.b2v, g.g2v, g.be2v = g.vecs[:, 24:28], g.vecs[:, 28:32], g.vecs[:, 32:36]
        g.b1cols = keep("b1cols", [128, 128], F32)
        g.b2half = keep("b2half", [128, 32], F32)
        g.zeros = keep("zeros", [128, 128], BF16)
        g.bounds = keep("bounds", [1, 2 * NW], I32)
        g.key = keep("key", [EB, NB + SLOTS], F32)
        g.share = keep("share", [TR, NT], F32)
        g.place_to = keep("place_to", [TR, NT], I32)
        g.place_from = keep("place_from", [TR, NT], I32)
        g.stats = keep("stats", [TR, NT, 6], F32)
        g.meanvar = keep("meanvar", [TR, NT, 2], F32)
        g.dev = keep("dev", [TR, NT], F32)
        g.shift = keep("norm_shift", [TR, NT], F32)
        g.eps_col = keep("eps_col", [128, 1], F32)
        g.rstd = keep("rstd", [TR, NT], F32)
        bn = g.bn = Record()
        bn.stats = keep("bn_stats", [128, 12, 6], F32)
        bn.mv = keep("bn_mv", [128, 2], F32)
        bn.mv4 = keep("bn_mv4", [128, KD, 2], F32)
        bn.a = keep("bn_var", [128, KH0], F32)
        bn.b = keep("bn_mean", [128, KH0], F32)
        bn.c = keep("bn_dev", [128, KH0], F32)
        bn.d = keep("bn_rdev", [128, KH0], F32)
        bn.scale = keep("bn_scale", [128, KH0], F32)
        bn.shift = keep("bn_shift", [128, KH0], F32)
        g.route_small = keep.next
        assert keep.next + 32 * 13 <= X_AT, keep.next
        g.x_rows = Room(nc, X_AT)("x_rows", [TR, NT, D], F32)

        room = Room(nc, REG)
        g.A1T = room("A1T", [128, NT, ND], F32)
        g.A0T = room("A0T", [128, NT, ND], BF16)
        g.D_all = room("dst_onehot", [EB, NB + SLOTS, 4, WIN], BF16)
        g.D_flat = g.D_all[:, :, :, :].rearrange("p b a w -> p (b a w)")
        g.i10 = room("i10", [EB, NC], F16)
        g.scratch_at = room.next
        g.xn = Room(nc, XN_AT)("xn", [TR, NT, D], F32)
        phase_edges(nc, sem, g)
        phase_adjacency(nc, sem, g)

        room = Room(nc, A1_END + NT * ND * 2)
        g.rhi = room("xn_hi", [TR, NT, D], F32R)
        g.rlo = room("xn_lo", [TR, NT, D], F32R)
        g.thi = room("hT_hi", [128, KD, N], F32R)
        g.tlo = room("hT_lo", [128, KD, N], F32R)
        g.a0chunk = room("A0_chunk", [TR, 2, BW], F32R)
        assert room.next <= XN_AT
        phase_gather0(nc, sem, g)
        room = Room(nc, A1_END)
        g.h1 = room("h1", [128, KH0, N], F32)
        g.w1_at = g.y_at = room.next
        g.yT = room("yT", [128, KD, N], F32)
        g.W2_raw = Room(nc, XN_AT)("W2_raw", [128, KH0, D], F32)
        g.w2_cut_at = room.next
        phase_mlp1(nc, sem, g)
        phase_mlp2(nc, sem, g)

        room = Room(nc, A1_END)
        g.eraw = room("expert_raw", [128, 2, KD, D], F32)
        g.ewhi0 = room("expert_hi0", [128, KD, D], F32R)
        g.ewlo0 = room("expert_lo0", [128, KD, D], F32R)
        places_at = room.next
        room.next = g.y_at + COLS
        g.route_end = room.next
        g.cthi = room("c_xT_hi", [128, KD, N], F32R)
        g.ctlo = room("c_xT_lo", [128, KD, N], F32R)
        sent_at = room.next
        g.c_rows = room("c_rows", [TR, NT, D], F32)
        g.route_at, g.route_at2 = places_at, room.next
        g.y_rows = room("expert_results", [CH, 4, D], F32)
        room = Room(nc, sent_at)
        g.ewhi1 = room("expert_hi1", [128, KD, D], F32R)
        g.ewlo1 = room("expert_lo1", [128, KD, D], F32R)
        room = Room(nc, places_at)
        g.g_rows = room("rows_by_place", [128, NG, D], F32)
        fetched_at = room.next
        g.gxhi = room("xT_by_place_hi", [128, KD, NP], F32R)
        g.gxlo = room("xT_by_place_lo", [128, KD, NP], F32R)
        assert room.next <= sent_at
        g.fetched_rows = Room(nc, fetched_at)("fetched_rows", [TR, NT, D], F32)
        g.placed_d = nc.dram_tensor("rows_by_place_d", (NP, D), F32).ap()
        g.results_d = nc.dram_tensor("expert_results_d", (NP, D), F32).ap()
        g.w_loaded = [sem("expert_loaded0"), sem("expert_loaded1")]
        g.placed_zero = sem("placed_zero")
        add_norm_turn(nc, sem, g, "c", turn_y(g), g.c_rows, g.cthi, g.ctlo)
        phase_route(nc, sem, g)

        room = Room(nc, A1_END)
        g.xn1 = Room(nc, room.next)("d_rows", [TR, NT, D], F32)
        room.next += ROWS
        g.WThi = room("WT_hi", [128, KD, D], F32R)
        g.WTlo = room("WT_lo", [128, KD, D], F32R)
        g.gthi = room("aggT_hi", [128, KD, N], F32R)
        g.gtlo = room("aggT_lo", [128, KD, N], F32R)
        assert room.next >= fetched_at + ROWS
        g.r1hi = room("d_rows_hi", [TR, NT, D], F32R)
        f_rows_at = room.next - ROWS
        g.r1lo = room("d_rows_lo", [TR, NT, D], F32R)
        g.a1hi = room("A1_hi", [TR, 3, BW], F32R)
        g.a1lo = room("A1_lo", [TR, 3, BW], F32R)
        g.W_rows = Room(nc, places_at + KD * D * 4)("W_rows", [128, KD, D], F32)
        phase_experts(nc, sem, g)

        room = Room(nc, REG)
        g.fthi = room("f_xT_hi", [128, KD, N], F32R)
        g.ftlo = room("f_xT_lo", [128, KD, N], F32R)
        tree_buffers(nc, g, room)
        f_rows = Room(nc, f_rows_at)("f_rows", [TR, NT, D], F32)
        assert f_rows_at + ROWS <= g.raw_at, (f_rows_at, g.raw_at)
        add_norm_turn(nc, sem, g, "f", project(g), f_rows, g.fthi, g.ftlo, tree_first_loads(g, sem))
        phase_tree(nc, sem, g)
        phase_out(nc, sem, g)


def kernel(**inputs):
    import concourse.bacc as bacc
    from concourse.bass_utils import run_bass_kernel_spmd

    nc = bacc.Bacc("TRN2", target_bir_lowering=False, num_devices=1)
    names = {
        "gnn0_eps": "L0_gnn_eps", "gnn0_W1": "L0_gnn_W1", "gnn0_b1": "L0_gnn_b1", "gnn0_g1": "L0_gnn_g1",
        "gnn0_be1": "L0_gnn_be1", "gnn0_W2": "L0_gnn_W2", "gnn0_b2": "L0_gnn_b2", "gnn0_g2": "L0_gnn_g2",
        "gnn0_be2": "L0_gnn_be2", "gate_w": "L0_ffn_gate_w", "experts": "L0_ffn_experts",
        "gnn1_weight": "L1_gnn_weight", "rw": "L1_ffn_rw", "rb": "L1_ffn_rb", "w1": "L1_ffn_w1",
        "b1": "L1_ffn_b1", "w2": "L1_ffn_w2", "b2": "L1_ffn_b2",
    }
    consts, bits = shape_constants()
    arrays, drams = {}, {}
    for name in INPUTS:
        a = {"consts_d": consts, "bits_d": bits}.get(name)
        if a is None:
            a = np.ascontiguousarray(inputs[names.get(name, name)])
            a = a.reshape(1) if a.ndim == 0 else a
        arrays["in_" + name] = a
        drams[name] = nc.dram_tensor("in_" + name, a.shape, mybir.dt.from_np(a.dtype), kind="ExternalInput").ap()
    drams["out"] = nc.dram_tensor("out_rows", (N, D), F32, kind="ExternalOutput").ap()
    gnn_ffn_kernel(nc, **drams)
    got = run_bass_kernel_spmd(nc, [arrays], core_ids=[0])
    return got.results[0]["out_rows"]
```
